# Optimizing a Trainium2 kernel written in Bass

```python
import numpy as np
import jax
import jax.numpy as jnp

def _softmax(x, axis=-1):
    return jax.nn.softmax(x, axis=axis)

def _gelu(x):
    return jax.nn.gelu(x, approximate=True)

def _silu(x):
    return jax.nn.silu(x)

def _sigmoid(x):
    return jax.nn.sigmoid(x)

def _layernorm(x, axis=-1, eps=1e-05):
    m = jnp.mean(x, axis=axis, keepdims=True)
    v = jnp.var(x, axis=axis, keepdims=True)
    return (x - m) / jnp.sqrt(v + eps)

def _scatter_add(tgt, idx, src, axis=0):
    return tgt.at[idx].add(src)

def _segment_sum(src, seg, n):
    return jax.ops.segment_sum(src, seg, n)
kernel_name = 'mk_gps_d1_gnn_r32_3a6891'

def setup_inputs(seed: int=0):
    np.random.seed(seed)
    _w = jnp.asarray

    def _rec_inputs():
        import jax
        import jax.numpy as jnp
        _gk = jax.random.key(seed)
        x = -0.0002117 + 1 * jax.random.normal(jax.random.fold_in(_gk, 1), (3125, 256), jnp.float32)
        _s = jax.random.randint(jax.random.fold_in(_gk, 2), (25000,), 0, 3125, jnp.int32)
        _d = jax.random.randint(jax.random.fold_in(_gk, 3), (25000,), 0, 3125, jnp.int32)
        _loop = jnp.arange(3125, dtype=jnp.int32)
        src = jnp.concatenate([_s, _d, _loop])
        dst = jnp.concatenate([_d, _s, _loop])
        _o = jnp.argsort(dst, stable=True)
        src = src[_o]
        dst = dst[_o]
        edge_weight = jax.random.uniform(jax.random.fold_in(_gk, 12), (53125,), jnp.float32, 0.0, 1)
        return (x, src, dst, edge_weight)
    x, src, dst, edge_weight = _rec_inputs()

    def _L0_gnn_setup():
        import jax, jax.numpy as jnp
        import numpy as np
        N_NODES = 3125
        N_EDGES = 100000
        D = 256
        key = jax.random.key(seed)
        k1, k2, k3, k4, k5, k6 = jax.random.split(key, 6)
        x = jax.random.normal(k1, (N_NODES, D), dtype=jnp.float32)
        edge_row = jax.random.randint(k2, (N_EDGES,), 0, N_NODES, dtype=jnp.int32)
        edge_col = jax.random.randint(k3, (N_EDGES,), 0, N_NODES, dtype=jnp.int32)
        edge_val = jax.random.uniform(k4, (N_EDGES,), dtype=jnp.float32)
        stdv = 1.0 / np.sqrt(D)
        weight = jax.random.uniform(k5, (D, D), dtype=jnp.float32, minval=-stdv, maxval=stdv)
        b = jax.random.uniform(k6, (D,), dtype=jnp.float32, minval=-stdv, maxval=stdv)
        return {'x': x, 'edge_row': edge_row, 'edge_col': edge_col, 'edge_val': edge_val, 'weight': weight, 'b': b}
    _L0_gnn_all = _L0_gnn_setup()
    _L0_gnn_in = {k: v for k, v in _L0_gnn_all.items() if k in ('weight', 'b')}
    del _L0_gnn_all

    def _L0_mix_setup():
        import jax, jax.numpy as jnp
        import numpy as np
        N, F, C, H = (32, 128, 256, 8)
        D = C // H
        EPS_ATTN = 1e-06
        EPS_LN = 1e-05

        def layer_norm(x, g, b):
            mu = jnp.mean(x, axis=-1, keepdims=True)
            var = jnp.var(x, axis=-1, keepdims=True)
            return (x - mu) * jax.lax.rsqrt(var + EPS_LN) * g + b
        key = jax.random.key(seed)
        ks = jax.random.split(key, 8)
        s = 1.0 / np.sqrt(C)
        return {'x': jax.random.normal(ks[0], (N, F, C), jnp.float32), 'Wqkv': jax.random.uniform(ks[1], (3 * C, C), jnp.float32, -s, s), 'ln1_g': jnp.ones((C,), jnp.float32), 'ln1_b': jnp.zeros((C,), jnp.float32), 'W1': jax.random.uniform(ks[2], (C, C), jnp.float32, -s, s), 'b1': jax.random.uniform(ks[3], (C,), jnp.float32, -s, s), 'W2': jax.random.uniform(ks[4], (C, C), jnp.float32, -s, s), 'b2': jax.random.uniform(ks[5], (C,), jnp.float32, -s, s), 'ln2_g': jnp.ones((C,), jnp.float32), 'ln2_b': jnp.zeros((C,), jnp.float32)}
    _L0_mix_all = _L0_mix_setup()
    _L0_mix_in = {k: v for k, v in _L0_mix_all.items() if k in ('Wqkv', 'ln1_g', 'ln1_b', 'W1', 'b1', 'W2', 'b2', 'ln2_g', 'ln2_b')}
    del _L0_mix_all

    def _L0_ffn_setup():
        import jax, jax.numpy as jnp
        import numpy as np
        B, S, H, F, E, K = (8, 128, 256, 512, 16, 2)
        EPS = 1e-05
        key = jax.random.key(seed)
        ks = jax.random.split(key, 9)
        sc = 0.02
        return {'x': jax.random.normal(ks[0], (B, S, H), dtype=jnp.float32), 'gate_w': jax.random.normal(ks[1], (H, E), dtype=jnp.float32) * sc, 'gate_b': jnp.zeros((E,), dtype=jnp.float32), 'w1': jax.random.normal(ks[2], (E, H, F), dtype=jnp.float32) * sc, 'b1': jnp.zeros((E, F), dtype=jnp.float32), 'w2': jax.random.normal(ks[3], (E, F, H), dtype=jnp.float32) * sc, 'b2': jnp.zeros((E, H), dtype=jnp.float32), 'gamma': jnp.ones((H,), dtype=jnp.float32), 'beta': jnp.zeros((H,), dtype=jnp.float32)}
    _L0_ffn_all = _L0_ffn_setup()
    _L0_ffn_in = {k: v for k, v in _L0_ffn_all.items() if k in ('gate_w', 'gate_b', 'w1', 'b1', 'w2', 'b2', 'gamma', 'beta')}
    del _L0_ffn_all
    return {'x': x, 'src': src, 'dst': dst, 'edge_weight': edge_weight, 'L0_gnn_weight': _L0_gnn_in['weight'], 'L0_gnn_b': _L0_gnn_in['b'], 'L0_mix_Wqkv': _L0_mix_in['Wqkv'], 'L0_mix_ln1_g': _L0_mix_in['ln1_g'], 'L0_mix_ln1_b': _L0_mix_in['ln1_b'], 'L0_mix_W1': _L0_mix_in['W1'], 'L0_mix_b1': _L0_mix_in['b1'], 'L0_mix_W2': _L0_mix_in['W2'], 'L0_mix_b2': _L0_mix_in['b2'], 'L0_mix_ln2_g': _L0_mix_in['ln2_g'], 'L0_mix_ln2_b': _L0_mix_in['ln2_b'], 'L0_ffn_gate_w': _L0_ffn_in['gate_w'], 'L0_ffn_gate_b': _L0_ffn_in['gate_b'], 'L0_ffn_w1': _L0_ffn_in['w1'], 'L0_ffn_b1': _L0_ffn_in['b1'], 'L0_ffn_w2': _L0_ffn_in['w2'], 'L0_ffn_b2': _L0_ffn_in['b2'], 'L0_ffn_gamma': _L0_ffn_in['gamma'], 'L0_ffn_beta': _L0_ffn_in['beta']}

def reference(x, src, dst, edge_weight, L0_gnn_weight, L0_gnn_b, L0_mix_Wqkv, L0_mix_ln1_g, L0_mix_ln1_b, L0_mix_W1, L0_mix_b1, L0_mix_W2, L0_mix_b2, L0_mix_ln2_g, L0_mix_ln2_b, L0_ffn_gate_w, L0_ffn_gate_b, L0_ffn_w1, L0_ffn_b1, L0_ffn_w2, L0_ffn_b2, L0_ffn_gamma, L0_ffn_beta):
    import jax
    import jax.numpy as jnp

    def _L0_gnn_ref(x, edge_row, edge_col, edge_val, weight, b):
        import jax, jax.numpy as jnp
        import numpy as np
        N_NODES = 3125
        N_EDGES = 100000
        D = 256
        support = x @ weight
        msgs = support[edge_col] * edge_val[:, None]
        out = jax.ops.segment_sum(msgs, edge_row, num_segments=N_NODES)
        return out + b

    def _L0_mix_ref(x, Wqkv, ln1_g, ln1_b, W1, b1, W2, b2, ln2_g, ln2_b):
        import jax, jax.numpy as jnp
        import numpy as np
        N, F, C, H = (32, 128, 256, 8)
        D = C // H
        EPS_ATTN = 1e-06
        EPS_LN = 1e-05

        def layer_norm(x, g, b):
            mu = jnp.mean(x, axis=-1, keepdims=True)
            var = jnp.var(x, axis=-1, keepdims=True)
            return (x - mu) * jax.lax.rsqrt(var + EPS_LN) * g + b
        n, f, c = x.shape
        qkv = jnp.einsum('nfc,oc->nfo', x, Wqkv)
        q, k, v = jnp.split(qkv, 3, axis=-1)
        q = q.reshape(n, f, H, D)
        k = k.reshape(n, f, H, D)
        v = v.reshape(n, f, H, D)
        q = jax.nn.elu(q) + 1.0
        k = jax.nn.elu(k) + 1.0
        kv = jnp.einsum('nshd,nshm->nhmd', k, v)
        ksum = jnp.sum(k, axis=1)
        z = 1.0 / (jnp.einsum('nlhd,nhd->nlh', q, ksum) + EPS_ATTN)
        t = jnp.einsum('nlhd,nhmd,nlh->nlhm', q, kv, z)
        t = t.reshape(n, f, c)
        x1 = layer_norm(t + x, ln1_g, ln1_b)
        h = jax.nn.gelu(jnp.einsum('nfc,oc->nfo', x1, W1) + b1, approximate=False)
        y = jnp.einsum('nfc,oc->nfo', h, W2) + b2
        return layer_norm(y + x1, ln2_g, ln2_b)

    def _L0_ffn_ref(x, gate_w, gate_b, w1, b1, w2, b2, gamma, beta):
        import jax, jax.numpy as jnp
        import numpy as np
        B, S, H, F, E, K = (8, 128, 256, 512, 16, 2)
        EPS = 1e-05
        gate_logits = x @ gate_w + gate_b
        topk_vals, topk_idx = jax.lax.top_k(gate_logits, K)
        topk_w = jax.nn.softmax(topk_vals, axis=-1)
        h = jax.nn.relu(jnp.einsum('bsh,ehf->bsef', x, w1) + b1)
        expert_out = jnp.einsum('bsef,efh->bseh', h, w2) + b2
        sel = jnp.take_along_axis(expert_out, topk_idx[:, :, :, None], axis=2)
        moe = jnp.sum(topk_w[..., None] * sel, axis=2)
        y = x + moe
        mu = jnp.mean(y, axis=-1, keepdims=True)
        var = jnp.var(y, axis=-1, keepdims=True)
        return (y - mu) / jnp.sqrt(var + EPS) * gamma + beta
    xn = _layernorm(x, axis=-1)
    x = x + _L0_gnn_ref(xn, src, dst, edge_weight, L0_gnn_weight, L0_gnn_b) + _L0_mix_ref(xn[None], L0_mix_Wqkv, L0_mix_ln1_g, L0_mix_ln1_b, L0_mix_W1, L0_mix_b1, L0_mix_W2, L0_mix_b2, L0_mix_ln2_g, L0_mix_ln2_b)[0]
    x = x + _L0_ffn_ref(_layernorm(x, axis=-1)[None], L0_ffn_gate_w, L0_ffn_gate_b, L0_ffn_w1, L0_ffn_b1, L0_ffn_w2, L0_ffn_b2, L0_ffn_gamma, L0_ffn_beta)[0]
    return x

_drawn_inputs = setup_inputs


def setup_inputs(seed=0):
    import zlib

    import numpy as np

    out = dict(_drawn_inputs(seed))
    spreads = {'L0_mix_ln1_g': (1.0, 0.2),
     'L0_mix_ln1_b': (0.0, 0.1),
     'L0_mix_ln2_g': (1.0, 0.2),
     'L0_mix_ln2_b': (0.0, 0.1),
     'L0_ffn_gate_b': (0.0, 0.39),
     'L0_ffn_b1': (0.0, 0.8),
     'L0_ffn_b2': (0.0, 0.373),
     'L0_ffn_gamma': (1.0, 0.2),
     'L0_ffn_beta': (0.0, 0.278)}
    factors = {'L0_gnn_b': 3.581,
     'L0_mix_Wqkv': 8.0,
     'L0_mix_b1': 8.0,
     'L0_mix_b2': 3.753,
     'L0_ffn_w1': 3.137}
    for name, (base, spread) in spreads.items():
        noise = np.random.default_rng([zlib.crc32(name.encode()), seed]).standard_normal(out[name].shape)
        drawn = base * np.exp(spread * noise) if base else spread * noise
        out[name] = jnp.asarray(drawn.astype(out[name].dtype))
    for name, factor in factors.items():
        out[name] = (out[name] * factor).astype(out[name].dtype)
    return out
```

```python
import concourse.bass as bass
from concourse import mybir
from contextlib import ExitStack

N = 3125
D = 256
NE = 53125
P = 128
TT = -(-N // P)
LAST = N - (TT - 1) * P
NB = TT
EC = -(-NE // P)
NCH = 4
CC = EC // NCH
ST = (CC * P + NB * (P - 1)) // P
E = 16
F = 512
PT = 2 * TT
MT = (2 * N + E * (P - 1)) // P
YROWS = (2 * TT + MT) * P
U = 16
HU = U // 2
SORT = CC // (ST // U)
RING = 7
NROW = 8
assert CC * NCH == EC and ST % U == 0 and SORT * (ST // U) == CC

C_ID, C_IOTA, C_NEG, C_INV, C_SLOT, C_ROW, C_LN, C_AT, CW = 0, 128, 256, 384, 384 + TT, 385 + TT, 386 + TT, 387 + TT, 388 + TT


def gps_layer(nc, x, src, dst, ew, wA, wm, rows, cols, gate_w, gate_b, w1, b1, w2, b2, cst, out):
    f32, i32, u32, bf16 = mybir.dt.float32, mybir.dt.int32, mybir.dt.uint32, mybir.dt.bfloat16
    ALU, ACT, AX = mybir.AluOpType, mybir.ActivationFunctionType, mybir.AxisListType
    ds = bass.ds

    support = nc.dram_tensor("support", (TT * P, D), f32).ap()
    mixrec = nc.dram_tensor("mixrec", (TT * P, 2 * D), f32).ap()
    xn2_d = nc.dram_tensor("xn2", (TT * P, D), f32).ap()
    y_d = nc.dram_tensor("y_rows", (YROWS, D), f32).ap()

    ctx = ExitStack()
    with ctx:
        def sb(name, shape, dt, c=ctx):
            return c.enter_context(nc.sbuf_tensor(name, shape, dt))

        def sem(name):
            return ctx.enter_context(nc.semaphore(name))

        cs = sb("cs", [P, CW], f32)
        ident, iota = cs[:, C_ID:C_ID + P], cs[:, C_IOTA:C_IOTA + P]
        negtri = sb("negtri", [P, P], bf16)
        ones_b = sb("ones_b", [P, P], bf16)
        ones_f = sb("ones_f", [P, P], f32)
        vec = sb("vec", [P, NROW, D], f32)
        xa = sb("xa", [P, TT * D], f32)
        u = sb("u", [P, TT * D], f32)
        stats = sb("stats", [P, TT * 6], f32)
        mv = sb("mv", [P, TT * 2], f32)
        rstd = sb("rstd", [P, TT], f32)
        btab = sb("btab", [1, NCH * P], i32)

        c0 = ExitStack()
        M = sb("M", [P, NB, CC], bf16, c0)
        T = sb("T", [P, NB, CC + 1], f32, c0)
        S = sb("S", [P, NB, CC + 1], f32, c0)
        V = sb("V", [P, NB, CC], f32, c0)
        xr = sb("xr", [P, 2, D], f32, c0)
        xT = sb("xT", [P, 2, D], f32, c0)
        Er = sb("Er", [P, 2, 2 * D], f32, c0)
        Rr = sb("Rr", [P, 2, 2 * D], f32, c0)
        kq = sb("kq", [P, 2, 2 * D], f32, c0)
        vs = sb("vs", [P, 2, 4, 132], f32, c0)
        qT = sb("qT", [P, 2, D], f32, c0)
        srci = sb("srci", [P, EC], i32, c0)
        dsti = sb("dsti", [P, EC], i32, c0)
        loi = sb("loi", [P, EC], i32, c0)
        endb = sb("endb", [P, 32], f32, c0)
        nb_ = sb("nb_", [P, NB], f32, c0)
        nbi = sb("nbi", [P, NB], i32, c0)
        dcol = sb("dcol", [P, P], f32, c0)
        c0.close()
        w1s = sb("w1s", [P, E, 2, F], f32)

        cm = ExitStack()
        wAs = sb("wAs", [P, 2, 4 * D], f32, cm)
        wms = sb("wms", [P, 2, 2, D], f32, cm)
        lo = sb("lo", [P, EC], f32, cm)
        hi = sb("hi", [P, EC], f32, cm)
        eid = sb("eid", [P, EC], f32, cm)
        wt = sb("wt", [P, EC], f32, cm)
        posi = sb("posi", [P, CC], i32, cm)
        zeros = sb("zeros", [P, 264], f32, cm)
        L = sb("L", [P, RING, P], f32, cm)
        O = sb("O", [P, RING, P], f32, cm)
        OV = sb("OV", [P, RING, 2, P], f32, cm)
        rec = sb("rec", [P, 2, P], f32, cm)
        reci = sb("reci", [P, 3, P], i32, cm)
        g = sb("g", [P, U, D], f32, cm)
        sel = sb("sel", [P, U, P], f32, cm)
        win = sb("win", [P, 2, 2, HU], f32, cm)
        idxw = sb("idxw", [P, U], i32, cm)
        KV = sb("KV", [P, 2, 132], f32, cm)
        colsb = sb("colsb", [P, 6], f32, cm)
        bb = sb("bb", [P, D], f32, cm)
        cb = sb("cb", [P, D], f32, cm)
        mr = sb("mr", [P, 2 * D], f32, cm)
        mu = sb("mu", [P, D], f32, cm)
        xh = sb("xh", [P, D], f32, cm)
        x1T = sb("x1T", [P, 2, P], f32, cm)
        r1 = sb("r1", [P, D], f32, cm)
        hTm = sb("hTm", [P, 2, P], f32, cm)
        y2 = sb("y2", [P, D], f32, cm)
        sm = sb("sm", [P, 48], f32, cm)
        cm.close()

        w2s = sb("w2s", [P, 4, 4, D], f32)
        b2s = sb("b2s", [P, E, D], f32)
        b1s = sb("b1s", [P, E * 4], f32)
        gws = sb("gws", [P, 2, E], f32)
        gbs = sb("gbs", [P, E], f32)
        x2 = sb("x2", [P, 2, D], f32)
        x2T = sb("x2T", [P, 2, D], f32)
        LG = sb("LG", [P, TT * E], f32)
        V8 = sb("V8", [P, TT, 8], f32)
        I8 = sb("I8", [P, TT, 8], u32)
        IF = sb("IF", [P, 2, TT], f32)
        gw_ = sb("gw_", [P, 2, TT], f32)
        MM = sb("MM", [P, E, PT], bf16)
        TM = sb("TM", [P, E, PT + 1], f32)
        SM = sb("SM", [P, E, PT + 1], f32)
        VM = sb("VM", [P, E, PT], f32)
        pl = sb("pl", [P, 4, PT], f32)
        pli = sb("pli", [P, PT], i32)
        n16 = sb("n16", [P, E], f32)
        n16i = sb("n16i", [P, E], i32)
        mcol = sb("mcol", [P, 32], f32)
        mdiag = sb("mdiag", [P, 64], f32)
        LM = sb("LM", [P, 2, P], f32)
        OM = sb("OM", [P, 2, MT], f32)
        slotf = sb("slotf", [P, 4, MT], f32)
        sloti = sb("sloti", [P, 2, MT + 4], i32)
        etab = sb("etab", [1, MT + 4], i32)
        gi = sb("gi", [P, 4], i32)
        si = sb("si", [P, 4], i32)
        gx = sb("gx", [P, 4, D], f32)
        hs = sb("hs", [P, 2, F], f32)
        hT = sb("hT", [P, 2, 4, P], f32)
        yo = sb("yo", [P, 4, D], f32)
        yl = sb("yl", [P, 2, 2 * D], f32)
        ya = sb("ya", [P, 2, D], f32)
        yn = sb("yn", [P, 2, D], f32)
        sm2 = sb("sm2", [P, 32], f32)

        B = [ctx.enter_context(nc.psum_tensor(f"bank{i}", [P, 512], f32)) for i in range(8)]
        btr, bkq, bvs, bkv0, bkv1, bsort, bqT, _spare = B
        bt, bh, by = bkq, bkq, bvs
        bmsg = (B[3], B[4], B[6], B[7])

        names = ("cst vec wA wm src dst ew colsb gate w1l expert w2l0 w2l1 w2l2 w2l3 "
                 "setup edges prep onehot tot tcp filled pos dcolr bt btc pmul mready "
                 "stat sd rs xn xT xTc xTfree kqp vsp elu kqs vsc kvmm qTp qTc xcb "
                 "sx0 sx1 ss0 ss1 sq0 sq1 kvdone kvs "
                 "oh ov smm sorted recs idx sel msg add "
                 "mr mrf mt mz mstat msd mxh mxt mxc mhp mg my mr1 mst2 msd2 mdone "
                 "rstat rsd rrs rx rT rTc rlg rlgc rxd0 rxd1 ucp route rtot rtcp rpos rdc rdcp roh rmm rslot "
                 "fidx xt2 xt2c hp hc htp htc yp yc sidx "
                 "tst tsd trs tyn tfin to0 to1 tl0 tl1 warm held").split()
        s = {n: sem("s_" + n) for n in names}
        s_x = [sem(f"s_x{i}") for i in range(5)]
        s_g = [sem(f"s_g{i}") for i in range(U)]
        s_gx = [sem(f"s_gx{i}") for i in range(4)]
        s_sc = [sem(f"s_sc{i}") for i in range(4)]
        block = ctx.enter_context(nc.Block())

        def held(eng, name, value):
            eng.wait_ge(s[name], value)
            eng.sem_inc(s["held"], 1)

        def free_at(j):
            before = j - RING if j >= RING else max(k for k in range(SORT) if k % RING == j) - SORT
            return before + 1 + RING

        def xt(t):
            return xa[:, ds(t * D, D)]

        x_parts = [(5 * i, min(5 * i + 5, TT)) for i in range(5)]

        @block.sync
        def _(sp):
            sp.dma_start(cs[:, :], cst).then_inc(s["cst"], 16)
            full, rest = NE // EC, NE % EC
            sp.wait_ge(s["setup"], 1)
            for tile, a, n in ((srci, src, "src"), (dsti, dst, "dst"), (wt, ew, "ew")):
                sp.dma_start(tile[0:full, :], a[0:full * EC].rearrange("(p t) -> p t", t=EC)).then_inc(s[n], 16)
                sp.dma_start(tile[full:full + 1, 0:rest], a[full * EC:NE].rearrange("(p t) -> p t", p=1)).then_inc(s[n], 16)
            for i, (a, b) in enumerate(x_parts):
                n = b - a if b < TT else b - a - 1
                sp.dma_start(xa[:, a * D:(a + n) * D].rearrange("p (t c) -> p t c", c=D),
                             x[a * P:(a + n) * P, :].rearrange("(t p) c -> p t c", p=P)).then_inc(s_x[i], 16)
            sp.dma_start(xa[0:LAST, (TT - 1) * D:TT * D], x[(TT - 1) * P:N, :]).then_inc(s_x[4], 16)
            sp.dma_start(wAs[:, :, :], wA.rearrange("(k p) o -> p k o", p=P)).then_inc(s["wA"], 16)
            sp.dma_start(vec[:, :, :], rows.rearrange("n d -> (n d)").partition_broadcast(P).rearrange("p (n d) -> p n d", d=D)).then_inc(s["vec"], 16)
            sp.dma_start(wms[:, :, :, :], wm.rearrange("(k p) a o -> p k a o", p=P)).then_inc(s["wm"], 16)
            sp.dma_start(colsb[:, :], cols).then_inc(s["colsb"], 16)

            def pass1_out(t, r):
                held(sp, "xn", t + 1)
                sp.dma_start(mixrec[ds(t * P, P), D:2 * D], xr[:, r, :]).then_inc(s[f"sx{r}"], 16)
                held(sp, "vsc", t + 1)
                sp.dma_start(support[ds(t * P, P), :].rearrange("p (a b) -> p a b", a=2), vs[:, r, 2:4, 0:P]).then_inc(s[f"ss{r}"], 16)
                held(sp, "qTc", t + 1)
                sp.dma_start(mixrec[ds(t * P, P), 0:D], qT[:, r, :]).then_inc(s[f"sq{r}"], 16)
            with sp.Fori(0, TT // 2) as i:
                pass1_out(2 * i, 0)
                pass1_out(2 * i + 1, 1)
            pass1_out(TT - 1, 0)
            for r in range(2):
                n = 16 * ((TT + 1 - r) // 2)
                for k in ("sx", "ss", "sq"):
                    sp.wait_ge(s[f"{k}{r}"], n)
            sp.sem_inc(s["kvs"], 1)

            def record(t):
                held(sp, "mrf", t)
                sp.dma_start(mr[:, :], mixrec[ds(t * P, P), :]).then_inc(s["mr"], 16)
            sp.wait_ge(s["kvdone"], 1)
            sp.dma_start(w1s[:, 0:8, :, :], w1[0:8].rearrange("e (k p) f -> p e k f", p=P)).then_inc(s["w1l"], 16)
            sp.dma_start(w1s[:, 8:16, :, :], w1[8:16].rearrange("e (k p) f -> p e k f", p=P)).then_inc(s["w1l"], 16)
            with sp.Fori(0, TT) as t:
                record(t)

            sp.wait_ge(s["rstat"], 1)
            sp.dma_start(b1s[:, :], b1).then_inc(s["expert"], 16)
            sp.dma_start(gws[:, :, :], gate_w.rearrange("(k p) e -> p k e", p=P)).then_inc(s["expert"], 16)
            sp.dma_start(gbs[:, :], gate_b.partition_broadcast(P)).then_inc(s["expert"], 16)
            sp.dma_start(b2s[:, :, :].rearrange("p e d -> p (e d)"), b2.rearrange("e d -> (e d)").partition_broadcast(P)).then_inc(s["expert"], 16)

            def xn2_out(t, r):
                held(sp, "rx", t + 1)
                sp.dma_start(xn2_d[ds(t * P, P), :], x2[:, r, :]).then_inc(s[f"rxd{r}"], 16)
            with sp.Fori(0, TT // 2) as i:
                xn2_out(2 * i, 0)
                xn2_out(2 * i + 1, 1)
            xn2_out(TT - 1, 0)
            w2v = w2.rearrange("e (c p) h -> e p c h", p=P)
            sp.wait_ge(s["rslot"], 1)
            eregs = [sp.alloc_register(f"sp_e{k}") for k in range(4)]
            with sp.Fori(0, MT // 4) as i:
                sp.load(eregs, etab[0:1, ds(i * 4, 4)])
                for k in range(4):
                    e = sp.snap(eregs[k], min_val=0, max_val=E - 1)
                    held(sp, "yp", i * 4 + k + 1)
                    sp.dma_start(w2s[:, k, :, :], w2v[ds(e, 1), :, :, :].rearrange("e p c h -> (e p) c h")).then_inc(s[f"w2l{k}"], 16)

            for k in range(4):
                sp.wait_ge(s_sc[k], 16 * (MT // 4))

            def tail_in(t, r, rows_=P):
                held(sp, "tyn", t + 1)
                sp.dma_start(yl[0:rows_, r, :], y_d[ds(t * 2 * P, 2 * rows_), :].rearrange("(p k) d -> p (k d)", k=2)).then_inc(s[f"tl{r}"], 16)

            def tail_out(t, r, rows_=P):
                held(sp, "tfin", t + 1)
                sp.dma_start(out[ds(t * P, rows_), :], ya[0:rows_, r, :]).then_inc(s[f"to{r}"], 16)
            tail_in(0, 0)
            tail_in(1, 1)
            with sp.Fori(0, TT // 2 - 1) as i:
                for r in range(2):
                    tail_out(2 * i + r, r)
                    tail_in(2 * i + 2 + r, r)
            tail_out(TT - 3, 0)
            tail_in(TT - 1, 0, LAST)
            tail_out(TT - 2, 1)
            tail_out(TT - 1, 0, LAST)
            sp.wait_ge(s["to0"], 16 * ((TT + 1) // 2))
            held(sp, "to1", 16 * (TT // 2))
            sp.wait_ge(s["rxd0"], 16 * ((TT + 1) // 2))
            held(sp, "rxd1", 16 * (TT // 2))

        @block.gpsimd
        def _(pool):
            nc.gpsimd.memset(zeros[:, :], 0.0)
            nc.gpsimd.memset(KV[:, :, :], 0.0)
            nc.gpsimd.memset(vs[:, :, :, :], 1.0).then_inc(s["prep"], 1)

            def bias_in(t):
                held(pool, "xn", t + 1)
                nc.gpsimd.tensor_tensor(xt(t), xt(t), cb[:, :], ALU.add).then_inc(s["xcb"], 1)
            with pool.Fori(0, TT) as t:
                bias_in(t)

            def gather(j, turn):
                if j % HU == 0:
                    held(pool, "idx", 2 * turn + j // HU + 1)
                pool.indirect_dma_start(out=g[:, j, :], out_offset=None, in_=support[:, :],
                                        in_offset=bass.IndirectOffsetOnAxis(ap=idxw[:, j:j + 1], axis=0)).then_inc(s_g[j], 16)
            pool.wait_ge(s["kvs"], 1)
            with pool.Fori(0, NCH * (ST // U)) as turn:
                for j in range(U):
                    gather(j, turn)

            def to_u(t, r):
                held(pool, "rx", t + 1)
                nc.gpsimd.tensor_copy(u[:, ds(t * D, D)], x2[:, r, :]).then_inc(s["ucp"], 1)
            with pool.Fori(0, TT // 2) as i:
                to_u(2 * i, 0)
                to_u(2 * i + 1, 1)
            to_u(TT - 1, 0)

            def token_rows(m, k):
                held(pool, "fidx", m + 1)
                pool.indirect_dma_start(out=gx[:, k, :], out_offset=None, in_=xn2_d[:, :],
                                        in_offset=bass.IndirectOffsetOnAxis(ap=gi[:, k:k + 1], axis=0)).then_inc(s_gx[k], 16)

            def expert_rows(m, k):
                held(pool, "yc", m + 1)
                pool.indirect_dma_start(out=y_d[:, :], out_offset=bass.IndirectOffsetOnAxis(ap=si[:, k:k + 1], axis=0),
                                        in_=yo[:, k, :], in_offset=None).then_inc(s_sc[k], 16)
            pool.wait_ge(s["rxd0"], 16 * ((TT + 1) // 2))
            pool.wait_ge(s["rxd1"], 16 * (TT // 2))
            token_rows(0, 0)
            token_rows(1, 1)
            with pool.Fori(0, MT // 4 - 1) as i:
                for k in range(4):
                    token_rows(4 * i + k + 2, (k + 2) % 4)
                    expert_rows(4 * i + k, k)
            for m in range(MT - 4, MT):
                if m + 2 < MT:
                    token_rows(m + 2, (m + 2) % 4)
                expert_rows(m, m % 4)

        @block.scalar
        def _(act):
            A = nc.scalar.activation
            act.wait_ge(s["cst"], 16)
            eps = cs[:, C_LN:C_LN + 1]
            for c in range(NCH):
                for q in range(NB // 4 + 1):
                    n = min(4, NB - 4 * q)
                    act.wait_ge(s["tot"], c * (NB // 4 + 1) + q + 1)
                    if c:
                        act.wait_ge(s["pos"], c)
                    A(T[:, 4 * q:4 * q + n, 0:CC], B[q % 4][:, 0:n * CC].rearrange("p (b t) -> p b t", t=CC), ACT.Copy).then_inc(s["tcp"], 1)
            act.wait_ge(s["stat"], 1)
            A(rstd[:, :], mv[:, :].rearrange("p (t k) -> p t k", k=2)[:, :, 1], ACT.Sqrt, bias=eps).then_inc(s["sd"], 1)

            def xT_copy(t, r):
                act.wait_ge(s["xT"], t + 1)
                act.wait_ge(s["vsp"], t + 1)
                A(xT[:, r, :], btr[:, 0:D], ACT.Copy).then_inc(s["xTc"], 1)

            def elu_parts(t, r):
                act.wait_ge(s["kqp"], t + 1)
                act.wait_ge(s["kqs"], t + 1)
                A(Er[:, r, :], bkq[:, :], ACT.Exp)
                A(Rr[:, r, :], bkq[:, :], ACT.Relu).then_inc(s["elu"], 1)

            def qT_copy(t, r):
                act.wait_ge(s["qTp"], t + 1)
                act.wait_ge(s[f"sq{r}"], (t // 2) * 16 if isinstance(t, int) else t)
                A(qT[:, r, :], bqT[:, 0:D], ACT.Copy).then_inc(s["qTc"], 1)

            def qT_copy2(t, r, turn):
                act.wait_ge(s["qTp"], t + 1)
                act.wait_ge(s[f"sq{r}"], turn * 16)
                A(qT[:, r, :], bqT[:, 0:D], ACT.Copy).then_inc(s["qTc"], 1)
            xT_copy(0, 0)
            elu_parts(0, 0)
            xT_copy(1, 1)
            with act.Fori(0, (TT - 3) // 2) as i:
                elu_parts(2 * i + 1, 1)
                xT_copy(2 * i + 2, 0)
                qT_copy2(2 * i, 0, i)
                elu_parts(2 * i + 2, 0)
                xT_copy(2 * i + 3, 1)
                qT_copy2(2 * i + 1, 1, i)
            n = (TT - 3) // 2
            elu_parts(TT - 2, 1)
            xT_copy(TT - 1, 0)
            qT_copy2(TT - 3, 0, n)
            elu_parts(TT - 1, 0)
            qT_copy2(TT - 2, 1, n)
            qT_copy2(TT - 1, 0, n + 1)

            def values(n, j):
                r = j % RING
                act.wait_ge(s["oh"], n + j + 1)
                act.wait_ge(s["smm"], n + free_at(j))
                A(OV[:, r, 0, :], O[:, r, :], ACT.Copy, scale=wt[:, ds(n + j, 1)])
                A(OV[:, r, 1, :], O[:, r, :], ACT.Copy, scale=eid[:, ds(n + j, 1)]).then_inc(s["ov"], 1)
            with act.Fori(0, CC // SORT) as i:
                for j in range(SORT):
                    values(i * SORT, j)

            def mix_mid(t):
                act.wait_ge(s["mstat"], t + 1)
                A(sm[:, 8:9], sm[:, 7:8], ACT.Sqrt, bias=eps).then_inc(s["msd"], 1)

            def mix_x1T(t):
                act.wait_ge(s["mxt"], t + 1)
                A(x1T[:, 0, :], btr[:, 0:P], ACT.Identity, scale=colsb[:, 0:1], bias=colsb[:, 2:3])
                A(x1T[:, 1, :], btr[:, P:2 * P], ACT.Identity, scale=colsb[:, 1:2], bias=colsb[:, 3:4]).then_inc(s["mxc"], 1)

            def mix_gelu(t):
                act.wait_ge(s["mhp"], t + 1)
                for o in range(2):
                    last = A(hTm[:, o, :], bh[:, o * P:(o + 1) * P], ACT.Gelu, bias=colsb[:, 4 + o:5 + o])
                last.then_inc(s["mg"], 1)

            def mix_end(t):
                act.wait_ge(s["mst2"], t + 1)
                A(sm[:, 18:19], sm[:, 17:18], ACT.Sqrt, bias=eps).then_inc(s["msd2"], 1)

            def turn_act(n, t):
                for j in range(SORT):
                    values(n, j)
                    if j == 2:
                        mix_mid(t)
                    if j == 6:
                        mix_x1T(t)
                    if j == 8:
                        mix_gelu(t)
                    if j == 12:
                        mix_end(t)
            act.wait_ge(s["colsb"], 16)
            with act.Fori(0, (NCH - 1) * (ST // U)) as i:
                turn_act((i + CC // SORT) * SORT, i)
            mix_mid(TT - 1)
            mix_x1T(TT - 1)
            mix_gelu(TT - 1)
            mix_end(TT - 1)

            act.wait_ge(s["rstat"], 2)
            A(rstd[:, :], mv[:, :].rearrange("p (t k) -> p t k", k=2)[:, :, 1], ACT.Sqrt, bias=eps).then_inc(s["rsd"], 1)

            def x2T_copy(t, r):
                act.wait_ge(s["rT"], t + 1)
                act.wait_ge(s["rlg"], t + 1)
                A(x2T[:, r, :], btr[:, 0:D], ACT.Copy).then_inc(s["rTc"], 1)
            with act.Fori(0, TT // 2) as i:
                x2T_copy(2 * i, 0)
                x2T_copy(2 * i + 1, 1)
            x2T_copy(TT - 1, 0)
            act.wait_ge(s["route"], 1)
            A(gw_[:, 1, :], pl[:, 3, 0:TT], ACT.Exp).then_inc(s["route"], 1)
            for q in range(2):
                act.wait_ge(s["rtot"], q + 1)
                A(TM[:, 8 * q:8 * q + 8, 0:PT], B[1 + q][:, 0:8 * PT].rearrange("p (b t) -> p b t", t=PT), ACT.Copy).then_inc(s["rtcp"], 1)

            def xT2_copy(m, r):
                act.wait_ge(s["xt2"], m + 1)
                act.wait_ge(s["hp"], m + 1)
                A(x2T[:, r, :], btr[:, 0:D], ACT.Copy).then_inc(s["xt2c"], 1)

            def relu(m, k, e):
                act.wait_ge(s["htp"], m + 1)
                act.wait_ge(s["yp"], m + 3)
                for c in range(4):
                    last = A(hT[:, k % 2, c, :], B[3 + k % 2][:, c * P:(c + 1) * P], ACT.Relu, bias=b1s[:, ds(e * 4 + c, 1)])
                last.then_inc(s["htc"], 1)
            act.wait_ge(s["rslot"], 1)
            act.wait_ge(s["expert"], 64)
            eregs = [act.alloc_register(f"act_e{k}") for k in range(4)]
            xT2_copy(0, 0)
            xT2_copy(1, 1)
            with act.Fori(0, MT // 4 - 1) as i:
                act.load(eregs, etab[0:1, ds(i * 4, 4)])
                for k in range(4):
                    relu(4 * i + k, k, act.snap(eregs[k], min_val=0, max_val=E - 1))
                    xT2_copy(4 * i + k + 2, k % 2)
            act.load(eregs, etab[0:1, MT - 4:MT])
            for k in range(4):
                relu(MT - 4 + k, k, act.snap(eregs[k], min_val=0, max_val=E - 1))
                if k < 2:
                    xT2_copy(MT - 2 + k, k % 2)

            def tail_sd(t):
                act.wait_ge(s["tst"], t + 1)
                A(sm2[:, 8:9], sm2[:, 7:8], ACT.Sqrt, bias=eps).then_inc(s["tsd"], 1)
            with act.Fori(0, TT) as t:
                tail_sd(t)

        @block.vector
        def _(dve):
            v = nc.vector
            TS, TTo, STT = v.tensor_scalar, v.tensor_tensor, v.scalar_tensor_tensor
            v.memset(srci[:, :], NB * P)
            v.memset(dsti[:, :], 0)
            v.memset(wt[:, :], 0.0)
            v.memset(xa[:, (TT - 1) * D:TT * D], 0.0).then_inc(s["setup"], 1)
            v.memset(ones_b[:, :], 1.0)
            v.memset(ones_f[:, :], 1.0)
            dve.wait_ge(s["cst"], 16)
            v.tensor_copy(negtri[:, :], cs[:, C_NEG:C_NEG + P])
            dve.wait_ge(s["src"], 32)
            dve.wait_ge(s["dst"], 32)
            dve.wait_ge(s["ew"], 32)
            TS(loi[:, :], srci[:, :], P - 1, None, ALU.bitwise_and)
            TS(srci[:, :], srci[:, :], 7, None, ALU.arith_shift_right)
            dve.drain()
            v.tensor_copy(hi[:, :], srci[:, :])
            STT(eid[:, :], dsti[:, :], float(P), loi[:, :], ALU.mult, ALU.add)
            dve.drain()

            for c in range(NCH):
                a = c * CC
                hc = hi[:, a:a + CC]
                TTo(M[:, :, :], hc.unsqueeze(1).broadcast_to([P, NB, CC]),
                    cs[:, C_IOTA:C_IOTA + NB].unsqueeze(2).broadcast_to([P, NB, CC]), ALU.is_equal).then_inc(s["mready"], 1)
                dve.wait_ge(s["tcp"], (c + 1) * (NB // 4 + 1))
                v.tensor_reduce(nb_[:, :], T[:, :, 0:CC], AX.X, ALU.add)
                dve.drain()
                TS(nb_[:, :], nb_[:, :], float(P - 1), None, ALU.add)
                dve.drain()
                v.tensor_copy(nbi[:, :], nb_[:, :])
                dve.drain()
                TS(nbi[:, :], nbi[:, :], 7, 7, ALU.arith_shift_right, ALU.arith_shift_left)
                dve.drain()
                v.tensor_copy(endb[:, 0:NB], nbi[:, :])
                dve.drain()
                TTo(nb_[:, :], endb[:, 0:NB], nb_[:, :], ALU.subtract)
                dve.drain()
                TS(T[:, :, CC], nb_[:, :], float(P - 1), None, ALU.add)
                dve.drain()
                Tf = T[:, :, :].rearrange("p b t -> p (b t)")
                Sf = S[:, :, :].rearrange("p b t -> p (b t)")
                v.tensor_tensor_scan(Sf, Tf, Tf, 0.0, ALU.add, ALU.bypass)
                dve.drain()
                for q in range(NB // 4 + 1):
                    n = min(4, NB - 4 * q)
                    dve.wait_ge(s["pmul"], c * (NB // 4 + 1) + q + 1)
                    TTo(V[:, 4 * q:4 * q + n, :], B[4 + q % 4][:, 0:n * CC].rearrange("p (b t) -> p b t", t=CC),
                        S[:, 4 * q:4 * q + n, 0:CC], ALU.add).then_inc(s["filled"], 1)
                v.tensor_copy(endb[:, 0:NB], S[:, :, CC])
                dve.drain()
                TTo(V[:, :, :], V[:, :, :], M[:, :, :], ALU.mult)
                TS(nb_[:, :], endb[:, 0:NB], cs[:, C_SLOT:C_SLOT + 1], 0.0, ALU.is_le, ALU.add, accum_out=endb[:, 31:32])
                dve.drain()
                v.tensor_reduce(lo[:, a:a + CC], V[:, :, :].rearrange("p b t -> p t b"), AX.X, ALU.add)
                TS(endb[:, 30:31], endb[:, 31:32], float(NB - 1), None, ALU.min)
                dve.drain()
                if c:
                    dve.wait_ge(s["bt"], c)
                TS(dcol[:, :], ident, endb[:, 30:31], None, ALU.mult).then_inc(s["dcolr"], 1)
                TS(lo[:, a:a + CC], lo[:, a:a + CC], -1.0, None, ALU.add)
                dve.drain()
                v.tensor_copy(posi[:, :], lo[:, a:a + CC])
                dve.drain()
                TS(loi[:, 0:CC], posi[:, :], P - 1, None, ALU.bitwise_and)
                TS(posi[:, :], posi[:, :], 7, None, ALU.arith_shift_right)
                dve.drain()
                v.tensor_copy(lo[:, a:a + CC], loi[:, 0:CC])
                v.tensor_copy(hi[:, a:a + CC], posi[:, :])
                dve.wait_ge(s["bt"], c + 1)
                v.tensor_copy(btab[0:1, c * P:c * P + ST], B[0][0:1, 0:ST]).then_inc(s["pos"], 1)
                dve.drain()

            for i, (a, b) in enumerate(x_parts):
                dve.wait_ge(s_x[i], 16 if b < TT else 32)
                for t in range(a, b):
                    v.bn_stats(stats[:, 6 * t:6 * t + 6], xa[:, t * D:(t + 1) * D])
            dve.drain()
            for t in range(TT):
                last = v.bn_aggr(mv[:, 2 * t:2 * t + 2], stats[:, 6 * t:6 * t + 6])
            last.then_inc(s["stat"], 1)
            dve.wait_ge(s["vec"], 16)
            TTo(cb[:, :], vec[:, 4, :], vec[:, 5, :], ALU.add)
            TTo(bb[:, :], vec[:, 1, :], vec[:, 2, :], ALU.add)
            dve.wait_ge(s["sd"], 1)
            v.reciprocal(rstd[:, :], rstd[:, :])
            dve.wait_ge(s["prep"], 1)
            dve.drain()

            def xn(t, r, turn):
                dve.wait_ge(s["xTfree"], t + 1)
                dve.wait_ge(s[f"sx{r}"], 16 * turn)
                TS(xr[:, r, :], xt(t), mv[:, ds(2 * t, 1)], rstd[:, ds(t, 1)], ALU.subtract, ALU.mult).then_inc(s["xn"], 1)

            def kqv(t, r, turn):
                dve.wait_ge(s["elu"], t + 1)
                dve.wait_ge(s["kvmm"], t + 1)
                STT(kq[:, r, :], Er[:, r, :], 1.0, Rr[:, r, :], ALU.min, ALU.add).then_inc(s["kqs"], 1)
                dve.wait_ge(s["vsp"], t + 3)
                dve.wait_ge(s[f"ss{r}"], 16 * turn)
                v.tensor_copy(vs[:, r, :, 0:P], bvs[:, :].rearrange("p (a b) -> p a b", a=4)).then_inc(s["vsc"], 1)
            xn(0, 0, 0)
            with dve.Fori(0, TT // 2) as i:
                xn(2 * i + 1, 1, i)
                kqv(2 * i, 0, i)
                xn(2 * i + 2, 0, i + 1)
                kqv(2 * i + 1, 1, i)
            kqv(TT - 1, 0, TT // 2)
            dve.wait_ge(s["kvmm"], TT + 2)
            for h in range(2):
                src_b = (bkv0, bkv1)[h]
                for k in range(4):
                    p0 = 32 * k
                    v.tensor_copy(KV[p0:p0 + 32, h, p0:p0 + 32], src_b[p0:p0 + 32, p0:p0 + 32])
                    v.tensor_copy(KV[p0:p0 + 32, h, P + k:P + k + 1], src_b[p0:p0 + 32, P:P + 1])
            dve.drain()
            dve.sem_inc(s["kvdone"], 1)

            def onehot(n, j):
                r = j % RING
                dve.wait_ge(s["smm"], n + free_at(j))
                TS(L[:, r, :], iota, lo[:, ds(n + j, 1)], None, ALU.is_equal)
                TS(O[:, r, :], iota, hi[:, ds(n + j, 1)], None, ALU.is_equal).then_inc(s["oh"], 1)

            def records(c):
                dve.wait_ge(s["sorted"], c + 1)
                v.tensor_copy(reci[:, 0, :], bsort[:, P:2 * P])
                v.tensor_copy(rec[:, 0, :], bsort[:, 0:P])
                dve.drain()
                TS(reci[:, 1, :], reci[:, 0, :], P - 1, None, ALU.bitwise_and)
                TS(reci[:, 2, :], reci[:, 0, :], 7, None, ALU.arith_shift_right)
                dve.drain()
                v.tensor_copy(rec[:, 1, :], reci[:, 1, :]).then_inc(s["recs"], 1)
                dve.drain()

            def window(turn, h, at):
                dve.wait_ge(s["msg"], turn * U + (h + 1) * HU)
                v.tensor_copy(win[:, h, :, :], rec[:, :, ds(at * U + h * HU, HU)])
                v.tensor_copy(idxw[:, h * HU:(h + 1) * HU], reci[:, 2, ds(at * U + h * HU, HU)]).then_inc(s["idx"], 1)

            def mix_a(t):
                dve.wait_ge(s["mt"], t + 1)
                den = bt[:, 0:264].rearrange("p (h c) -> p h c", h=2)
                TS(sm[:, 20:28].rearrange("p (h c) -> p h c", h=2), den[:, :, P:P + 4], 1e-6, None, ALU.add)
                dve.drain()
                v.reciprocal(sm[:, 28:36], sm[:, 20:28])
                dve.drain()
                for h in range(2):
                    TTo(mu[:, h * P:(h + 1) * P].rearrange("p (k m) -> p k m", k=4), den[:, h, 0:P].rearrange("p (k m) -> p k m", k=4),
                        sm[:, 28 + 4 * h:32 + 4 * h].unsqueeze(2).broadcast_to([P, 4, 32]), ALU.mult)
                dve.drain()
                TTo(mu[:, :], mu[:, :], mr[:, D:2 * D], ALU.add).then_inc(s["mrf"], 1)
                dve.drain()
                v.bn_stats(sm[:, 0:6], mu[:, :])
                dve.drain()
                v.bn_aggr(sm[:, 6:8], sm[:, 0:6]).then_inc(s["mstat"], 1)

            def mix_b(t):
                dve.wait_ge(s["msd"], t + 1)
                v.reciprocal(sm[:, 9:10], sm[:, 8:9])
                dve.drain()
                TS(xh[:, :], mu[:, :], sm[:, 6:7], sm[:, 9:10], ALU.subtract, ALU.mult).then_inc(s["mxh"], 1)
                dve.drain()
                TTo(r1[:, :], xh[:, :], vec[:, 0, :], ALU.mult)
                dve.drain()
                TTo(r1[:, :], r1[:, :], bb[:, :], ALU.add)
                dve.drain()

            def mix_c(t):
                dve.wait_ge(s["my"], t + 1)
                TTo(y2[:, :], by[:, 0:D], r1[:, :], ALU.add)
                dve.drain()
                v.bn_stats(sm[:, 10:16], y2[:, :])
                dve.drain()
                v.bn_aggr(sm[:, 16:18], sm[:, 10:16]).then_inc(s["mst2"], 1)

            def mix_d(t):
                dve.wait_ge(s["msd2"], t + 1)
                v.reciprocal(sm[:, 19:20], sm[:, 18:19])
                dve.drain()
                TS(y2[:, :], y2[:, :], sm[:, 16:17], sm[:, 19:20], ALU.subtract, ALU.mult)
                dve.drain()
                TTo(y2[:, :], y2[:, :], vec[:, 3, :], ALU.mult)
                dve.drain()
                TTo(xt(t), xt(t), y2[:, :], ALU.add).then_inc(s["mdone"], 1)
                dve.drain()

            regs = [dve.alloc_register(f"bucket{k}") for k in range(HU)]

            def turn_dve(turn, at, base, sort_at, mix, refill):
                for h in range(2):
                    dve.load(regs, btab[0:1, ds(base + at * U + h * HU, HU)])
                    dve.wait_ge(s["idx"], 2 * turn + h + 1)
                    for j in range(HU):
                        k = h * HU + j
                        TS(sel[:, k, :], iota, win[:, h, 1, j:j + 1], win[:, h, 0, j:j + 1], ALU.is_equal, ALU.mult).then_inc(s["sel"], 1)
                    for j in range(HU):
                        k = h * HU + j
                        if sort_at is not None and k < SORT:
                            onehot(sort_at, k)
                        b = dve.snap(regs[j], min_val=0, max_val=NB - 1)
                        dve.wait_ge(s["msg"], turn * U + k + 1 + U)
                        dve.wait_ge(s["add"], turn * U + k + 4)
                        TTo(xt(b), xt(b), bmsg[k % 4][:, 0:D], ALU.add).then_inc(s["add"], 1)
                        if mix is not None:
                            if k == 2:
                                mix_a(mix)
                            if k == 4:
                                mix_b(mix)
                            if k == 12:
                                mix_c(mix)
                            if k == 14:
                                mix_d(mix)
                    if refill:
                        window(turn + 1, h, at + 1)
                dve.drain()

            with dve.Fori(0, CC // SORT) as i:
                for j in range(SORT):
                    onehot(i * SORT, j)
            dve.wait_ge(s["xcb"], TT)
            records(0)
            window(0, 0, 0)
            window(0, 1, 0)
            TL = ST // U
            with dve.Fori(0, NCH - 1) as c:
                with dve.Fori(0, TL - 1) as i:
                    turn_dve(c * TL + i, i, c * P, (c * TL + i + TL) * SORT, c * TL + i, True)
                turn_dve(c * TL + TL - 1, TL - 1, c * P, (c * TL + 2 * TL - 1) * SORT, c * TL + TL - 1, False)
                records(c + 1)
                window(c * TL + TL, 0, 0)
                window(c * TL + TL, 1, 0)
            mix_a(TT - 1)
            mix_b(TT - 1)
            mix_c(TT - 1)
            mix_d(TT - 1)
            c = NCH - 1
            with dve.Fori(0, TL - 1) as i:
                turn_dve(c * TL + i, i, c * P, None, None, True)
            turn_dve(c * TL + TL - 1, TL - 1, c * P, None, None, False)

            dve.sem_inc(s["rstat"], 1)
            for t in range(TT):
                v.bn_stats(stats[:, 6 * t:6 * t + 6], xa[:, t * D:(t + 1) * D])
            dve.drain()
            for t in range(TT):
                last = v.bn_aggr(mv[:, 2 * t:2 * t + 2], stats[:, 6 * t:6 * t + 6])
            last.then_inc(s["rstat"], 1)
            dve.wait_ge(s["rsd"], 1)
            v.reciprocal(rstd[:, :], rstd[:, :])
            dve.wait_ge(s["expert"], 64)
            dve.drain()

            def xn2(t, r, turn):
                dve.wait_ge(s["rTc"], t + 1)
                dve.wait_ge(s[f"rxd{r}"], 16 * turn)
                dve.wait_ge(s["ucp"], t + 1)
                TS(x2[:, r, :], xt(t), mv[:, ds(2 * t, 1)], rstd[:, ds(t, 1)], ALU.subtract, ALU.mult).then_inc(s["rx"], 1)

            def logits(t):
                dve.wait_ge(s["rlg"], t + 3)
                TTo(LG[:, ds(t * E, E)], B[1][:, 0:E], gbs[:, :], ALU.add).then_inc(s["rlgc"], 1)
            xn2(0, 0, 0)
            with dve.Fori(0, TT // 2) as i:
                xn2(2 * i + 1, 1, i)
                logits(2 * i)
                xn2(2 * i + 2, 0, i + 1)
                logits(2 * i + 1)
            logits(TT - 1)
            dve.drain()
            for t in range(TT):
                v.max(V8[:, t, :], LG[:, t * E:(t + 1) * E])
            dve.drain()
            for t in range(TT):
                v.max_index(I8[:, t, :], V8[:, t, :], LG[:, t * E:(t + 1) * E])
            TTo(pl[:, 3, 0:TT], V8[:, :, 1], V8[:, :, 0], ALU.subtract).then_inc(s["route"], 1)
            dve.drain()
            for k in range(2):
                v.tensor_copy(IF[:, k, :], I8[:, :, k])
            dve.drain()
            for k in range(2):
                TTo(IF[:, k, :], IF[:, k, :], cs[:, C_INV:C_INV + TT], ALU.add)
            dve.drain()
            TTo(MM[:, :, :], IF[:, :, :].rearrange("p k t -> p (k t)").unsqueeze(1).broadcast_to([P, E, PT]),
                cs[:, C_IOTA:C_IOTA + E].unsqueeze(2).broadcast_to([P, E, PT]), ALU.is_equal).then_inc(s["mready"], 1)
            dve.wait_ge(s["route"], 2)
            TS(gw_[:, 0, :], gw_[:, 1, :], 1.0, None, ALU.add)
            dve.drain()
            v.reciprocal(gw_[:, 0, :], gw_[:, 0, :])
            dve.drain()
            TTo(gw_[:, 1, :], gw_[:, 1, :], gw_[:, 0, :], ALU.mult)
            dve.wait_ge(s["rtcp"], 2)
            v.tensor_reduce(n16[:, :], TM[:, :, 0:PT], AX.X, ALU.add)
            dve.drain()
            TS(n16[:, :], n16[:, :], float(P - 1), None, ALU.add)
            dve.drain()
            v.tensor_copy(n16i[:, :], n16[:, :])
            dve.drain()
            TS(n16i[:, :], n16i[:, :], 7, 7, ALU.arith_shift_right, ALU.arith_shift_left)
            dve.drain()
            v.tensor_copy(mcol[:, 0:E], n16i[:, :])
            dve.drain()
            TTo(n16[:, :], mcol[:, 0:E], n16[:, :], ALU.subtract)
            dve.drain()
            TS(TM[:, :, PT], n16[:, :], float(P - 1), None, ALU.add)
            dve.drain()
            TMf = TM[:, :, :].rearrange("p b t -> p (b t)")
            v.tensor_tensor_scan(SM[:, :, :].rearrange("p b t -> p (b t)"), TMf, TMf, 0.0, ALU.add, ALU.bypass)
            dve.drain()
            for q in range(2):
                dve.wait_ge(s["rpos"], q + 1)
                TTo(VM[:, 8 * q:8 * q + 8, :], B[3 + q][:, 0:8 * PT].rearrange("p (b t) -> p b t", t=PT), SM[:, 8 * q:8 * q + 8, 0:PT], ALU.add)
            v.tensor_copy(mcol[:, 0:E], SM[:, :, PT])
            dve.drain()
            TTo(VM[:, :, :], VM[:, :, :], MM[:, :, :], ALU.mult)
            TS(n16[:, :], mcol[:, 0:E], cs[:, C_SLOT:C_SLOT + 1], 0.0, ALU.is_le, ALU.add, accum_out=mcol[:, 31:32])
            dve.drain()
            v.tensor_reduce(pl[:, 0, :], VM[:, :, :].rearrange("p b t -> p t b"), AX.X, ALU.add)
            TS(mcol[:, 30:31], mcol[:, 31:32], float(E - 1), None, ALU.min)
            dve.drain()
            TS(mdiag[:, :], ident[:, 0:MT], mcol[:, 30:31], None, ALU.mult).then_inc(s["rdc"], 1)
            TS(pl[:, 0, :], pl[:, 0, :], -1.0, None, ALU.add)
            TS(pl[:, 2, 0:TT], iota[:, 0:TT], 2.0 * P, cs[:, C_ROW:C_ROW + 1], ALU.mult, ALU.add)
            dve.drain()
            TS(pl[:, 2, TT:PT], pl[:, 2, 0:TT], 1.0, None, ALU.add)
            v.tensor_copy(pli[:, :], pl[:, 0, :])
            dve.drain()
            TS(sloti[:, 0, 0:PT], pli[:, :], P - 1, None, ALU.bitwise_and)
            TS(pli[:, :], pli[:, :], 7, None, ALU.arith_shift_right)
            dve.drain()
            v.tensor_copy(pl[:, 0, :], sloti[:, 0, 0:PT])
            v.tensor_copy(pl[:, 1, :], pli[:, :])
            dve.drain()

            def pair(n, r):
                dve.wait_ge(s["rmm"], n + 1)
                TS(LM[:, r, :], iota, pl[:, 0, ds(n, 1)], None, ALU.is_equal)
                TS(OM[:, r, :], iota[:, 0:MT], pl[:, 1, ds(n, 1)], pl[:, 2, ds(n, 1)], ALU.is_equal, ALU.mult).then_inc(s["roh"], 1)
            with dve.Fori(0, TT) as i:
                pair(2 * i, 0)
                pair(2 * i + 1, 1)
            dve.wait_ge(s["rdcp"], 1)
            v.tensor_copy(etab[0:1, 0:MT], B[1][0:1, 0:MT])
            dve.wait_ge(s["rmm"], PT + 2)
            v.tensor_copy(slotf[:, 0, :], B[2][:, 0:MT])
            dve.drain()
            TS(slotf[:, 1, :], slotf[:, 0, :], -1.0, 0.0, ALU.add, ALU.max)
            TS(slotf[:, 2, :], iota[:, 0:MT], float(P), cs[:, C_AT:C_AT + 1], ALU.mult, ALU.add)
            TS(slotf[:, 3, :], slotf[:, 0, :], 0.0, None, ALU.is_equal)
            v.memset(sloti[:, 0, MT:MT + 4], 0)
            dve.drain()
            TTo(slotf[:, 3, :], slotf[:, 3, :], slotf[:, 2, :], ALU.mult)
            dve.drain()
            TTo(slotf[:, 3, :], slotf[:, 1, :], slotf[:, 3, :], ALU.add)
            v.tensor_copy(sloti[:, 0, 0:MT], slotf[:, 1, :])
            dve.drain()
            TS(sloti[:, 0, 0:MT], sloti[:, 0, 0:MT], 1, None, ALU.arith_shift_right)
            v.tensor_copy(sloti[:, 1, 0:MT], slotf[:, 3, :])
            dve.drain()
            dve.sem_inc(s["rslot"], 1)

            def token_index(m, k):
                v.tensor_copy(gi[:, k:k + 1], sloti[:, 0, ds(m, 1)]).then_inc(s["fidx"], 1)

            def hidden(m, k):
                dve.wait_ge(s["hp"], m + 3)
                dve.wait_ge(s["htp"], m - 1 if isinstance(m, int) and m >= 2 else m)
                v.tensor_copy(hs[:, k % 2, :], B[1 + k % 2][:, :]).then_inc(s["hc"], 1)

            def hidden2(m, k, first):
                dve.wait_ge(s["hp"], m + 3)
                if not first:
                    dve.wait_ge(s["htp"], m - 1)
                v.tensor_copy(hs[:, k % 2, :], B[1 + k % 2][:, :]).then_inc(s["hc"], 1)

            def result(m, k, turn, e):
                v.tensor_copy(si[:, k:k + 1], sloti[:, 1, ds(m, 1)])
                dve.wait_ge(s["yp"], m + 5)
                dve.wait_ge(s_sc[k], 16 * turn)
                TTo(yo[:, k, :], B[5 + k % 2][:, 0:D], b2s[:, :, :].rearrange("p e d -> p (e d)")[:, ds(e * D, D)], ALU.add).then_inc(s["yc"], 1)
            for m in range(4):
                token_index(m, m)
            ereg = [dve.alloc_register(f"dve_e{k}") for k in range(4)]
            hidden2(0, 0, True)
            hidden2(1, 1, True)
            with dve.Fori(0, MT // 4 - 1) as i:
                dve.load(ereg, etab[0:1, ds(4 * i, 4)])
                for k in range(4):
                    m = 4 * i + k
                    result_wait = s_sc[k]
                    dve.wait_ge(result_wait, 16 * i)
                    result(m, k, i, dve.snap(ereg[k], min_val=0, max_val=E - 1))
                    token_index(m + 4, k)
                    hidden2(m + 2, k, False)
            dve.load(ereg, etab[0:1, MT - 4:MT])
            for k in range(4):
                m = MT - 4 + k
                dve.wait_ge(s_sc[k], 16 * (MT // 4 - 1))
                result(m, k, MT // 4 - 1, dve.snap(ereg[k], min_val=0, max_val=E - 1))
                if m + 2 < MT:
                    hidden2(m + 2, k, False)

            def tail(t, r, turn, rows_=P):
                dve.wait_ge(s[f"tl{r}"], 16 * (turn + 1))
                STT(yn[0:rows_, 0, :], yl[0:rows_, r, 0:D], gw_[0:rows_, 0, ds(t, 1)], u[0:rows_, ds(t * D, D)], ALU.mult, ALU.add)
                dve.drain()
                STT(yn[0:rows_, 1, :], yl[0:rows_, r, D:2 * D], gw_[0:rows_, 1, ds(t, 1)], yn[0:rows_, 0, :], ALU.mult, ALU.add).then_inc(s["tyn"], 1)
                dve.drain()
                v.bn_stats(sm2[0:rows_, 0:6], yn[0:rows_, 1, :])
                dve.drain()
                v.bn_aggr(sm2[0:rows_, 6:8], sm2[0:rows_, 0:6]).then_inc(s["tst"], 1)
                dve.wait_ge(s["tsd"], t + 1)
                v.reciprocal(sm2[0:rows_, 9:10], sm2[0:rows_, 8:9])
                dve.drain()
                TS(yn[0:rows_, 0, :], yn[0:rows_, 1, :], sm2[0:rows_, 6:7], sm2[0:rows_, 9:10], ALU.subtract, ALU.mult)
                dve.drain()
                TTo(yn[0:rows_, 0, :], yn[0:rows_, 0, :], vec[0:rows_, 6, :], ALU.mult)
                dve.drain()
                TTo(yn[0:rows_, 0, :], yn[0:rows_, 0, :], vec[0:rows_, 7, :], ALU.add)
                dve.drain()
                dve.wait_ge(s[f"to{r}"], 16 * turn)
                TTo(ya[0:rows_, r, :], yn[0:rows_, 0, :], xa[0:rows_, ds(t * D, D)], ALU.add).then_inc(s["tfin"], 1)
                dve.drain()
            dve.wait_ge(s["ucp"], TT + 2)
            with dve.Fori(0, TT // 2) as i:
                tail(2 * i, 0, i)
                tail(2 * i + 1, 1, i)
            tail(TT - 1, 0, TT // 2, LAST)

        @block.tensor
        def _(pe):
            mm, tr = nc.tensor.matmul, nc.tensor.transpose
            for n, k in (("xTfree", 2), ("vsp", 2), ("kvmm", 2), ("smm", RING), ("msg", U), ("rlg", 2), ("hp", 2), ("yp", 4), ("rmm", 2), ("kqs", 2), ("add", 4), ("rTc", 2), ("ucp", 2), ("tyn", 2), ("warm", 1)):
                pe.sem_inc(s[n], k)
            NQ = NB // 4 + 1
            Mf = M[:, :, :].rearrange("p b t -> p (b t)")
            for c in range(NCH):
                pe.wait_ge(s["mready"], c + 1)
                for q in range(NQ):
                    a, b = 4 * q * CC, min(4 * q + 4, NB) * CC
                    if c * NQ + q >= 4:
                        pe.wait_ge(s["tcp"], c * NQ + q - 3 if q >= 4 else c * NQ)
                    if c and q == 0:
                        pe.wait_ge(s["pos"], c)
                    mm(B[q % 4][:, 0:b - a], ones_b[:, :], Mf[:, a:b], start=True, stop=True).then_inc(s["tot"], 1)
                for q in range(NQ):
                    a, b = 4 * q * CC, min(4 * q + 4, NB) * CC
                    if q >= 4 or c:
                        pe.wait_ge(s["filled"], c * NQ + max(q - 3, 0))
                    mm(B[4 + q % 4][:, 0:b - a], negtri[:, :], Mf[:, a:b], start=True, stop=True).then_inc(s["pmul"], 1)
                pe.wait_ge(s["dcolr"], c + 1)
                mm(B[0][:, 0:P], ones_f[:, :], dcol[:, :], start=True, stop=True).then_inc(s["bt"], 1)
            pe.wait_ge(s["pos"], NCH)

            def T_(t, r):
                pe.wait_ge(s["xn"], t + 1)
                pe.wait_ge(s["xTc"], t)
                for k in range(2):
                    last = tr(btr[:, k * P:(k + 1) * P], xr[:, r, k * P:(k + 1) * P], ident)
                last.then_inc(s["xT"], 1)
                pe.wait_ge(s["xT"], t + 1)
                pe.sem_inc(s["xTfree"], 1)

            def MM_(t, r):
                pe.wait_ge(s["xTc"], t + 1)
                pe.wait_ge(s["elu"], t)
                for k in range(2):
                    last = mm(bkq[:, :], xT[:, r, k * P:(k + 1) * P], wAs[:, k, 0:2 * D], start=(k == 0), stop=(k == 1))
                last.then_inc(s["kqp"], 1)
                pe.wait_ge(s["vsc"], t)
                for k in range(2):
                    last = mm(bvs[:, :], xT[:, r, k * P:(k + 1) * P], wAs[:, k, 2 * D:4 * D], start=(k == 0), stop=(k == 1))
                last.then_inc(s["vsp"], 1)

            def KVQ(t, r, rows_=P):
                pe.wait_ge(s["kqs"], t + 3)
                pe.wait_ge(s["vsc"], t + 1)
                for h in range(2):
                    mm((bkv0, bkv1)[h][:, 0:P + 1], kq[0:rows_, r, h * P:(h + 1) * P], vs[0:rows_, r, h, 0:P + 1], start=False, stop=False, skip_group_check=True)
                pe.wait_ge(s["qTc"], t)
                for h in range(2):
                    last = tr(bqT[:, h * P:(h + 1) * P], kq[:, r, D + h * P:D + (h + 1) * P], ident)
                last.then_inc(s["qTp"], 1)
                pe.wait_ge(s["qTp"], t + 1)
                pe.sem_inc(s["kvmm"], 1)
            pe.wait_ge(s["wA"], 16)
            pe.wait_ge(s["prep"], 1)
            for h in range(2):
                mm((bkv0, bkv1)[h][:, 0:P + 1], zeros[:, 0:P], zeros[:, 0:P + 1], start=True, stop=False, skip_group_check=True)
            T_(0, 0)
            MM_(0, 0)
            T_(1, 1)
            with pe.Fori(0, (TT - 3) // 2) as i:
                MM_(2 * i + 1, 1)
                T_(2 * i + 2, 0)
                KVQ(2 * i, 0)
                MM_(2 * i + 2, 0)
                T_(2 * i + 3, 1)
                KVQ(2 * i + 1, 1)
            MM_(TT - 2, 1)
            T_(TT - 1, 0)
            KVQ(TT - 3, 0)
            MM_(TT - 1, 0)
            KVQ(TT - 2, 1)
            for h in range(2):
                pass
            KVQ(TT - 1, 0, LAST)

            def sort_open():
                mm(bsort[:, 0:2 * P], zeros[:, 0:P], zeros[:, 0:2 * P], start=True, stop=False, skip_group_check=True)

            def sort(n, j):
                r = j % RING
                pe.wait_ge(s["ov"], n + j + 1)
                mm(bsort[:, 0:2 * P], L[:, r, :], OV[:, r, :, :].rearrange("p a b -> p (a b)"), start=False, stop=False, skip_group_check=True).then_inc(s["smm"], 1)

            def sort_close():
                mm(bsort[:, 0:2 * P], zeros[:, 0:P], zeros[:, 0:2 * P], start=False, stop=True, skip_group_check=True).then_inc(s["sorted"], 1)

            def message(turn, k):
                pe.wait_ge(s_g[k], 16 * turn + 16)
                pe.wait_ge(s["sel"], turn * U + k + 1)
                pe.wait_ge(s["add"], turn * U + k + 1)
                mm(bmsg[k % 4][:, 0:D], sel[:, k, :], g[:, k, :], start=True, stop=True).then_inc(s["msg"], 1)

            def mix_t(t):
                pe.wait_ge(s["mr"], 16 * t + 16)
                for h in range(2):
                    last = mm(bt[:, h * 132:(h + 1) * 132], mr[:, h * P:(h + 1) * P], KV[:, h, :], start=True, stop=True)
                last.then_inc(s["mt"], 1)

            def mix_x(t):
                pe.wait_ge(s["mxh"], t + 1)
                for k in range(2):
                    last = tr(btr[:, k * P:(k + 1) * P], xh[:, k * P:(k + 1) * P], ident)
                last.then_inc(s["mxt"], 1)

            def mix_h(t):
                pe.wait_ge(s["mxc"], t + 1)
                for o in range(2):
                    for k in range(2):
                        last = mm(bh[:, o * P:(o + 1) * P], wms[:, k, 0, o * P:(o + 1) * P], x1T[:, k, :], start=(k == 0), stop=(k == 1))
                last.then_inc(s["mhp"], 1)

            def mix_y(t):
                pe.wait_ge(s["mg"], t + 1)
                for k in range(2):
                    last = mm(by[:, 0:D], hTm[:, k, :], wms[:, k, 1, :], start=(k == 0), stop=(k == 1))
                last.then_inc(s["my"], 1)

            sort_open()
            with pe.Fori(0, CC // SORT) as i:
                for j in range(SORT):
                    sort(i * SORT, j)
            sort_close()
            pe.wait_ge(s["wm"], 16)
            pe.wait_ge(s["kvdone"], 1)

            def turn_pe(turn, n, t):
                for k in range(U):
                    message(turn, k)
                    if n is not None and k < SORT:
                        sort(n, k)
                    if t is not None:
                        if k == 0:
                            mix_t(t)
                        if k == 5:
                            mix_x(t)
                        if k == 8:
                            mix_h(t)
                        if k == 10:
                            mix_y(t)
            TL = ST // U
            with pe.Fori(0, NCH - 1) as c:
                pe.wait_ge(s["recs"], c + 1)
                sort_open()
                with pe.Fori(0, TL) as i:
                    turn_pe(c * TL + i, (c * TL + i + TL) * SORT, c * TL + i)
                sort_close()
            mix_t(TT - 1)
            mix_x(TT - 1)
            mix_h(TT - 1)
            mix_y(TT - 1)
            with pe.Fori((NCH - 1) * TL, NCH * TL) as turn:
                turn_pe(turn, None, None)

            def RT(t, r):
                pe.wait_ge(s["rx"], t + 1)
                pe.wait_ge(s["rTc"], t + 2)
                for k in range(2):
                    last = tr(btr[:, k * P:(k + 1) * P], x2[:, r, k * P:(k + 1) * P], ident)
                last.then_inc(s["rT"], 1)

            def RL(t, r):
                pe.wait_ge(s["rTc"], t + 3)
                pe.wait_ge(s["rlgc"], t)
                for k in range(2):
                    last = mm(B[1][:, 0:E], x2T[:, r, k * P:(k + 1) * P], gws[:, k, :], start=(k == 0), stop=(k == 1))
                last.then_inc(s["rlg"], 1)
            pe.wait_ge(s["expert"], 64)
            with pe.Fori(0, TT // 2) as i:
                for r in range(2):
                    RT(2 * i + r, r)
                    RL(2 * i + r, r)
            RT(TT - 1, 0)
            RL(TT - 1, 0)
            pe.wait_ge(s["mready"], NCH + 1)
            pe.wait_ge(s["rlgc"], TT)
            MMf = MM[:, :, :].rearrange("p b t -> p (b t)")
            for q in range(2):
                mm(B[1 + q][:, 0:8 * PT], ones_b[:, :], MMf[:, 8 * PT * q:8 * PT * (q + 1)], start=True, stop=True).then_inc(s["rtot"], 1)
            for q in range(2):
                mm(B[3 + q][:, 0:8 * PT], negtri[:, :], MMf[:, 8 * PT * q:8 * PT * (q + 1)], start=True, stop=True).then_inc(s["rpos"], 1)
            pe.wait_ge(s["rdc"], 1)
            mm(B[1][:, 0:MT], ones_f[:, :], mdiag[:, :], start=True, stop=True).then_inc(s["rdcp"], 1)

            def pair_mm(n, r, first=False, last=False):
                pe.wait_ge(s["roh"], n + 1)
                mm(B[2][:, 0:MT], LM[:, r, :], OM[:, r, :], start=first, stop=last, skip_group_check=True).then_inc(s["rmm"], 1)
            pair_mm(0, 0, first=True)
            pair_mm(1, 1)
            with pe.Fori(1, TT - 1) as i:
                pair_mm(2 * i, 0)
                pair_mm(2 * i + 1, 1)
            pair_mm(PT - 2, 0)
            pair_mm(PT - 1, 1, last=True)

            def XT(m, k, turn):
                pe.wait_ge(s_gx[k], 16 * (turn + 1))
                pe.wait_ge(s["xt2c"], m)
                for c in range(2):
                    last = tr(btr[:, c * P:(c + 1) * P], gx[:, k, c * P:(c + 1) * P], ident)
                last.then_inc(s["xt2"], 1)

            w1f = w1s[:, :, :, :].rearrange("p e k f -> p (e k f)")

            def HH(m, k, e, first=False):
                pe.wait_ge(s["xt2c"], m + 1)
                if not first:
                    pe.wait_ge(s["hc"], m - 1)
                for c in range(2):
                    last = mm(B[1 + k % 2][:, :], x2T[:, k % 2, c * P:(c + 1) * P], w1f[:, ds((e * 2 + c) * F, F)], start=(c == 0), stop=(c == 1))
                last.then_inc(s["hp"], 1)

            def HT(m, k, first=False):
                pe.wait_ge(s["hc"], m + 1)
                if not first:
                    pe.wait_ge(s["htc"], m - 1)
                for c in range(4):
                    last = tr(B[3 + k % 2][:, c * P:(c + 1) * P], hs[:, k % 2, c * P:(c + 1) * P], ident)
                last.then_inc(s["htp"], 1)

            def YY(m, k, turn, first=False):
                pe.wait_ge(s["htc"], m + 1)
                pe.wait_ge(s[f"w2l{k}"], 16 * (turn + 1))
                if not first:
                    pe.wait_ge(s["yc"], m - 1)
                for c in range(4):
                    last = mm(B[5 + k % 2][:, 0:D], hT[:, k % 2, c, :], w2s[:, k, c, :], start=(c == 0), stop=(c == 3))
                last.then_inc(s["yp"], 1)
            pe.wait_ge(s["rslot"], 1)
            pe.wait_ge(s["w1l"], 32)
            er = [pe.alloc_register(f"pe_e{k}") for k in range(4)]

            def step(m, k, turn, e, first=0):
                k1 = (k - 1) % 4
                HT(m - 1, k1, first=first >= 2)
                HH(m, k, e, first=first == 3)
                YY(m - 1, k1, turn - (k == 0), first=first >= 2)
                if first != -1:
                    XT(m + 1, (k + 1) % 4, turn + (k == 3))
            pe.load(er, etab[0:1, 0:4])
            XT(0, 0, 0)
            HH(0, 0, pe.snap(er[0], min_val=0, max_val=E - 1), first=True)
            XT(1, 1, 0)
            step(1, 1, 0, pe.snap(er[1], min_val=0, max_val=E - 1), first=3)
            step(2, 2, 0, pe.snap(er[2], min_val=0, max_val=E - 1), first=2 if False else 1)
            step(3, 3, 0, pe.snap(er[3], min_val=0, max_val=E - 1))
            with pe.Fori(1, MT // 4 - 1) as i:
                pe.load(er, etab[0:1, ds(4 * i, 4)])
                for k in range(4):
                    step(4 * i + k, k, i, pe.snap(er[k], min_val=0, max_val=E - 1))
            pe.load(er, etab[0:1, MT - 4:MT])
            for k in range(4):
                step(MT - 4 + k, k, MT // 4 - 1, pe.snap(er[k], min_val=0, max_val=E - 1), first=-1 if k == 3 else 0)
            HT(MT - 1, 3)
            YY(MT - 1, 3, MT // 4 - 1)


def kernel(**inputs):
    import numpy as np
    import concourse.bacc as bacc
    from concourse.bass_utils import run_bass_kernel_spmd as run

    a = {k: np.asarray(v) for k, v in inputs.items()}
    c = np.ascontiguousarray
    wq, wk, wv = (a["L0_mix_Wqkv"][i * D:(i + 1) * D].T for i in range(3))
    cst = np.zeros((P, CW), np.float32)
    cst[:, C_ID:C_ID + P] = np.eye(P)
    cst[:, C_IOTA:C_IOTA + P] = np.arange(P)
    cst[:, C_NEG:C_NEG + P] = -np.tril(np.ones((P, P)), -1)
    cst[LAST:, C_INV + TT - 1] = 100.0
    cst[:, C_SLOT] = P * np.arange(P)
    cst[:, C_ROW] = 2 * np.arange(P) + 1
    cst[:, C_LN] = 1e-5
    cst[:, C_AT] = 2 * TT * P + np.arange(P)
    feed = {
        "x": c(a["x"]), "src": c(a["src"]), "dst": c(a["dst"]), "ew": c(a["edge_weight"]),
        "wA": c(np.concatenate([wk, wq, wv, a["L0_gnn_weight"]], 1)),
        "wm": c(np.stack([a["L0_mix_W1"].T, a["L0_mix_W2"].T], 1)),
        "rows": c(np.stack([a[n] for n in ("L0_mix_ln1_g", "L0_mix_ln1_b", "L0_mix_b2", "L0_mix_ln2_g", "L0_mix_ln2_b",
                                           "L0_gnn_b", "L0_ffn_gamma", "L0_ffn_beta")])),
        "cols": c(np.concatenate([a[n].reshape(2, P).T for n in ("L0_mix_ln1_g", "L0_mix_ln1_b", "L0_mix_b1")], 1)),
        "gate_w": c(a["L0_ffn_gate_w"]), "gate_b": c(a["L0_ffn_gate_b"]),
        "w1": c(a["L0_ffn_w1"]), "b1": c(a["L0_ffn_b1"].reshape(E, 4, P).transpose(2, 0, 1).reshape(P, E * 4)),
        "w2": c(a["L0_ffn_w2"]), "b2": c(a["L0_ffn_b2"]), "cst": cst,
    }
    nc = bacc.Bacc("TRN2", target_bir_lowering=False, num_devices=1)
    args = {k: nc.dram_tensor(f"in_{k}", v.shape, mybir.dt.from_np(v.dtype), kind="ExternalInput").ap() for k, v in feed.items()}
    res = nc.dram_tensor("out_x", (N, D), mybir.dt.float32, kind="ExternalOutput").ap()
    gps_layer(nc, *args.values(), res)
    got = run(nc, [{f"in_{k}": v for k, v in feed.items()}], core_ids=[0])
    return got.results[0]["out_x"]
```

```python
import concourse.bass as bass
from concourse import mybir
from contextlib import ExitStack

N = 3125
D = 256
NE = 53125
P = 128
TT = -(-N // P)
LAST = N - (TT - 1) * P
NB = TT
EC = -(-NE // P)
NCH = 4
CC = EC // NCH
ST = (CC * P + NB * (P - 1)) // P
E = 16
F = 512
PT = 2 * TT
PB = 10
PQ = PT // PB
MT = (2 * N + E * (P - 1)) // P
YROWS = (2 * TT + MT) * P
U = 16
HU = U // 2
SORT = CC // (ST // U)
BATCH = ((0, 5), (5, 9), (9, 13))
NQ = -(-NB // 4)
P1 = 3
LAG = 3
assert CC * NCH == EC and ST % U == 0 and SORT * (ST // U) == CC

C_ID, C_IOTA, C_NEG, C_INV, C_SLOT, C_ROW, C_LN, C_AT, CW = 0, 128, 256, 384, 384 + TT, 385 + TT, 386 + TT, 387 + TT, 388 + TT


def gps_layer(nc, x, src, dst, ew, wA, wm, rows, cols, gate_w, gate_b, w1, b1, w2, b2, cst, out):
    f32, i32, u32, bf16 = mybir.dt.float32, mybir.dt.int32, mybir.dt.uint32, mybir.dt.bfloat16
    ALU, ACT, AX = mybir.AluOpType, mybir.ActivationFunctionType, mybir.AxisListType
    ds = bass.ds

    support = nc.dram_tensor("support", (TT * P, D), f32).ap()
    mixrec = nc.dram_tensor("mixrec", (TT * P, 2 * D), f32).ap()
    xn2_d = nc.dram_tensor("xn2", (TT * P, D), f32).ap()
    y_d = nc.dram_tensor("y_rows", (YROWS, D), f32).ap()

    ctx = ExitStack()
    with ctx:
        def sb(name, shape, dt, c=ctx):
            return c.enter_context(nc.sbuf_tensor(name, shape, dt))

        def sem(name):
            return ctx.enter_context(nc.semaphore(name))

        cs = sb("cs", [P, CW], f32)
        ident, iota = cs[:, C_ID:C_ID + P], cs[:, C_IOTA:C_IOTA + P]
        negtri = sb("negtri", [P, P], bf16)
        ones_b = sb("ones_b", [P, P], bf16)
        ones_f = sb("ones_f", [P, P], f32)
        vec = sb("vec", [P, 6, D], f32)
        xa = sb("xa", [P, TT * D], f32)
        stats = sb("stats", [P, TT * 6], f32)
        mv = sb("mv", [P, TT * 2], f32)
        rstd = sb("rstd", [P, TT], f32)
        btab = sb("btab", [1, NCH * P], i32)

        c0 = ExitStack()
        M = sb("M", [P, NB, CC], bf16, c0)
        T = sb("T", [P, NB, CC + 1], f32, c0)
        S = sb("S", [P, NB, CC + 1], f32, c0)
        V = sb("V", [P, NB, CC], f32, c0)
        xr = sb("xr", [P, P1, D], f32, c0)
        xT = sb("xT", [P, P1, D], f32, c0)
        Er = sb("Er", [P, P1, 2 * D], f32, c0)
        Rr = sb("Rr", [P, P1, 2 * D], f32, c0)
        kq = sb("kq", [P, P1, 2 * D], f32, c0)
        vs = sb("vs", [P, P1, 4, 132], f32, c0)
        qT = sb("qT", [P, P1, D], f32, c0)
        srci = sb("srci", [P, EC], i32, c0)
        dsti = sb("dsti", [P, EC], i32, c0)
        loi = sb("loi", [P, EC], i32, c0)
        endb = sb("endb", [P, 32], f32, c0)
        nb_ = sb("nb_", [P, NB], f32, c0)
        nbi = sb("nbi", [P, NB], i32, c0)
        dcol = sb("dcol", [P, P], f32, c0)
        c0.close()
        u = sb("u", [P, TT * D], f32)
        w1s = sb("w1s", [P, E, 2, F], f32)       

        cm = ExitStack()
        wAs = sb("wAs", [P, 2, 4 * D], f32, cm)
        wms = sb("wms", [P, 2, 2, D], f32, cm)
        lohi = sb("lohi", [P, 2, EC], f32, cm)
        eid = sb("eid", [P, EC], f32, cm)
        wt = sb("wt", [P, EC], f32, cm)
        posi = sb("posi", [P, CC], i32, cm)
        zeros = sb("zeros", [P, 264], f32, cm)
        L = sb("L", [P, SORT, P], f32, cm)
        O = sb("O", [P, 2, 5, P], f32, cm)
        OV = sb("OV", [P, SORT, 2, P], f32, cm)
        rec = sb("rec", [P, 2, P], f32, cm)
        reci = sb("reci", [P, 3, P], i32, cm)
        g = sb("g", [P, U, D], f32, cm)
        sel = sb("sel", [P, U, P], f32, cm)
        win = sb("win", [P, 2, U], f32, cm)
        idxw = sb("idxw", [P, U], i32, cm)
        KV = sb("KV", [P, 2, 132], f32, cm)
        colsb = sb("colsb", [P, 6], f32, cm)
        cb = sb("cb", [P, D], f32, cm)
        mr = sb("mr", [P, 2 * D], f32, cm)
        mu = sb("mu", [P, D], f32, cm)
        xh = sb("xh", [P, D], f32, cm)
        x1T = sb("x1T", [P, 2, P], f32, cm)
        hTm = sb("hTm", [P, 2, P], f32, cm)
        y2 = sb("y2", [P, D], f32, cm)
        sm = sb("sm", [P, 48], f32, cm)
        cm.close()

        w2s = sb("w2s", [P, 4, 4, D], f32)
        b2s = sb("b2s", [P, E, D], f32)
        b1s = sb("b1s", [P, E * 4], f32)
        gws = sb("gws", [P, 2, E], f32)
        gbs = sb("gbs", [P, E], f32)
        x2T = sb("x2T", [P, 2, D], f32)
        nmr = sb("nmr", [P, TT], f32)
        gw_ = sb("gw_", [P, 2, TT], f32)
        sloti = sb("sloti", [P, 2, MT + 4], i32)
        etab = sb("etab", [1, MT + 4], i32)
        gi = sb("gi", [P, 4], i32)
        si = sb("si", [P, 4], i32)

        cr = ExitStack()
        x2 = sb("x2", [P, 4, D], f32, cr)
        LG = sb("LG", [P, TT * E], f32, cr)
        V8 = sb("V8", [P, TT, 8], f32, cr)
        I8 = sb("I8", [P, TT, 8], u32, cr)
        IF = sb("IF", [P, 2, TT], f32, cr)
        MM = sb("MM", [P, E, PT], bf16, cr)
        TM = sb("TM", [P, E, PT + 1], f32, cr)
        SM = sb("SM", [P, E, PT + 1], f32, cr)
        VM = sb("VM", [P, E, PT], f32, cr)
        pl = sb("pl", [P, 4, PT], f32, cr)
        pli = sb("pli", [P, PT], i32, cr)
        n16 = sb("n16", [P, E], f32, cr)
        n16i = sb("n16i", [P, E], i32, cr)
        mcol = sb("mcol", [P, 32], f32, cr)
        mdiag = sb("mdiag", [P, 64], f32, cr)
        LM = sb("LM", [P, PT, P], bf16, cr)
        OM = sb("OM", [P, PT, 2, MT], bf16, cr)
        slotf = sb("slotf", [P, 4, MT], f32, cr)
        cr.close()
        gx = sb("gx", [P, 4, D], f32)
        hs = sb("hs", [P, 2, F], f32)
        hT = sb("hT", [P, 2, 4, P], f32)
        yo = sb("yo", [P, 4, D], f32)
        yl = sb("yl", [P, 3, 2 * D], f32)
        yn = sb("yn", [P, 2, D], f32)
        yc2 = sb("yc2", [P, 3, D], f32)

        B = [ctx.enter_context(nc.psum_tensor(f"bank{i}", [P, 512], f32)) for i in range(8)]
        btr, bkq, bvs, bkv0, bkv1, bsort, bqT, bspare = B
        brank = (bkq, bvs, bqT, bspare)
        bt, bh, by = bkq, bkq, bvs
        bmsg = (B[3], B[4], B[6], B[7])

        credit = {"xT": P1, "xTc": 1, "kqp": P1, "vsp": P1, "elu": 1, "kqs": P1, "vsc": 1, "kvmm": P1, "qTp": P1, "qTc": 1,
                  "out1": P1, "ov": SORT, "smm": SORT, "msg": U, "add": 4, "mrf": 1, "rx": 1, "rT": 4, "rTc": 2, "rlg": 2, "rlgc": 2,
                  "ucp": 4, "rout": 4, "xt2": 1, "xt2c": 1, "hp": 2, "hc": 2, "htp": 2, "htc": 2, "yp": 4, "yc": 2,
                  "tcomb": 3, "tnorm": 2, "tfin": 1, "tout": 3}
        names = ("cst vec wA wm src dst ew colsb w1l expert o1_0 o1_1 o1_2 w2l0 w2l1 w2l2 w2l3 "
                 "setup prep mready tot tcp filled pmul pos dcolr bt stat sd xn xcb kvdone kvs "
                 "oh sorted recs win idx sel mr mt mstat msd mxh mxt mxc mhp mg my mst2 msd2 "
                 "rstat rsd ro0 ro1 ro2 ro3 rtot rtcp rpos rdc rdcp roh rmm rslot route "
                 "fidx si tld0 tld1 tld2 tst tsd trs tb to0 to1 to2 beta held").split()
        s = {n: sem("s_" + n) for n in (*names, *credit)}

        def after(eng, name, t):
            eng.wait_ge(s[name], t + 1 + credit.get(name, 0))

        def held_after(eng, name, t):
            after(eng, name, t)
            eng.sem_inc(s["held"], 1)

        s_x = [sem(f"s_x{i}") for i in range(5)]
        s_g = [sem(f"s_g{i}") for i in range(U)]
        s_gx = [sem(f"s_gx{i}") for i in range(4)]
        s_sc = [sem(f"s_sc{i}") for i in range(4)]
        block = ctx.enter_context(nc.Block())

        def xt(t):
            return xa[:, ds(t * D, D)]

        def xu(t):
            return u[:, ds(t * D, D)]

        def batch_of(j):
            b = next(b for b, (a, e) in enumerate(BATCH) if a <= j < e)
            return b, j - BATCH[b][0]

        def oslot(b):
            return (0, 1, 0)[b]

        def ov_before(b):
            return (-1, 5 - SORT + 3, 4)[b]

        x_parts = [(5 * i, min(5 * i + 5, TT)) for i in range(5)]

        @block.sync
        def _(sp):
            sp.dma_start(cs[:, :], cst).then_inc(s["cst"], 16)
            full, rest = NE // EC, NE % EC
            sp.wait_ge(s["setup"], 1)
            for tile, a, n in ((srci, src, "src"), (dsti, dst, "dst"), (wt, ew, "ew")):
                sp.dma_start(tile[0:full, :], a[0:full * EC].rearrange("(p t) -> p t", t=EC)).then_inc(s[n], 16)
                sp.dma_start(tile[full:full + 1, 0:rest], a[full * EC:NE].rearrange("(p t) -> p t", p=1)).then_inc(s[n], 16)
            for i, (a, b) in enumerate(x_parts):
                n = b - a if b < TT else b - a - 1
                sp.dma_start(xa[:, a * D:(a + n) * D].rearrange("p (t c) -> p t c", c=D),
                             x[a * P:(a + n) * P, :].rearrange("(t p) c -> p t c", p=P)).then_inc(s_x[i], 16)
            sp.dma_start(xa[0:LAST, (TT - 1) * D:TT * D], x[(TT - 1) * P:N, :]).then_inc(s_x[4], 16)
            sp.dma_start(wAs[:, :, :], wA.rearrange("(k p) o -> p k o", p=P)).then_inc(s["wA"], 16)
            sp.dma_start(vec[:, :, :], rows.rearrange("n d -> (n d)").partition_broadcast(P).rearrange("p (n d) -> p n d", d=D)).then_inc(s["vec"], 16)
            sp.dma_start(wms[:, :, :, :], wm.rearrange("(k p) a o -> p k a o", p=P)).then_inc(s["wm"], 16)
            sp.dma_start(colsb[:, :], cols).then_inc(s["colsb"], 16)

            def pass1_out(t, r):
                held_after(sp, "xn", t)
                sp.dma_start(mixrec[ds(t * P, P), D:2 * D], xr[:, r, :]).then_inc(s[f"o1_{r}"], 16)
                held_after(sp, "vsc", t)
                sp.dma_start(support[ds(t * P, P), :].rearrange("p (a b) -> p a b", a=2), vs[:, r, 2:4, 0:P]).then_inc(s[f"o1_{r}"], 16)
                held_after(sp, "qTc", t)
                sp.dma_start(mixrec[ds(t * P, P), 0:D], qT[:, r, :]).then_inc(s[f"o1_{r}"], 16)

            def pass1_stored(r, rnd):
                sp.wait_ge(s[f"o1_{r}"], 48 * (rnd + 1))
                sp.sem_inc(s["out1"], 1)
            with sp.Fori(0, TT // P1) as i:
                pass1_out(P1 * i, 0)
                pass1_out(P1 * i + 1, 1)
                pass1_stored(0, i)
                pass1_out(P1 * i + 2, 2)
                pass1_stored(1, i)
                pass1_stored(2, i)
            pass1_out(TT - 1, 0)
            pass1_stored(0, TT // P1)
            sp.sem_inc(s["kvs"], 1)

            def record(t):
                held_after(sp, "mrf", t - 1)
                sp.dma_start(mr[:, :], mixrec[ds(t * P, P), :]).then_inc(s["mr"], 16)
            sp.wait_ge(s["kvdone"], 1)
            sp.dma_start(w1s[:, 0:8, :, :], w1[0:8].rearrange("e (k p) f -> p e k f", p=P)).then_inc(s["w1l"], 16)
            sp.dma_start(w1s[:, 8:16, :, :], w1[8:16].rearrange("e (k p) f -> p e k f", p=P)).then_inc(s["w1l"], 16)
            with sp.Fori(0, TT) as t:
                record(t)

            sp.wait_ge(s["rstat"], 1)
            sp.dma_start(b1s[:, :], b1).then_inc(s["expert"], 16)
            sp.dma_start(gws[:, :, :], gate_w.rearrange("(k p) e -> p k e", p=P)).then_inc(s["expert"], 16)
            sp.dma_start(gbs[:, :], gate_b.partition_broadcast(P)).then_inc(s["expert"], 16)
            sp.dma_start(b2s[:, :, :].rearrange("p e d -> p (e d)"), b2.rearrange("e d -> (e d)").partition_broadcast(P)).then_inc(s["expert"], 16)

            def xn2_out(t, r):
                held_after(sp, "rx", t)
                sp.dma_start(xn2_d[ds(t * P, P), :], x2[:, r, :]).then_inc(s[f"ro{r}"], 16)

            def xn2_stored(r, rnd):
                sp.wait_ge(s[f"ro{r}"], 16 * (rnd + 1))
                sp.sem_inc(s["rout"], 1)
            with sp.Fori(0, TT // 4) as i:
                for r in range(4):
                    xn2_out(4 * i + r, r)
                    if r >= 2:
                        xn2_stored(r - 2, i)
                xn2_stored(2, i)
                xn2_stored(3, i)
            xn2_out(TT - 1, 0)
            xn2_stored(0, TT // 4)
            w2v = w2.rearrange("e (c p) h -> e p c h", p=P)
            sp.wait_ge(s["rslot"], 1)
            eregs = [sp.alloc_register(f"sp_e{k}") for k in range(4)]
            with sp.Fori(0, MT // 4) as i:
                sp.load(eregs, etab[0:1, ds(i * 4, 4)])
                for k in range(4):
                    e = sp.snap(eregs[k], min_val=0, max_val=E - 1)
                    held_after(sp, "yp", i * 4 + k - 4)
                    sp.dma_start(w2s[:, k, :, :], w2v[ds(e, 1), :, :, :].rearrange("e p c h -> (e p) c h")).then_inc(s[f"w2l{k}"], 16)

            for k in range(4):
                sp.wait_ge(s_sc[k], 16 * (MT // 4))

            def tail_in(t, r, rows_=P):
                held_after(sp, "tcomb", t - 3)
                sp.dma_start(yl[0:rows_, r, :], y_d[ds(t * 2 * P, 2 * rows_), :].rearrange("(p k) d -> p (k d)", k=2)).then_inc(s[f"tld{r}"], 16)
            with sp.Fori(0, TT // 3) as i:
                for r in range(3):
                    tail_in(3 * i + r, r)
            tail_in(TT - 1, 0, LAST)

            def tail_out(t, r, rows_=P):
                held_after(sp, "tfin", t)
                sp.dma_start(out[ds(t * P, rows_), :], yo[0:rows_, r, :]).then_inc(s[f"to{r}"], 16)

            def tail_stored(r, rnd):
                sp.wait_ge(s[f"to{r}"], 16 * (rnd + 1))
                sp.sem_inc(s["tout"], 1)
            with sp.Fori(0, TT // 3) as i:
                tail_out(3 * i, 0)
                tail_out(3 * i + 1, 1)
                tail_stored(0, i)
                tail_out(3 * i + 2, 2)
                tail_stored(1, i)
                tail_stored(2, i)
            tail_out(TT - 1, 0, LAST)
            tail_stored(0, TT // 3)

        @block.gpsimd
        def _(pool):
            nc.gpsimd.memset(zeros[:, :], 0.0)
            nc.gpsimd.memset(KV[:, :, :], 0.0)
            nc.gpsimd.memset(vs[:, :, :, :], 1.0).then_inc(s["prep"], 1)

            def bias_in(t):
                after(pool, "xn", t)
                nc.gpsimd.tensor_tensor(xt(t), xt(t), cb[:, :], ALU.add).then_inc(s["xcb"], 1)
            with pool.Fori(0, TT) as t:
                bias_in(t)

            def gather(j, turn):
                if j % HU == 0:
                    held_after(pool, "idx", 2 * turn + j // HU)
                pool.indirect_dma_start(out=g[:, j, :], out_offset=None, in_=support[:, :],
                                        in_offset=bass.IndirectOffsetOnAxis(ap=idxw[:, j:j + 1], axis=0)).then_inc(s_g[j], 16)
            pool.wait_ge(s["kvs"], 1)
            with pool.Fori(0, NCH * (ST // U)) as turn:
                for j in range(U):
                    gather(j, turn)

            def to_u(t, r):
                held_after(pool, "rx", t)
                nc.gpsimd.tensor_copy(u[:, ds(t * D, D)], x2[:, r, :]).then_inc(s["ucp"], 1)
            with pool.Fori(0, TT // 4) as i:
                for r in range(4):
                    to_u(4 * i + r, r)
            to_u(TT - 1, 0)

            def token_rows(m, k):
                held_after(pool, "fidx", m)
                pool.indirect_dma_start(out=gx[:, k, :], out_offset=None, in_=xn2_d[:, :],
                                        in_offset=bass.IndirectOffsetOnAxis(ap=gi[:, k:k + 1], axis=0)).then_inc(s_gx[k], 16)

            def expert_rows(m, k):
                held_after(pool, "yc", m)
                pool.indirect_dma_start(out=y_d[:, :], out_offset=bass.IndirectOffsetOnAxis(ap=si[:, k:k + 1], axis=0),
                                        in_=yo[:, k, :], in_offset=None).then_inc(s_sc[k], 16)
            after(pool, "rout", TT - 1)
            after(pool, "ucp", TT - 1)
            with pool.Fori(0, TT) as t:
                nc.gpsimd.tensor_tensor(xt(t), xt(t), vec[:, 5, :], ALU.add).then_inc(s["beta"], 1)
            for m in range(3):
                token_rows(m, m)
            with pool.Fori(0, MT // 4 - 1) as i:
                for k in range(4):
                    token_rows(4 * i + k + 3, (k + 3) % 4)
                    expert_rows(4 * i + k, k)
            for m in range(MT - 4, MT):
                if m + 3 < MT:
                    token_rows(m + 3, (m + 3) % 4)
                expert_rows(m, m % 4)

        @block.scalar
        def _(act):
            A = nc.scalar.activation
            act.wait_ge(s["cst"], 16)
            eps = cs[:, C_LN:C_LN + 1]
            def totals_out(c):
                for q in range(NQ):
                    n = min(4, NB - 4 * q)
                    after(act, "tot", c * NQ + q)
                    A(T[:, 4 * q:4 * q + n, 0:CC], brank[q % 4][:, 0:n * CC].rearrange("p (b t) -> p b t", t=CC), ACT.Copy).then_inc(s["tcp"], 1)
            totals_out(0)
            act.wait_ge(s["stat"], 1)
            A(rstd[:, :], mv[:, :].rearrange("p (t k) -> p t k", k=2)[:, :, 1], ACT.Sqrt, bias=eps).then_inc(s["sd"], 1)

            def xT_copy(t, r):
                after(act, "xT", t)
                after(act, "vsp", t - P1)
                A(xT[:, r, :], btr[:, 0:D], ACT.Copy).then_inc(s["xTc"], 1)

            def elu_parts(t, r):
                after(act, "kqp", t)
                after(act, "kqs", t - P1)
                A(Er[:, r, :], bkq[:, :], ACT.Exp)
                A(Rr[:, r, :], bkq[:, :], ACT.Relu).then_inc(s["elu"], 1)

            def qT_copy(t, r):
                after(act, "qTp", t)
                after(act, "out1", t - P1)
                A(qT[:, r, :], bqT[:, 0:D], ACT.Copy).then_inc(s["qTc"], 1)

            def values(turn, j):
                b, r = batch_of(j)
                if j == BATCH[b][0]:
                    after(act, "oh", turn * len(BATCH) + b)
                after(act, "smm", turn * SORT + j - SORT)
                A(OV[:, j, 0, :], O[:, oslot(b), r, :], ACT.Copy, scale=wt[:, ds(turn * SORT + j, 1)])
                last = A(OV[:, j, 1, :], O[:, oslot(b), r, :], ACT.Copy, scale=eid[:, ds(turn * SORT + j, 1)])
                last.then_inc(s["ov"], 1)

            def round1(i):
                for a in range(P1):
                    t = P1 * i + a
                    for j in range(*BATCH[a]):
                        values(i, j)
                    elu_parts(t, a)
                    xT_copy(t + 1, (a + 1) % P1)
                    qT_copy(t, a)
            xT_copy(0, 0)
            with act.Fori(0, NCH - 1) as q:
                round1(2 * q)
                totals_out(q + 1)
                round1(2 * q + 1)
            with act.Fori(2 * NCH - 2, TT // P1) as i:
                round1(i)
            elu_parts(TT - 1, 0)
            qT_copy(TT - 1, 0)

            def mix_mid(t):
                act.wait_ge(s["mstat"], t + 1)
                A(sm[:, 8:9], sm[:, 7:8], ACT.Sqrt, bias=eps).then_inc(s["msd"], 1)

            def mix_x1T(t):
                act.wait_ge(s["mxt"], t + 1)
                A(x1T[:, 0, :], btr[:, 0:P], ACT.Identity, scale=colsb[:, 0:1], bias=colsb[:, 2:3])
                A(x1T[:, 1, :], btr[:, P:2 * P], ACT.Identity, scale=colsb[:, 1:2], bias=colsb[:, 3:4]).then_inc(s["mxc"], 1)

            def mix_gelu(t):
                act.wait_ge(s["mhp"], t + 1)
                for o in range(2):
                    last = A(hTm[:, o, :], bh[:, o * P:(o + 1) * P], ACT.Gelu, bias=colsb[:, 4 + o:5 + o])
                last.then_inc(s["mg"], 1)

            def mix_end(t):
                act.wait_ge(s["mst2"], t + 1)
                A(sm[:, 18:19], sm[:, 17:18], ACT.Sqrt, bias=eps).then_inc(s["msd2"], 1)

            def turn_act(turn, t):
                for j in range(SORT):
                    values(turn, j)
                    if j == 3:
                        mix_mid(t)
                    if j == 6:
                        mix_x1T(t)
                    if j == 9:
                        mix_gelu(t)
                    if j == 12:
                        mix_end(t)
            act.wait_ge(s["colsb"], 16)
            with act.Fori(0, (NCH - 1) * (ST // U)) as i:
                turn_act(i + CC // SORT, i)
            mix_mid(TT - 1)
            mix_x1T(TT - 1)
            mix_gelu(TT - 1)
            mix_end(TT - 1)

            act.wait_ge(s["rstat"], 2)
            A(rstd[:, :], mv[:, :].rearrange("p (t k) -> p t k", k=2)[:, :, 1], ACT.Sqrt, bias=eps).then_inc(s["rsd"], 1)

            def x2T_copy(t, r):
                after(act, "rT", t)
                after(act, "rlg", t - 2)
                A(x2T[:, r, :], (btr, bspare)[r][:, 0:D], ACT.Copy).then_inc(s["rTc"], 1)
            with act.Fori(0, TT // 2) as i:
                x2T_copy(2 * i, 0)
                x2T_copy(2 * i + 1, 1)
            x2T_copy(TT - 1, 0)
            act.wait_ge(s["route"], 1)
            A(gw_[:, 1, :], pl[:, 3, 0:TT], ACT.Exp).then_inc(s["route"], 1)
            for q in range(2):
                act.wait_ge(s["rtot"], q + 1)
                A(TM[:, 8 * q:8 * q + 8, 0:PT], B[1 + q][:, 0:8 * PT].rearrange("p (b t) -> p b t", t=PT), ACT.Copy).then_inc(s["rtcp"], 1)

            def xT2_copy(m, r):
                after(act, "xt2", m)
                after(act, "hp", m - 2)
                A(x2T[:, r, :], btr[:, 0:D], ACT.Copy).then_inc(s["xt2c"], 1)

            def relu(m, k, e):
                after(act, "htp", m)
                after(act, "yp", m - 2)
                for c in range(4):
                    last = A(hT[:, k % 2, c, :], B[3 + k % 2][:, c * P:(c + 1) * P], ACT.Relu, bias=b1s[:, ds(e * 4 + c, 1)])
                last.then_inc(s["htc"], 1)
            act.wait_ge(s["rslot"], 1)
            act.wait_ge(s["expert"], 64)
            eregs = [act.alloc_register(f"act_e{k}") for k in range(4)]
            xT2_copy(0, 0)
            xT2_copy(1, 1)
            with act.Fori(0, MT // 4 - 1) as i:
                act.load(eregs, etab[0:1, ds(i * 4, 4)])
                for k in range(4):
                    relu(4 * i + k, k, act.snap(eregs[k], min_val=0, max_val=E - 1))
                    xT2_copy(4 * i + k + 2, k % 2)
            act.load(eregs, etab[0:1, MT - 4:MT])
            for k in range(4):
                relu(MT - 4 + k, k, act.snap(eregs[k], min_val=0, max_val=E - 1))
                if k < 2:
                    xT2_copy(MT - 2 + k, k % 2)

            act.wait_ge(s["tst"], 1)
            A(rstd[:, :], mv[:, :].rearrange("p (t k) -> p t k", k=2)[:, :, 1], ACT.Sqrt, bias=eps).then_inc(s["tsd"], 1)
            act.wait_ge(s["trs"], 1)

            def tail_norm(t, r):
                after(act, "tnorm", t - 2)
                A(yn[:, r, :], u[:, ds(t * D, D)], ACT.Identity, scale=rstd[:, ds(t, 1)], bias=nmr[:, ds(t, 1)]).then_inc(s["tb"], 1)
            with act.Fori(0, TT // 2) as i:
                tail_norm(2 * i, 0)
                tail_norm(2 * i + 1, 1)
            tail_norm(TT - 1, 0)

        @block.vector
        def _(dve):
            v = nc.vector
            TS, TTo, STT = v.tensor_scalar, v.tensor_tensor, v.scalar_tensor_tensor
            v.memset(srci[:, :], NB * P)
            v.memset(dsti[:, :], 0)
            v.memset(wt[:, :], 0.0)
            v.memset(xa[:, (TT - 1) * D:TT * D], 0.0).then_inc(s["setup"], 1)
            v.memset(ones_b[:, :], 1.0)
            v.memset(ones_f[:, :], 1.0)
            dve.wait_ge(s["cst"], 16)
            v.tensor_copy(negtri[:, :], cs[:, C_NEG:C_NEG + P])
            dve.wait_ge(s["src"], 32)
            dve.wait_ge(s["dst"], 32)
            dve.wait_ge(s["ew"], 32)
            TS(loi[:, :], srci[:, :], P - 1, None, ALU.bitwise_and)
            TS(srci[:, :], srci[:, :], 7, None, ALU.arith_shift_right)
            dve.drain()
            v.tensor_copy(lohi[:, 1, :], srci[:, :])
            STT(eid[:, :], dsti[:, :], float(P), loi[:, :], ALU.mult, ALU.add)
            dve.drain()

            def buckets(c):
                TTo(M[:, :, :], lohi[:, 1, ds(c * CC, CC)].unsqueeze(1).broadcast_to([P, NB, CC]),
                    cs[:, C_IOTA:C_IOTA + NB].unsqueeze(2).broadcast_to([P, NB, CC]), ALU.is_equal).then_inc(s["mready"], 1)

            def bucket_sums(c):
                after(dve, "tcp", c * NQ + NQ - 1)
                v.tensor_reduce(nb_[:, :], T[:, :, 0:CC], AX.X, ALU.add)
                dve.drain()
                TS(nb_[:, :], nb_[:, :], float(P - 1), None, ALU.add)
                dve.drain()
                v.tensor_copy(nbi[:, :], nb_[:, :])
                dve.drain()
                TS(nbi[:, :], nbi[:, :], 7, 7, ALU.arith_shift_right, ALU.arith_shift_left)
                dve.drain()
                v.tensor_copy(endb[:, 0:NB], nbi[:, :])
                dve.drain()
                TTo(nb_[:, :], endb[:, 0:NB], nb_[:, :], ALU.subtract)
                dve.drain()
                TS(T[:, :, CC], nb_[:, :], float(P - 1), None, ALU.add)
                dve.drain()
                Tf = T[:, :, :].rearrange("p b t -> p (b t)")
                v.tensor_tensor_scan(S[:, :, :].rearrange("p b t -> p (b t)"), Tf, Tf, 0.0, ALU.add, ALU.bypass)
                dve.drain()
                v.tensor_copy(endb[:, 0:NB], S[:, :, CC])
                dve.drain()
                TS(nb_[:, :], endb[:, 0:NB], cs[:, C_SLOT:C_SLOT + 1], 0.0, ALU.is_le, ALU.add, accum_out=endb[:, 31:32])
                dve.drain()
                TS(endb[:, 30:31], endb[:, 31:32], float(NB - 1), None, ALU.min)
                dve.drain()
                TS(dcol[:, :], ident, endb[:, 30:31], None, ALU.mult).then_inc(s["dcolr"], 1)

            def places(c):
                for q in range(NQ):
                    n = min(4, NB - 4 * q)
                    after(dve, "pmul", c * NQ + q)
                    TTo(V[:, 4 * q:4 * q + n, :], brank[q % 4][:, 0:n * CC].rearrange("p (b t) -> p b t", t=CC),
                        S[:, 4 * q:4 * q + n, 0:CC], ALU.add).then_inc(s["filled"], 1)
                dve.drain()
                TTo(V[:, :, :], V[:, :, :], M[:, :, :], ALU.mult)
                dve.drain()
                lc, hc = lohi[:, 0, ds(c * CC, CC)], lohi[:, 1, ds(c * CC, CC)]
                v.tensor_reduce(lc, V[:, :, :].rearrange("p b t -> p t b"), AX.X, ALU.add)
                dve.drain()
                TS(lc, lc, -1.0, None, ALU.add)
                dve.drain()
                v.tensor_copy(posi[:, :], lc)
                dve.drain()
                TS(loi[:, 0:CC], posi[:, :], P - 1, None, ALU.bitwise_and)
                TS(posi[:, :], posi[:, :], 7, None, ALU.arith_shift_right)
                dve.drain()
                v.tensor_copy(lc, loi[:, 0:CC])
                v.tensor_copy(hc, posi[:, :])
                after(dve, "bt", c)
                v.tensor_copy(btab[0:1, ds(c * P, ST)], bspare[0:1, 0:ST]).then_inc(s["pos"], 1)
                dve.drain()
            buckets(0)
            bucket_sums(0)
            places(0)

            for i, (a, b) in enumerate(x_parts):
                dve.wait_ge(s_x[i], 16 if b < TT else 32)
                for t in range(a, b):
                    v.bn_stats(stats[:, 6 * t:6 * t + 6], xa[:, t * D:(t + 1) * D])
            dve.drain()
            for t in range(TT):
                last = v.bn_aggr(mv[:, 2 * t:2 * t + 2], stats[:, 6 * t:6 * t + 6])
            last.then_inc(s["stat"], 1)
            dve.wait_ge(s["vec"], 16)
            TTo(cb[:, :], vec[:, 2, :], vec[:, 3, :], ALU.add)
            dve.wait_ge(s["sd"], 1)
            v.reciprocal(rstd[:, :], rstd[:, :])
            dve.wait_ge(s["prep"], 1)
            dve.drain()

            def xn(t, r):
                after(dve, "xT", t - P1)
                after(dve, "out1", t - P1)
                TS(xr[:, r, :], xt(t), mv[:, ds(2 * t, 1)], rstd[:, ds(t, 1)], ALU.subtract, ALU.mult).then_inc(s["xn"], 1)

            def kqv(t, r):
                after(dve, "elu", t)
                after(dve, "kvmm", t - P1)
                STT(kq[:, r, :], Er[:, r, :], 1.0, Rr[:, r, :], ALU.min, ALU.add).then_inc(s["kqs"], 1)
                after(dve, "vsp", t)
                after(dve, "out1", t - P1)
                v.tensor_copy(vs[:, r, :, 0:P], bvs[:, :].rearrange("p (a b) -> p a b", a=4)).then_inc(s["vsc"], 1)

            def onehot(turn, b):
                j0, j1 = BATCH[b]
                n = j1 - j0
                after(dve, "smm", turn * SORT + j1 - 1 - SORT)
                for tab, dst_ in ((0, L[:, j0:j1, :]), (1, O[:, oslot(b), 0:n, :])):
                    if tab:
                        after(dve, "ov", turn * SORT + ov_before(b))
                    last = TTo(dst_, cs[:, C_IOTA:C_IOTA + P].unsqueeze(1).broadcast_to([P, n, P]),
                               lohi[:, tab, ds(turn * SORT + j0, n)].unsqueeze(2).broadcast_to([P, n, P]), ALU.is_equal)
                last.then_inc(s["oh"], 1)

            def round1(i):
                for a in range(P1):
                    t = P1 * i + a
                    xn(t + 1, (a + 1) % P1)
                    onehot(i, a)
                    kqv(t, a)
            xn(0, 0)
            with dve.Fori(0, NCH - 1) as q:
                buckets(q + 1)
                round1(2 * q)
                bucket_sums(q + 1)
                round1(2 * q + 1)
                places(q + 1)
            with dve.Fori(2 * NCH - 2, TT // P1) as i:
                round1(i)
            kqv(TT - 1, 0)
            after(dve, "kvmm", TT - 1)
            for h in range(2):
                src_b = (bkv0, bkv1)[h]
                for k in range(4):
                    p0 = 32 * k
                    v.tensor_copy(KV[p0:p0 + 32, h, p0:p0 + 32], src_b[p0:p0 + 32, p0:p0 + 32])
                    v.tensor_copy(KV[p0:p0 + 32, h, P + k:P + k + 1], src_b[p0:p0 + 32, P:P + 1])
            dve.drain()
            dve.sem_inc(s["kvdone"], 1)

            def records(c):
                after(dve, "sorted", c)
                v.tensor_copy(reci[:, 0, :], bsort[:, P:2 * P])
                v.tensor_copy(rec[:, 0, :], bsort[:, 0:P])
                dve.drain()
                TS(reci[:, 1, :], reci[:, 0, :], P - 1, None, ALU.bitwise_and)
                TS(reci[:, 2, :], reci[:, 0, :], 7, None, ALU.arith_shift_right)
                dve.drain()
                v.tensor_copy(rec[:, 1, :], reci[:, 1, :]).then_inc(s["recs"], 1)
                dve.drain()

            def window(at):
                v.tensor_copy(win[:, :, :], rec[:, :, ds(at * U, U)]).then_inc(s["win"], 1)

            def indices(turn, h, at):
                after(dve, "msg", turn * U + (h + 1) * HU - 1 - U)
                v.tensor_copy(idxw[:, h * HU:(h + 1) * HU], reci[:, 2, ds(at * U + h * HU, HU)]).then_inc(s["idx"], 1)

            def select(k):
                TS(sel[:, k, :], iota, win[:, 1, k:k + 1], win[:, 0, k:k + 1], ALU.is_equal, ALU.mult).then_inc(s["sel"], 1)

            def mix_a(t):
                dve.wait_ge(s["mt"], t + 1)
                den = bt[:, 0:264].rearrange("p (h c) -> p h c", h=2)
                TS(sm[:, 20:28].rearrange("p (h c) -> p h c", h=2), den[:, :, P:P + 4], 1e-6, None, ALU.add)
                dve.drain()
                v.reciprocal(sm[:, 28:36], sm[:, 20:28])
                dve.drain()
                for h in range(2):
                    TTo(mu[:, h * P:(h + 1) * P].rearrange("p (k m) -> p k m", k=4), den[:, h, 0:P].rearrange("p (k m) -> p k m", k=4),
                        sm[:, 28 + 4 * h:32 + 4 * h].unsqueeze(2).broadcast_to([P, 4, 32]), ALU.mult)
                dve.drain()
                TTo(mu[:, :], mu[:, :], mr[:, D:2 * D], ALU.add).then_inc(s["mrf"], 1)
                dve.drain()
                v.bn_stats(sm[:, 0:6], mu[:, :])
                dve.drain()
                v.bn_aggr(sm[:, 6:8], sm[:, 0:6]).then_inc(s["mstat"], 1)

            def mix_b(t):
                dve.wait_ge(s["msd"], t + 1)
                v.reciprocal(sm[:, 9:10], sm[:, 8:9])
                dve.drain()
                TS(xh[:, :], mu[:, :], sm[:, 6:7], sm[:, 9:10], ALU.subtract, ALU.mult).then_inc(s["mxh"], 1)

            def mix_c(t):
                dve.wait_ge(s["my"], t + 1)
                TTo(y2[:, :], by[:, 0:D], vec[:, 0, :], ALU.add)
                dve.drain()
                v.bn_stats(sm[:, 10:16], y2[:, :])
                dve.drain()
                v.bn_aggr(sm[:, 16:18], sm[:, 10:16]).then_inc(s["mst2"], 1)

            def mix_d(t):
                dve.wait_ge(s["msd2"], t + 1)
                v.reciprocal(sm[:, 19:20], sm[:, 18:19])
                dve.drain()
                TS(y2[:, :], y2[:, :], sm[:, 16:17], sm[:, 19:20], ALU.subtract, ALU.mult)
                dve.drain()
                TTo(y2[:, :], y2[:, :], vec[:, 1, :], ALU.mult)
                dve.drain()
                TTo(xt(t), xt(t), y2[:, :], ALU.add)
                dve.drain()

            regs = [dve.alloc_register(f"bucket{k}") for k in range(U)]

            def turn_dve(turn, at, base, sort_turn, mix, last):
                dve.load(regs, btab[0:1, ds(base + at * U, U)])

                def add(k):
                    b = dve.snap(regs[k], min_val=0, max_val=NB - 1)
                    after(dve, "msg", turn * U + k)
                    after(dve, "add", turn * U + k - 1)
                    TTo(xt(b), xt(b), bmsg[k % 4][:, 0:D], ALU.add).then_inc(s["add"], 1)
                for k in range(U):
                    if k < HU:
                        select(k + HU)
                    elif not last:
                        if k == HU:
                            after(dve, "sel", turn * U + U - 1)
                            window(at + 1)
                        if k >= HU + 2:
                            if k == HU + 2:
                                after(dve, "win", turn + 1)
                                select(0)
                                select(1)
                                indices(turn + 1, 0, at + 1)
                            select(k - HU)
                    if sort_turn is not None and k in (0, 4, 8):
                        onehot(sort_turn, k // 4)
                    if k >= 2:
                        add(k - 2)
                    if mix is not None:
                        if k == 4:
                            mix_a(mix)
                        if k == 6:
                            mix_b(mix)
                        if k == 14:
                            mix_c(mix)
                add(U - 2)
                add(U - 1)
                if not last:
                    indices(turn + 1, 1, at + 1)
                if mix is not None:
                    mix_d(mix)
                else:
                    dve.drain()

            def chunk_start(c, turn):
                records(c)
                window(0)
                indices(turn, 0, 0)
                indices(turn, 1, 0)
                after(dve, "win", turn)
                for k in range(HU):
                    select(k)

            dve.wait_ge(s["xcb"], TT)
            TL = ST // U
            chunk_start(0, 0)
            with dve.Fori(0, NCH - 1) as c:
                with dve.Fori(0, TL - 1) as i:
                    turn_dve(c * TL + i, i, c * P, c * TL + i + TL, c * TL + i, False)
                turn_dve(c * TL + TL - 1, TL - 1, c * P, c * TL + 2 * TL - 1, c * TL + TL - 1, True)
                chunk_start(c + 1, (c + 1) * TL)
            c = NCH - 1
            mix_a(TT - 1)
            mix_b(TT - 1)
            mix_c(TT - 1)
            mix_d(TT - 1)
            with dve.Fori(0, TL - 1) as i:
                turn_dve(c * TL + i, i, c * P, None, None, False)
            turn_dve(c * TL + TL - 1, TL - 1, c * P, None, None, True)

            dve.sem_inc(s["rstat"], 1)
            for t in range(TT):
                v.bn_stats(stats[:, 6 * t:6 * t + 6], xa[:, t * D:(t + 1) * D])
            dve.drain()
            for t in range(TT):
                last = v.bn_aggr(mv[:, 2 * t:2 * t + 2], stats[:, 6 * t:6 * t + 6])
            last.then_inc(s["rstat"], 1)
            dve.wait_ge(s["rsd"], 1)
            v.reciprocal(rstd[:, :], rstd[:, :])
            dve.wait_ge(s["expert"], 64)
            dve.drain()

            def xn2(t, r):
                after(dve, "rT", t - 4)
                after(dve, "rout", t - 4)
                after(dve, "ucp", t - 4)
                TS(x2[:, r, :], xt(t), mv[:, ds(2 * t, 1)], rstd[:, ds(t, 1)], ALU.subtract, ALU.mult).then_inc(s["rx"], 1)

            def logits(t, r):
                after(dve, "rlg", t)
                TTo(LG[:, ds(t * E, E)], B[1 + r][:, 0:E], gbs[:, :], ALU.add).then_inc(s["rlgc"], 1)
            for t in range(4):
                xn2(t, t)
            with dve.Fori(0, (TT - 4) // 4) as i:
                for r in range(4):
                    logits(4 * i + r, r % 2)
                    xn2(4 * i + r + 4, r)
            t = TT - 5
            logits(t, t % 2)
            xn2(t + 4, t % 4)
            for t in range(TT - 4, TT):
                logits(t, t % 2)
            dve.drain()
            for t in range(TT):
                v.max(V8[:, t, :], LG[:, t * E:(t + 1) * E])
            dve.drain()
            for t in range(TT):
                v.max_index(I8[:, t, :], V8[:, t, :], LG[:, t * E:(t + 1) * E])
            TTo(pl[:, 3, 0:TT], V8[:, :, 1], V8[:, :, 0], ALU.subtract).then_inc(s["route"], 1)
            dve.drain()
            for k in range(2):
                v.tensor_copy(IF[:, k, :], I8[:, :, k])
            dve.drain()
            for k in range(2):
                TTo(IF[:, k, :], IF[:, k, :], cs[:, C_INV:C_INV + TT], ALU.add)
            dve.drain()
            TTo(MM[:, :, :], IF[:, :, :].rearrange("p k t -> p (k t)").unsqueeze(1).broadcast_to([P, E, PT]),
                cs[:, C_IOTA:C_IOTA + E].unsqueeze(2).broadcast_to([P, E, PT]), ALU.is_equal).then_inc(s["mready"], 1)
            dve.wait_ge(s["route"], 2)
            TS(gw_[:, 0, :], gw_[:, 1, :], 1.0, None, ALU.add)
            dve.drain()
            v.reciprocal(gw_[:, 0, :], gw_[:, 0, :])
            dve.drain()
            TTo(gw_[:, 1, :], gw_[:, 1, :], gw_[:, 0, :], ALU.mult)
            dve.wait_ge(s["rtcp"], 2)
            v.tensor_reduce(n16[:, :], TM[:, :, 0:PT], AX.X, ALU.add)
            dve.drain()
            TS(n16[:, :], n16[:, :], float(P - 1), None, ALU.add)
            dve.drain()
            v.tensor_copy(n16i[:, :], n16[:, :])
            dve.drain()
            TS(n16i[:, :], n16i[:, :], 7, 7, ALU.arith_shift_right, ALU.arith_shift_left)
            dve.drain()
            v.tensor_copy(mcol[:, 0:E], n16i[:, :])
            dve.drain()
            TTo(n16[:, :], mcol[:, 0:E], n16[:, :], ALU.subtract)
            dve.drain()
            TS(TM[:, :, PT], n16[:, :], float(P - 1), None, ALU.add)
            dve.drain()
            TMf = TM[:, :, :].rearrange("p b t -> p (b t)")
            v.tensor_tensor_scan(SM[:, :, :].rearrange("p b t -> p (b t)"), TMf, TMf, 0.0, ALU.add, ALU.bypass)
            dve.drain()
            for q in range(2):
                dve.wait_ge(s["rpos"], q + 1)
                TTo(VM[:, 8 * q:8 * q + 8, :], B[3 + q][:, 0:8 * PT].rearrange("p (b t) -> p b t", t=PT), SM[:, 8 * q:8 * q + 8, 0:PT], ALU.add)
            v.tensor_copy(mcol[:, 0:E], SM[:, :, PT])
            dve.drain()
            TTo(VM[:, :, :], VM[:, :, :], MM[:, :, :], ALU.mult)
            TS(n16[:, :], mcol[:, 0:E], cs[:, C_SLOT:C_SLOT + 1], 0.0, ALU.is_le, ALU.add, accum_out=mcol[:, 31:32])
            dve.drain()
            v.tensor_reduce(pl[:, 0, :], VM[:, :, :].rearrange("p b t -> p t b"), AX.X, ALU.add)
            TS(mcol[:, 30:31], mcol[:, 31:32], float(E - 1), None, ALU.min)
            dve.drain()
            TS(mdiag[:, :], ident[:, 0:MT], mcol[:, 30:31], None, ALU.mult).then_inc(s["rdc"], 1)
            TS(pl[:, 0, :], pl[:, 0, :], -1.0, None, ALU.add)
            dve.drain()
            v.tensor_copy(pli[:, :], pl[:, 0, :])
            dve.drain()
            TS(sloti[:, 0, 0:PT], pli[:, :], P - 1, None, ALU.bitwise_and)
            TS(pli[:, :], pli[:, :], 7, None, ALU.arith_shift_right)
            dve.drain()
            v.tensor_copy(pl[:, 0, :], sloti[:, 0, 0:PT])
            v.tensor_copy(pl[:, 1, :], pli[:, :])
            dve.drain()
            for q in range(PQ):
                a, b = q * PB, (q + 1) * PB
                TTo(LM[:, a:b, :], iota.unsqueeze(1).broadcast_to([P, PB, P]), pl[:, 0, a:b].unsqueeze(2).broadcast_to([P, PB, P]), ALU.is_equal)
                TTo(OM[:, a:b, 0, :], iota[:, 0:MT].unsqueeze(1).broadcast_to([P, PB, MT]), pl[:, 1, a:b].unsqueeze(2).broadcast_to([P, PB, MT]), ALU.is_equal)
                dve.drain()
                TTo(OM[:, a:b, 1, :], OM[:, a:b, 0, :], iota[:, a:b].unsqueeze(2).broadcast_to([P, PB, MT]), ALU.mult)
                dve.drain()
                TS(OM[:, a:b, 0, :], OM[:, a:b, 0, :], cs[:, C_ROW:C_ROW + 1], None, ALU.mult).then_inc(s["roh"], 1)
            dve.wait_ge(s["rdcp"], 1)
            v.tensor_copy(etab[0:1, 0:MT], B[1][0:1, 0:MT])
            dve.wait_ge(s["rmm"], 1)
            v.tensor_copy(slotf[:, 0, :], B[2][:, 0:MT])
            v.tensor_copy(slotf[:, 1, :], B[2][:, MT:2 * MT])
            dve.drain()
            TS(slotf[:, 2, :], slotf[:, 1, :], float(TT), None, ALU.is_ge)
            TS(slotf[:, 3, :], slotf[:, 0, :], 2.0, -1.0, ALU.mult, ALU.add)
            dve.drain()
            STT(slotf[:, 1, :], slotf[:, 2, :], float(-TT), slotf[:, 1, :], ALU.mult, ALU.add)
            TTo(slotf[:, 3, :], slotf[:, 3, :], slotf[:, 2, :], ALU.add)
            dve.drain()
            STT(slotf[:, 3, :], slotf[:, 1, :], 2.0 * P, slotf[:, 3, :], ALU.mult, ALU.add)
            TS(slotf[:, 2, :], slotf[:, 0, :], 1.0, None, ALU.min)
            dve.drain()
            TTo(slotf[:, 0, :], slotf[:, 3, :], slotf[:, 2, :], ALU.mult)
            dve.drain()
            TS(slotf[:, 1, :], slotf[:, 0, :], -1.0, 0.0, ALU.add, ALU.max)
            TS(slotf[:, 2, :], iota[:, 0:MT], float(P), cs[:, C_AT:C_AT + 1], ALU.mult, ALU.add)
            TS(slotf[:, 3, :], slotf[:, 0, :], 0.0, None, ALU.is_equal)
            v.memset(sloti[:, 0, MT:MT + 4], 0)
            dve.drain()
            TTo(slotf[:, 3, :], slotf[:, 3, :], slotf[:, 2, :], ALU.mult)
            dve.drain()
            TTo(slotf[:, 3, :], slotf[:, 1, :], slotf[:, 3, :], ALU.add)
            v.tensor_copy(sloti[:, 0, 0:MT], slotf[:, 1, :])
            dve.drain()
            TS(sloti[:, 0, 0:MT], sloti[:, 0, 0:MT], 1, None, ALU.arith_shift_right)
            v.tensor_copy(sloti[:, 1, 0:MT], slotf[:, 3, :])
            dve.drain()
            dve.sem_inc(s["rslot"], 1)

            def token_index(m, k):
                v.tensor_copy(gi[:, k:k + 1], sloti[:, 0, ds(m, 1)]).then_inc(s["fidx"], 1)

            def hidden(m, k):
                after(dve, "hp", m)
                after(dve, "htp", m - 2)
                v.tensor_copy(hs[:, k % 2, :], B[1 + k % 2][:, :]).then_inc(s["hc"], 1)

            def result(m, k, turn, e):
                if not isinstance(turn, int) or turn > 0:
                    dve.wait_ge(s_sc[k], 16 * turn)
                v.tensor_copy(si[:, k:k + 1], sloti[:, 1, ds(m, 1)])
                after(dve, "yp", m)
                TTo(yo[:, k, :], B[5 + k % 2][:, 0:D], b2s[:, :, :].rearrange("p e d -> p (e d)")[:, ds(e * D, D)], ALU.add).then_inc(s["yc"], 1)
            for m in range(4):
                token_index(m, m)
            ereg = [dve.alloc_register(f"dve_e{k}") for k in range(4)]
            hidden(0, 0)
            hidden(1, 1)

            def four(turn, end=False):
                dve.load(ereg, etab[0:1, ds(4 * turn, 4)])
                for k in range(4):
                    m = 4 * turn + k
                    result(m, k, turn, dve.snap(ereg[k], min_val=0, max_val=E - 1))
                    if not end:
                        token_index(m + 4, k)
                    if not end or k < 2:
                        hidden(m + 2, k)
            four(0)
            with dve.Fori(1, MT // 4 - 1) as i:
                four(i)
            four(MT // 4 - 1, end=True)

            after(dve, "ucp", TT - 1)

            def combine(t, r, rnd, rows_=P):
                dve.wait_ge(s[f"tld{r}"], 16 * (rnd + 1))
                ut = u[0:rows_, ds(t * D, D)]
                STT(yc2[0:rows_, r, :], yl[0:rows_, r, 0:D], gw_[0:rows_, 0, ds(t, 1)], ut, ALU.mult, ALU.add).then_inc(s["si"], 1)

            def combine2(t, r, rows_=P):
                ut = u[0:rows_, ds(t * D, D)]
                dve.wait_ge(s["si"], t + 1)
                STT(ut, yl[0:rows_, r, D:2 * D], gw_[0:rows_, 1, ds(t, 1)], yc2[0:rows_, r, :], ALU.mult, ALU.add).then_inc(s["tcomb"], 1)

            def stats3(t):
                after(dve, "tcomb", t)
                v.bn_stats(stats[:, ds(6 * t, 6)], xu(t))
            with dve.Fori(0, TT // 3) as i:
                for r in range(3):
                    combine(3 * i + r, r, i)
                for r in range(3):
                    combine2(3 * i + r, r)
                for r in range(3):
                    stats3(3 * i + r)
            combine(TT - 1, 0, TT // 3, LAST)
            combine2(TT - 1, 0, LAST)
            stats3(TT - 1)
            dve.drain()
            for t in range(TT):
                last = v.bn_aggr(mv[:, 2 * t:2 * t + 2], stats[:, 6 * t:6 * t + 6])
            last.then_inc(s["tst"], 1)
            dve.wait_ge(s["tsd"], 1)
            v.reciprocal(rstd[:, :], rstd[:, :])
            dve.drain()
            STT(nmr[:, :], mv[:, :].rearrange("p (t k) -> p t k", k=2)[:, :, 0], -1.0, rstd[:, :], ALU.mult, ALU.mult).then_inc(s["trs"], 1)
            dve.wait_ge(s["beta"], TT)

            def scale_(t, r, r3):
                dve.wait_ge(s["tb"], t + 1)
                after(dve, "tout", t - 3)
                TTo(yo[:, r3, :], yn[:, r, :], vec[:, 4, :], ALU.mult).then_inc(s["tnorm"], 1)

            def finish(t, r3):
                after(dve, "tnorm", t)
                TTo(yo[:, r3, :], yo[:, r3, :], xt(t), ALU.add).then_inc(s["tfin"], 1)
            scale_(0, 0, 0)
            with dve.Fori(0, TT // 6) as i:
                for r in range(6):
                    scale_(6 * i + r + 1, (r + 1) % 2, (r + 1) % 3)
                    finish(6 * i + r, r % 3)
            finish(TT - 1, (TT - 1) % 3)

        @block.tensor
        def _(pe):
            mm, tr = nc.tensor.matmul, nc.tensor.transpose
            for n, k in credit.items():
                pe.sem_inc(s[n], k)

            Mf = M[:, :, :].rearrange("p b t -> p (b t)")

            def count(c):
                after(pe, "mready", c)
                for q in range(NQ):
                    a, b = 4 * q * CC, min(4 * q + 4, NB) * CC
                    if q >= 4:
                        after(pe, "tcp", c * NQ + q - 4)
                    mm(brank[q % 4][:, 0:b - a], ones_b[:, :], Mf[:, a:b], start=True, stop=True).then_inc(s["tot"], 1)
                after(pe, "tcp", c * NQ + NQ - 1)

            def behind(c):
                after(pe, "dcolr", c)
                for q in range(NQ):
                    a, b = 4 * q * CC, min(4 * q + 4, NB) * CC
                    if q >= 4:
                        after(pe, "filled", c * NQ + q - 4)
                    mm(brank[q % 4][:, 0:b - a], negtri[:, :], Mf[:, a:b], start=True, stop=True).then_inc(s["pmul"], 1)
                after(pe, "filled", c * NQ + NQ - 1)
                mm(bspare[:, 0:P], ones_f[:, :], dcol[:, :], start=True, stop=True).then_inc(s["bt"], 1)
            count(0)
            behind(0)
            after(pe, "pos", 0)

            def T_(t, r):
                after(pe, "xn", t)
                after(pe, "xTc", t - 1)
                for k in range(2):
                    last = tr(btr[:, k * P:(k + 1) * P], xr[:, r, k * P:(k + 1) * P], ident)
                last.then_inc(s["xT"], 1)

            def KQ(t, r):
                after(pe, "xTc", t)
                after(pe, "elu", t - 1)
                for k in range(2):
                    last = mm(bkq[:, :], xT[:, r, k * P:(k + 1) * P], wAs[:, k, 0:2 * D], start=(k == 0), stop=(k == 1))
                last.then_inc(s["kqp"], 1)

            def VS(t, r):
                after(pe, "vsc", t - 1)
                for k in range(2):
                    last = mm(bvs[:, :], xT[:, r, k * P:(k + 1) * P], wAs[:, k, 2 * D:4 * D], start=(k == 0), stop=(k == 1))
                last.then_inc(s["vsp"], 1)

            def KVQ(t, r, rows_=P):
                after(pe, "kqs", t)
                after(pe, "vsc", t)
                for h in range(2):
                    mm((bkv0, bkv1)[h][:, 0:P + 1], kq[0:rows_, r, h * P:(h + 1) * P], vs[0:rows_, r, h, 0:P + 1], start=False, stop=False, skip_group_check=True)
                after(pe, "qTc", t - 1)
                for h in range(2):
                    last = tr(bqT[:, h * P:(h + 1) * P], kq[:, r, D + h * P:D + (h + 1) * P], ident)
                last.then_inc(s["qTp"], 1)
                after(pe, "qTp", t)
                pe.sem_inc(s["kvmm"], 1)

            def sort_open():
                mm(bsort[:, 0:2 * P], zeros[:, 0:P], zeros[:, 0:2 * P], start=True, stop=False, skip_group_check=True)

            def sort(turn, j):
                after(pe, "ov", turn * SORT + j)
                mm(bsort[:, 0:2 * P], L[:, j, :], OV[:, j, :, :].rearrange("p a b -> p (a b)"), start=False, stop=False, skip_group_check=True).then_inc(s["smm"], 1)

            def sort_close():
                mm(bsort[:, 0:2 * P], zeros[:, 0:P], zeros[:, 0:2 * P], start=False, stop=True, skip_group_check=True).then_inc(s["sorted"], 1)

            def round1(i):
                for a in range(P1):
                    t = P1 * i + a
                    KQ(t, a)
                    T_(t + 1, (a + 1) % P1)
                    VS(t, a)
                    for j in range(*((0, 4), (4, 8), (8, SORT))[a]):
                        sort(i, j)
                    KVQ(t, a)
            pe.wait_ge(s["wA"], 16)
            pe.wait_ge(s["prep"], 1)
            for h in range(2):
                mm((bkv0, bkv1)[h][:, 0:P + 1], zeros[:, 0:P], zeros[:, 0:P + 1], start=True, stop=False, skip_group_check=True)
            sort_open()
            T_(0, 0)
            with pe.Fori(0, NCH - 1) as q:
                round1(2 * q)
                after(pe, "qTc", 6 * q + 2)
                count(q + 1)
                round1(2 * q + 1)
                after(pe, "qTc", 6 * q + 5)
                behind(q + 1)
                after(pe, "pos", q + 1)
            with pe.Fori(2 * NCH - 2, TT // P1) as i:
                round1(i)
            sort_close()
            KQ(TT - 1, 0)
            VS(TT - 1, 0)
            KVQ(TT - 1, 0, LAST)

            def message(turn, k):
                pe.wait_ge(s_g[k], 16 * turn + 16)
                after(pe, "sel", turn * U + k)
                after(pe, "add", turn * U + k - 4)
                mm(bmsg[k % 4][:, 0:D], sel[:, k, :], g[:, k, :], start=True, stop=True).then_inc(s["msg"], 1)

            def mix_t(t):
                pe.wait_ge(s["mr"], 16 * t + 16)
                for h in range(2):
                    last = mm(bt[:, h * 132:(h + 1) * 132], mr[:, h * P:(h + 1) * P], KV[:, h, :], start=True, stop=True)
                last.then_inc(s["mt"], 1)

            def mix_x(t):
                pe.wait_ge(s["mxh"], t + 1)
                for k in range(2):
                    last = tr(btr[:, k * P:(k + 1) * P], xh[:, k * P:(k + 1) * P], ident)
                last.then_inc(s["mxt"], 1)

            def mix_h(t):
                pe.wait_ge(s["mxc"], t + 1)
                for o in range(2):
                    for k in range(2):
                        last = mm(bh[:, o * P:(o + 1) * P], wms[:, k, 0, o * P:(o + 1) * P], x1T[:, k, :], start=(k == 0), stop=(k == 1))
                last.then_inc(s["mhp"], 1)

            def mix_y(t):
                pe.wait_ge(s["mg"], t + 1)
                mm(by[:, 0:D], hTm[:, 0, :], wms[:, 0, 1, :], start=True, stop=False, skip_group_check=True)
                for k in range(2):
                    mm(by[:, k * P:(k + 1) * P], x1T[:, k, :], ident, start=False, stop=False, skip_group_check=True)
                mm(by[:, 0:D], hTm[:, 1, :], wms[:, 1, 1, :], start=False, stop=True, skip_group_check=True).then_inc(s["my"], 1)

            pe.wait_ge(s["wm"], 16)
            pe.wait_ge(s["kvdone"], 1)

            def turn_pe(turn, sort_turn, t):
                for k in range(U):
                    message(turn, k)
                    if sort_turn is not None and k >= LAG:
                        sort(sort_turn, k - LAG)
                    if t is not None:
                        if k == 1:
                            mix_t(t)
                        if k == 7:
                            mix_x(t)
                        if k == 9:
                            mix_h(t)
                        if k == 12:
                            mix_y(t)
            TL = ST // U
            with pe.Fori(0, NCH - 1) as c:
                after(pe, "recs", c)
                sort_open()
                with pe.Fori(0, TL) as i:
                    turn_pe(c * TL + i, c * TL + i + TL, c * TL + i)
                sort_close()
            mix_t(TT - 1)
            mix_x(TT - 1)
            mix_h(TT - 1)
            mix_y(TT - 1)
            with pe.Fori((NCH - 1) * TL, NCH * TL) as turn:
                turn_pe(turn, None, None)

            def RT(t, r, r2):
                after(pe, "rx", t)
                after(pe, "rTc", t - 2)
                for k in range(2):
                    last = tr((btr, bspare)[r2][:, k * P:(k + 1) * P], x2[:, r, k * P:(k + 1) * P], ident)
                last.then_inc(s["rT"], 1)

            def RL(t, r):
                after(pe, "rTc", t)
                after(pe, "rlgc", t - 2)
                for k in range(2):
                    last = mm(B[1 + r][:, 0:E], x2T[:, r, k * P:(k + 1) * P], gws[:, k, :], start=(k == 0), stop=(k == 1))
                last.then_inc(s["rlg"], 1)
            pe.wait_ge(s["expert"], 64)
            RT(0, 0, 0)
            with pe.Fori(0, TT // 4) as i:
                for r in range(4):
                    RT(4 * i + r + 1, (r + 1) % 4, (r + 1) % 2)
                    RL(4 * i + r, r % 2)
            RL(TT - 1, 0)
            pe.wait_ge(s["mready"], NCH + 1)
            after(pe, "rlgc", TT - 1)
            MMf = MM[:, :, :].rearrange("p b t -> p (b t)")
            for q in range(2):
                mm(B[1 + q][:, 0:8 * PT], ones_b[:, :], MMf[:, 8 * PT * q:8 * PT * (q + 1)], start=True, stop=True).then_inc(s["rtot"], 1)
            for q in range(2):
                mm(B[3 + q][:, 0:8 * PT], negtri[:, :], MMf[:, 8 * PT * q:8 * PT * (q + 1)], start=True, stop=True).then_inc(s["rpos"], 1)
            pe.wait_ge(s["rdc"], 1)
            mm(B[1][:, 0:MT], ones_f[:, :], mdiag[:, :], start=True, stop=True).then_inc(s["rdcp"], 1)

            for q in range(PQ):
                pe.wait_ge(s["roh"], q + 1)
                for n in range(q * PB, (q + 1) * PB):
                    last = mm(B[2][:, 0:2 * MT], LM[:, n, :], OM[:, n, :, :].rearrange("p a b -> p (a b)"), start=(n == 0), stop=(n == PT - 1))
            last.then_inc(s["rmm"], 1)

            def XT(m, k, turn):
                pe.wait_ge(s_gx[k], 16 * (turn + 1))
                after(pe, "xt2c", m - 1)
                for c in range(2):
                    last = tr(btr[:, c * P:(c + 1) * P], gx[:, k, c * P:(c + 1) * P], ident)
                last.then_inc(s["xt2"], 1)

            w1f = w1s[:, :, :, :].rearrange("p e k f -> p (e k f)")

            def HH(m, k, e):
                after(pe, "xt2c", m)
                after(pe, "hc", m - 2)
                for c in range(2):
                    last = mm(B[1 + k % 2][:, :], x2T[:, k % 2, c * P:(c + 1) * P], w1f[:, ds((e * 2 + c) * F, F)], start=(c == 0), stop=(c == 1))
                last.then_inc(s["hp"], 1)

            def HT(m, k):
                after(pe, "hc", m)
                after(pe, "htc", m - 2)
                for c in range(4):
                    last = tr(B[3 + k % 2][:, c * P:(c + 1) * P], hs[:, k % 2, c * P:(c + 1) * P], ident)
                last.then_inc(s["htp"], 1)

            def YY(m, k, turn):
                after(pe, "htc", m)
                pe.wait_ge(s[f"w2l{k}"], 16 * (turn + 1))
                after(pe, "yc", m - 2)
                for c in range(4):
                    last = mm(B[5 + k % 2][:, 0:D], hT[:, k % 2, c, :], w2s[:, k, c, :], start=(c == 0), stop=(c == 3))
                last.then_inc(s["yp"], 1)
            pe.wait_ge(s["rslot"], 1)
            pe.wait_ge(s["w1l"], 32)
            er = [pe.alloc_register(f"pe_e{k}") for k in range(4)]

            def step(m, k, turn, e, end=False):
                HT(m - 1, (k - 1) % 4)
                HH(m, k, e)
                if not end:
                    XT(m + 1, (k + 1) % 4, turn + (k == 3))
                YY(m - 1, (k - 1) % 4, turn - (k == 0))
            pe.load(er, etab[0:1, 0:4])
            XT(0, 0, 0)
            HH(0, 0, pe.snap(er[0], min_val=0, max_val=E - 1))
            XT(1, 1, 0)
            for k in range(1, 4):
                step(k, k, 0, pe.snap(er[k], min_val=0, max_val=E - 1))
            with pe.Fori(1, MT // 4 - 1) as i:
                pe.load(er, etab[0:1, ds(4 * i, 4)])
                for k in range(4):
                    step(4 * i + k, k, i, pe.snap(er[k], min_val=0, max_val=E - 1))
            pe.load(er, etab[0:1, MT - 4:MT])
            for k in range(4):
                step(MT - 4 + k, k, MT // 4 - 1, pe.snap(er[k], min_val=0, max_val=E - 1), end=k == 3)
            HT(MT - 1, 3)
            YY(MT - 1, 3, MT // 4 - 1)


def kernel(**inputs):
    import numpy as np
    import concourse.bacc as bacc
    from concourse.bass_utils import run_bass_kernel_spmd as run

    a = {k: np.asarray(v) for k, v in inputs.items()}
    c = np.ascontiguousarray
    wq, wk, wv = (a["L0_mix_Wqkv"][i * D:(i + 1) * D].T for i in range(3))
    cst = np.zeros((P, CW), np.float32)
    cst[:, C_ID:C_ID + P] = np.eye(P)
    cst[:, C_IOTA:C_IOTA + P] = np.arange(P)
    cst[:, C_NEG:C_NEG + P] = -np.tril(np.ones((P, P)), -1)
    cst[LAST:, C_INV + TT - 1] = 100.0
    cst[:, C_SLOT] = P * np.arange(P)
    cst[:, C_ROW] = np.arange(P) + 1
    cst[:, C_LN] = 1e-5
    cst[:, C_AT] = 2 * TT * P + np.arange(P)
    feed = {
        "x": c(a["x"]), "src": c(a["src"]), "dst": c(a["dst"]), "ew": c(a["edge_weight"]),
        "wA": c(np.concatenate([wk, wq, wv, a["L0_gnn_weight"]], 1)),
        "wm": c(np.stack([a["L0_mix_W1"].T, a["L0_mix_W2"].T], 1)),
        "rows": c(np.stack([a[n] for n in ("L0_mix_b2", "L0_mix_ln2_g", "L0_mix_ln2_b", "L0_gnn_b", "L0_ffn_gamma", "L0_ffn_beta")])),
        "cols": c(np.concatenate([a[n].reshape(2, P).T for n in ("L0_mix_ln1_g", "L0_mix_ln1_b", "L0_mix_b1")], 1)),
        "gate_w": c(a["L0_ffn_gate_w"]), "gate_b": c(a["L0_ffn_gate_b"]),
        "w1": c(a["L0_ffn_w1"]), "b1": c(a["L0_ffn_b1"].reshape(E, 4, P).transpose(2, 0, 1).reshape(P, E * 4)),
        "w2": c(a["L0_ffn_w2"]), "b2": c(a["L0_ffn_b2"]), "cst": cst,
    }
    nc = bacc.Bacc("TRN2", target_bir_lowering=False, num_devices=1)
    args = {k: nc.dram_tensor(f"in_{k}", v.shape, mybir.dt.from_np(v.dtype), kind="ExternalInput").ap() for k, v in feed.items()}
    res = nc.dram_tensor("out_x", (N, D), mybir.dt.float32, kind="ExternalOutput").ap()
    gps_layer(nc, *args.values(), res)
    got = run(nc, [{f"in_{k}": v for k, v in feed.items()}], core_ids=[0])
    return got.results[0]["out_x"]
```

```python
import concourse.bass as bass
from concourse import mybir
from contextlib import ExitStack

N = 3125
D = 256
NE = 53125
P = 128
TT = -(-N // P)
LAST = N - (TT - 1) * P
NB = TT
EC = -(-NE // P)
NCH = 4
CC = EC // NCH
ST = (CC * P + NB * (P - 1)) // P
E = 16
F = 512
PT = 2 * TT
PB = 10
PQ = PT // PB
MT = (2 * N + E * (P - 1)) // P
G = 5
NG = TT // G
YROWS = (2 * TT + MT) * P
U = 16
HU = U // 2
QU = U // 4
SORT = CC // (ST // U)
BATCH = ((0, 5), (5, 9), (9, 13))
NQ = -(-NB // 4)
NR = 2 * NQ + 1
P1 = 3
LAG = 2
EDGES = EC + SORT
assert TT % 4 == 1 and NG * G == TT and CC * NCH == EC and ST % U == 0 and SORT * (ST // U) == CC

C_ID, C_IOTA, C_NEG, C_INV, C_SLOT, C_ROW, C_LN, C_AT, CW = 0, 128, 256, 384, 384 + TT, 385 + TT, 386 + TT, 387 + TT, 388 + TT


def gps_layer(nc, x, src, dst, ew, wA, wm, rows, cols, gate_w, gate_b, w1, b1, w2, b2, cst, out):
    f32, i32, u32, bf16 = mybir.dt.float32, mybir.dt.int32, mybir.dt.uint32, mybir.dt.bfloat16
    ALU, ACT, AX = mybir.AluOpType, mybir.ActivationFunctionType, mybir.AxisListType
    ds = bass.ds

    support = nc.dram_tensor("support", (TT * P, D), f32).ap()
    mixrec = nc.dram_tensor("mixrec", (TT * P, 2 * D), f32).ap()
    xn2_d = nc.dram_tensor("xn2", (TT * P, D), f32).ap()
    y_d = nc.dram_tensor("y_rows", (YROWS, D), f32).ap()

    ctx = ExitStack()
    with ctx:
        def sb(name, shape, dt, c=ctx):
            return c.enter_context(nc.sbuf_tensor(name, shape, dt))

        def sem(name):
            return ctx.enter_context(nc.semaphore(name))

        cs = sb("cs", [P, CW], f32)
        ident, iota = cs[:, C_ID:C_ID + P], cs[:, C_IOTA:C_IOTA + P]
        negtri = sb("negtri", [P, P], bf16)
        ones_b = sb("ones_b", [P, P], bf16)
        ones_f = sb("ones_f", [P, P], f32)
        vec = sb("vec", [P, 6, D], f32)
        xa = sb("xa", [P, TT * D], f32)
        stats = sb("stats", [P, TT * 6], f32)
        mv = sb("mv", [P, TT * 2], f32)
        rstd = sb("rstd", [P, TT], f32)
        btab = sb("btab", [1, NCH * P], i32)

        c0 = ExitStack()
        M = sb("M", [P, NB, CC], bf16, c0)
        T = sb("T", [P, NB, CC + 1], f32, c0)
        S = sb("S", [P, NB, CC + 1], f32, c0)
        V = sb("V", [P, NB, CC], f32, c0)
        xr = sb("xr", [P, P1, D], f32, c0)
        xT = sb("xT", [P, P1, D], f32, c0)
        Er = sb("Er", [P, P1, 2 * D], f32, c0)
        Rr = sb("Rr", [P, P1, 2 * D], f32, c0)
        kq = sb("kq", [P, P1, 2 * D], f32, c0)
        vs = sb("vs", [P, P1, 4, 132], f32, c0)
        qT = sb("qT", [P, P1, D], f32, c0)
        srci = sb("srci", [P, EC], i32, c0)
        dsti = sb("dsti", [P, EC], i32, c0)
        loi = sb("loi", [P, EC], i32, c0)
        endb = sb("endb", [P, 32], f32, c0)
        nb_ = sb("nb_", [P, NB], f32, c0)
        nbi = sb("nbi", [P, NB], i32, c0)
        dcol = sb("dcol", [P, P], f32, c0)
        posi = sb("posi", [P, CC], i32, c0)
        cb = sb("cb", [P, D], f32, c0)
        c0.close()
        u = sb("u", [P, TT * D], f32)
        w1s = sb("w1s", [P, E, 2, F], f32)       

        cm = ExitStack()
        wAs = sb("wAs", [P, 2, 4 * D], f32, cm)
        wms = sb("wms", [P, 2, 2, D], f32, cm)
        lohi = sb("lohi", [P, 2, EDGES], f32, cm)
        eid = sb("eid", [P, EDGES], f32, cm)
        wt = sb("wt", [P, EDGES], f32, cm)
        zeros = sb("zeros", [P, 264], f32, cm)
        L = sb("L", [P, SORT, P], f32, cm)
        O = sb("O", [P, 3, 5, P], f32, cm)
        OV = sb("OV", [P, SORT, 2, P], f32, cm)
        rec = sb("rec", [P, 2, P], f32, cm)
        reci = sb("reci", [P, 3, P], i32, cm)
        g = sb("g", [P, U, D], f32, cm)
        sel = sb("sel", [P, U, P], f32, cm)
        win = sb("win", [P, 2, U], f32, cm)
        idxw = sb("idxw", [P, U], i32, cm)
        KV = sb("KV", [P, 2, 132], f32, cm)
        colsb = sb("colsb", [P, 6], f32, cm)
        mr = sb("mr", [P, 2 * D], f32, cm)
        mu = sb("mu", [P, D], f32, cm)
        xh = sb("xh", [P, D], f32, cm)
        x1T = sb("x1T", [P, 2, P], f32, cm)
        hTm = sb("hTm", [P, 2, P], f32, cm)
        y2 = sb("y2", [P, D], f32, cm)
        sm = sb("sm", [P, 48], f32, cm)
        cm.close()

        w2s = sb("w2s", [P, 4, 4, D], f32)
        b2s = sb("b2s", [P, E, D], f32)
        b1s = sb("b1s", [P, E * 4], f32)
        gws = sb("gws", [P, 2, E], f32)
        gbs = sb("gbs", [P, E], f32)
        x2T = sb("x2T", [P, 2, 2 * D], f32)
        nmr = sb("nmr", [P, TT], f32)
        gw_ = sb("gw_", [P, 2, TT], f32)
        sloti = sb("sloti", [P, 2, MT + 4], i32)
        etab = sb("etab", [1, MT + 4], i32)
        gi = sb("gi", [P, 4], i32)
        si = sb("si", [P, 4], i32)

        cr = ExitStack()
        LG = sb("LG", [P, TT * E], f32, cr)
        V8 = sb("V8", [P, TT, 8], f32, cr)
        I8 = sb("I8", [P, TT, 8], u32, cr)
        IF = sb("IF", [P, 2, TT], f32, cr)
        MM = sb("MM", [P, E, PT], bf16, cr)
        TM = sb("TM", [P, E, PT + 1], f32, cr)
        SM = sb("SM", [P, E, PT + 1], f32, cr)
        VM = sb("VM", [P, E, PT], f32, cr)
        pl = sb("pl", [P, 4, PT], f32, cr)
        pli = sb("pli", [P, PT], i32, cr)
        n16 = sb("n16", [P, E], f32, cr)
        n16i = sb("n16i", [P, E], i32, cr)
        mcol = sb("mcol", [P, 32], f32, cr)
        mdiag = sb("mdiag", [P, 64], f32, cr)
        LM = sb("LM", [P, PT, P], bf16, cr)
        OM = sb("OM", [P, PT, 2, MT], bf16, cr)
        slotf = sb("slotf", [P, 4, MT], f32, cr)
        cr.close()
        gx = sb("gx", [P, 4, D], f32)
        hs = sb("hs", [P, 2, F], f32)
        hT = sb("hT", [P, 2, 4, P], f32)
        yo = sb("yo", [P, 4, D], f32)
        yw = w1s[:, :, :, :].rearrange("p e k f -> p (e k f)")

        B = [ctx.enter_context(nc.psum_tensor(f"bank{i}", [P, 512], f32)) for i in range(8)]
        btr, bkq, bvs, bkv0, bkv1, bsort, bqT, bspare = B
        brank = (bkq, bvs, bqT, bspare)
        bt, by, bh = bkq, bvs[:, 0:D], bvs[:, D:2 * D]
        bmsg = [B[i][:, h * D:(h + 1) * D] for i in (3, 4, 6, 7) for h in range(2)]

        credit = {"x_transposed": P1, "xT_copied": 1, "kq_product": P1, "vs_product": P1, "elu_parts": 1,
                  "kq_ready": P1, "vs_copied": 1, "q_transposed": P1, "qT_copied": 1, "pass1_stored": P1,
                  "sort_product": SORT, "message_product": U, "message_added": 8, "mix_y_read": 1,
                  "mix_record_used": 1, "r_xT_copied": 2, "r_logits_product": 2, "r_logits": 2,
                  "token_transposed": 1, "token_xT_copied": 1, "hidden_product": 2, "hidden_copied": 2,
                  "hidden_transposed": 2, "hT_ready": 2, "expert_product": 4, "expert_result": 2}
        names = ("constants_in rows_in proj_weights_in mix_weights_in src_in dst_in edge_weights_in columns_in "
                 "w1_in expert_params_in pass1_out0 pass1_out1 pass1_out2 w2_in0 w2_in1 w2_in2 w2_in3 "
                 "edge_table_cleared ones_set onehot_buckets rank_product rank_copied places_known tile_buckets "
                 "x_stats x_deviation x_normed biases_added kv_done support_stored onehot_edges onehot_valued "
                 "chunk_sorted records_ready window_ready indices_ready selections mix_record_in mix_product "
                 "mix_denominator mix_reciprocal mix_quotient mix_bn1 mix_bn2 mix_stats1 mix_deviations "
                 "mix_scales mix_shift mix_normed mix_transposed mix_x1T mix_h_product mix_gelu mix_y_product "
                 "mix_stats2 mix_added r_stats r_deviation r_normed r_transposed r_rows_stored r_counts "
                 "r_counts_copied r_behind r_tile_experts r_experts_product r_onehot r_onehot_rows r_sorted "
                 "slots_ready top2_softmax token_index t_load0 t_load1 t_load2 t_load3 t_load4 t_rows_in "
                 "t_rows_weighted t_stats t_deviation t_scales t_normed t_times_gamma t_finished t_stored "
                 "beta_added held").split()
        s = {n: sem("s_" + n) for n in (*names, *credit)}

        def after(eng, name, t):
            eng.wait_ge(s[name], t + 1 + credit.get(name, 0))

        def held_after(eng, name, t):
            after(eng, name, t)
            eng.sem_inc(s["held"], 1)

        s_x = [sem(f"s_x{i}") for i in range(5)]
        s_g = [sem(f"s_g{i}") for i in range(U)]
        s_gx = [sem(f"s_gx{i}") for i in range(4)]
        s_sc = [sem(f"s_sc{i}") for i in range(4)]
        block = ctx.enter_context(nc.Block())

        def xt(t):
            return xa[:, ds(t * D, D)]

        def xu(t):
            return u[:, ds(t * D, D)]

        def batch_of(j):
            b = next(b for b, (a, e) in enumerate(BATCH) if a <= j < e)
            return b, j - BATCH[b][0]

        def following(turn, b):
            return (turn, b + 1) if b < 2 else (turn + 1, 0)

        def rank_parts(n):
            q = n % NQ
            return 4 * q, min(4, NB - 4 * q), (T, V)[n // NQ]

        def woven(a, half, slot):
            n = 4 * (P1 * half + a) + slot - 3
            return n if 0 <= n < 2 * NQ else NR - 1 if n == 2 * NQ + 3 else None

        x_parts = [(5 * i, min(5 * i + 5, TT)) for i in range(5)]

        @block.sync
        def _(sp):
            sp.dma_start(cs[:, :], cst).then_inc(s["constants_in"], 16)
            full, rest = NE // EC, NE % EC
            sp.wait_ge(s["edge_table_cleared"], 1)
            for tile, a, n in ((srci, src, "src_in"), (dsti, dst, "dst_in"), (wt, ew, "edge_weights_in")):
                sp.dma_start(tile[0:full, 0:EC], a[0:full * EC].rearrange("(p t) -> p t", t=EC)).then_inc(s[n], 16)
                sp.dma_start(tile[full:full + 1, 0:rest], a[full * EC:NE].rearrange("(p t) -> p t", p=1)).then_inc(s[n], 16)
            for i, (a, b) in enumerate(x_parts):
                n = b - a if b < TT else b - a - 1
                sp.dma_start(xa[:, a * D:(a + n) * D].rearrange("p (t c) -> p t c", c=D),
                             x[a * P:(a + n) * P, :].rearrange("(t p) c -> p t c", p=P)).then_inc(s_x[i], 16)
            sp.dma_start(xa[0:LAST, (TT - 1) * D:TT * D], x[(TT - 1) * P:N, :]).then_inc(s_x[4], 16)
            sp.dma_start(wAs[:, :, :], wA.rearrange("(k p) o -> p k o", p=P)).then_inc(s["proj_weights_in"], 16)
            sp.dma_start(vec[:, :, :], rows.rearrange("n d -> (n d)").partition_broadcast(P).rearrange("p (n d) -> p n d", d=D)).then_inc(s["rows_in"], 16)
            sp.dma_start(wms[:, :, :, :], wm.rearrange("(k p) a o -> p k a o", p=P)).then_inc(s["mix_weights_in"], 16)
            sp.dma_start(colsb[:, :], cols).then_inc(s["columns_in"], 16)

            def pass1_out(t, r):
                held_after(sp, "x_normed", t)
                sp.dma_start(mixrec[ds(t * P, P), D:2 * D], xr[:, r, :]).then_inc(s[f"pass1_out{r}"], 16)
                held_after(sp, "vs_copied", t)
                sp.dma_start(support[ds(t * P, P), :].rearrange("p (a b) -> p a b", a=2), vs[:, r, 2:4, 0:P]).then_inc(s[f"pass1_out{r}"], 16)
                held_after(sp, "qT_copied", t)
                sp.dma_start(mixrec[ds(t * P, P), 0:D], qT[:, r, :]).then_inc(s[f"pass1_out{r}"], 16)

            def pass1_stored(r, rnd):
                sp.wait_ge(s[f"pass1_out{r}"], 48 * (rnd + 1))
                sp.sem_inc(s["pass1_stored"], 1)
            with sp.Fori(0, TT // P1) as i:
                pass1_out(P1 * i, 0)
                pass1_out(P1 * i + 1, 1)
                pass1_stored(0, i)
                pass1_out(P1 * i + 2, 2)
                pass1_stored(1, i)
                pass1_stored(2, i)
            pass1_out(TT - 1, 0)
            pass1_stored(0, TT // P1)
            sp.sem_inc(s["support_stored"], 1)

            def record(t):
                held_after(sp, "mix_record_used", t - 1)
                sp.dma_start(mr[:, :], mixrec[ds(t * P, P), :]).then_inc(s["mix_record_in"], 16)
            sp.wait_ge(s["kv_done"], 1)
            w1v = w1.rearrange("e (k p) f -> e p k f", p=P)
            w1f = w1s[:, :, :, :].rearrange("p e k f -> p e (k f)")
            with sp.Fori(0, E) as t:
                record(t)
                sp.dma_start(w1f[:, ds(t, 1), :].rearrange("p e (k f) -> p (e k) f", k=2), w1v[ds(t, 1), :, :, :].rearrange("e p k f -> (e p) k f")).then_inc(s["w1_in"], 16)
            with sp.Fori(E, TT) as t:
                record(t)

            sp.wait_ge(s["r_stats"], 1)
            sp.dma_start(b1s[:, :], b1).then_inc(s["expert_params_in"], 16)
            sp.dma_start(gws[:, :, :], gate_w.rearrange("(k p) e -> p k e", p=P)).then_inc(s["expert_params_in"], 16)
            sp.dma_start(gbs[:, :], gate_b.partition_broadcast(P)).then_inc(s["expert_params_in"], 16)
            sp.dma_start(b2s[:, :, :].rearrange("p e d -> p (e d)"), b2.rearrange("e d -> (e d)").partition_broadcast(P)).then_inc(s["expert_params_in"], 16)

            for a, b in x_parts:
                after(sp, "r_normed", b - 1)
                sp.dma_start(xn2_d[a * P:b * P, :].rearrange("(t p) c -> p t c", p=P), u[:, a * D:b * D].rearrange("p (t c) -> p t c", c=D)).then_inc(s["r_rows_stored"], 16)
            w2v = w2.rearrange("e (c p) h -> e p c h", p=P)
            sp.wait_ge(s["slots_ready"], 1)
            eregs = [sp.alloc_register(f"sp_e{k}") for k in range(4)]
            with sp.Fori(0, MT // 4) as i:
                sp.load(eregs, etab[0:1, ds(i * 4, 4)])
                for k in range(4):
                    e = sp.snap(eregs[k], min_val=0, max_val=E - 1)
                    held_after(sp, "expert_product", i * 4 + k - 4)
                    sp.dma_start(w2s[:, k, :, :], w2v[ds(e, 1), :, :, :].rearrange("e p c h -> (e p) c h")).then_inc(s[f"w2_in{k}"], 16)

            for k in range(4):
                sp.wait_ge(s_sc[k], 16 * (MT // 4))

            def rows_in(a, b, rows_=P):
                return (yw[0:rows_, a * 2 * D:b * 2 * D].rearrange("p (t c) -> p t c", c=2 * D),
                        y_d[a * 2 * P:(b - 1) * 2 * P + 2 * rows_, :].rearrange("(t p k) d -> p t (k d)", k=2, t=b - a))
            for g_ in range(NG):
                a, b = g_ * G, min(g_ * G + G, TT - 1)
                sp.dma_start(*rows_in(a, b)).then_inc(s[f"t_load{g_}"], 16)
            sp.dma_start(*rows_in(TT - 1, TT, LAST)).then_inc(s[f"t_load{NG - 1}"], 16)
            for g_ in range(NG):
                sp.wait_ge(s[f"t_load{g_}"], 16 if g_ < NG - 1 else 32)
                sp.sem_inc(s["t_rows_in"], 1)
            with sp.Fori(0, NG - 1) as i:
                held_after(sp, "t_finished", i)
                sp.dma_start(out[ds(i * G * P, G * P), :].rearrange("(t p) c -> p t c", p=P),
                             u[:, ds(i * G * D, G * D)].rearrange("p (t c) -> p t c", c=D)).then_inc(s["t_stored"], 16)
            after(sp, "t_finished", NG - 1)
            a = (NG - 1) * G
            sp.dma_start(out[a * P:(TT - 1) * P, :].rearrange("(t p) c -> p t c", p=P),
                         u[:, a * D:(TT - 1) * D].rearrange("p (t c) -> p t c", c=D)).then_inc(s["t_stored"], 16)
            sp.dma_start(out[(TT - 1) * P:N, :], u[0:LAST, (TT - 1) * D:TT * D]).then_inc(s["t_stored"], 16)
            sp.wait_ge(s["t_stored"], 16 * (NG + 1))

        @block.gpsimd
        def _(pool):
            nc.gpsimd.memset(zeros[:, :], 0.0)
            nc.gpsimd.memset(KV[:, :, :], 0.0)
            nc.gpsimd.memset(vs[:, :, :, :], 1.0).then_inc(s["ones_set"], 1)

            def bias_in(t):
                after(pool, "x_normed", t)
                nc.gpsimd.tensor_tensor(xt(t), xt(t), cb[:, :], ALU.add).then_inc(s["biases_added"], 1)
            with pool.Fori(0, TT) as t:
                bias_in(t)

            def gather(j, turn):
                if j % QU == 0:
                    held_after(pool, "indices_ready", 4 * turn + j // QU)
                pool.indirect_dma_start(out=g[:, j, :], out_offset=None, in_=support[:, :],
                                        in_offset=bass.IndirectOffsetOnAxis(ap=idxw[:, j:j + 1], axis=0)).then_inc(s_g[j], 16)
            pool.wait_ge(s["support_stored"], 1)
            with pool.Fori(0, NCH * (ST // U)) as turn:
                for j in range(U):
                    gather(j, turn)

            def token_rows(m, k):
                held_after(pool, "token_index", m)
                pool.indirect_dma_start(out=gx[:, k, :], out_offset=None, in_=xn2_d[:, :],
                                        in_offset=bass.IndirectOffsetOnAxis(ap=gi[:, k:k + 1], axis=0)).then_inc(s_gx[k], 16)

            def expert_rows(m, k):
                held_after(pool, "expert_result", m)
                pool.indirect_dma_start(out=y_d[:, :], out_offset=bass.IndirectOffsetOnAxis(ap=si[:, k:k + 1], axis=0),
                                        in_=yo[:, k, :], in_offset=None).then_inc(s_sc[k], 16)
            pool.wait_ge(s["r_rows_stored"], 16 * len(x_parts))
            with pool.Fori(0, TT) as t:
                nc.gpsimd.tensor_tensor(xt(t), xt(t), vec[:, 5, :], ALU.add).then_inc(s["beta_added"], 1)
            for m in range(3):
                token_rows(m, m)
            with pool.Fori(0, MT // 4 - 1) as i:
                for k in range(4):
                    token_rows(4 * i + k + 3, (k + 3) % 4)
                    expert_rows(4 * i + k, k)
            for m in range(MT - 4, MT):
                if m + 3 < MT:
                    token_rows(m + 3, (m + 3) % 4)
                expert_rows(m, m % 4)

            pool.wait_ge(s["beta_added"], TT)
            with pool.Fori(0, NG) as i:
                after(pool, "t_times_gamma", i)
                nc.gpsimd.tensor_tensor(u[:, ds(i * G * D, G * D)], u[:, ds(i * G * D, G * D)], xa[:, ds(i * G * D, G * D)], ALU.add).then_inc(s["t_finished"], 1)

        @block.scalar
        def _(act):
            A = nc.scalar.activation
            act.wait_ge(s["constants_in"], 16)
            eps = cs[:, C_LN:C_LN + 1]
            def rank_out(c, n, bank):
                b, m, to = rank_parts(n)
                after(act, "rank_product", c * NR + n)
                A(to[:, b:b + m, 0:CC], bank[:, 0:m * CC].rearrange("p (b t) -> p b t", t=CC), ACT.Copy).then_inc(s["rank_copied"], 1)
            for n in range(2 * NQ):
                rank_out(0, n, brank[n % 4])
            act.wait_ge(s["x_stats"], 1)
            A(rstd[:, :], mv[:, :].rearrange("p (t k) -> p t k", k=2)[:, :, 1], ACT.Sqrt, bias=eps).then_inc(s["x_deviation"], 1)

            def xT_copy(t, r):
                after(act, "x_transposed", t)
                after(act, "vs_product", t - P1)
                A(xT[:, r, :], btr[:, 0:D], ACT.Copy).then_inc(s["xT_copied"], 1)

            def elu_parts(t, r):
                after(act, "kq_product", t)
                after(act, "kq_ready", t - P1)
                A(Er[:, r, :], bkq[:, :], ACT.Exp)
                A(Rr[:, r, :], bkq[:, :], ACT.Relu).then_inc(s["elu_parts"], 1)

            def vs_copy(t, r):
                after(act, "vs_product", t)
                after(act, "q_transposed", t - P1)
                after(act, "pass1_stored", t - P1)
                A(vs[:, r, :, 0:P], bvs[:, :].rearrange("p (a b) -> p a b", a=4), ACT.Copy).then_inc(s["vs_copied"], 1)

            def qT_copy(t, r):
                after(act, "q_transposed", t)
                after(act, "pass1_stored", t - P1)
                A(qT[:, r, :], bqT[:, 0:D], ACT.Copy).then_inc(s["qT_copied"], 1)

            def values(turn, j):
                b, r = batch_of(j)
                if j == BATCH[b][0]:
                    after(act, "onehot_edges", turn * len(BATCH) + b)
                A(OV[:, j, 0, :], O[:, b, r, :], ACT.Copy, scale=wt[:, ds(turn * SORT + j, 1)])
                last = A(OV[:, j, 1, :], O[:, b, r, :], ACT.Copy, scale=eid[:, ds(turn * SORT + j, 1)])
                last.then_inc(s["onehot_valued"], 1)

            def round1(i, c=None, half=0):
                for a in range(P1):
                    def rank(slot):
                        n = woven(a, half, slot)
                        if c is not None and n is not None and n < 2 * NQ:
                            rank_out(c, n, bspare)
                    t = P1 * i + a
                    turn, b = following(i, a)
                    j0, j1 = BATCH[b]
                    elu_parts(t, a)
                    rank(0)
                    vs_copy(t, a)
                    rank(1)
                    xT_copy(t + 1, (a + 1) % P1)
                    for j in range(j0, j0 + 2):
                        values(turn, j)
                    rank(2)
                    for j in range(j0 + 2, j1):
                        values(turn, j)
                    qT_copy(t, a)
                    rank(3)
            xT_copy(0, 0)
            for j in range(*BATCH[0]):
                values(0, j)
            with act.Fori(0, NCH - 1) as q:
                round1(2 * q, q + 1, 0)
                round1(2 * q + 1, q + 1, 1)
            with act.Fori(2 * NCH - 2, TT // P1) as i:
                round1(i)
            elu_parts(TT - 1, 0)
            vs_copy(TT - 1, 0)
            qT_copy(TT - 1, 0)

            def mix_sqrt(n, start=True, finish=True):
                if start:
                    act.wait_ge(s["mix_stats1"], n + 1)
                if finish:
                    act.wait_ge(s["mix_stats2"], n)
                A(sm[:, 8:19:10], sm[:, 7:18:10], ACT.Sqrt, bias=eps).then_inc(s["mix_deviations"], 1)

            def mix_norm(t):
                act.wait_ge(s["mix_shift"], t + 1)
                A(xh[:, :], mu[:, :], ACT.Identity, scale=sm[:, 9:10], bias=sm[:, 36:37]).then_inc(s["mix_normed"], 1)

            def mix_x1T(t):
                act.wait_ge(s["mix_transposed"], t + 1)
                A(x1T[:, 0, :], btr[:, 0:P], ACT.Identity, scale=colsb[:, 0:1], bias=colsb[:, 2:3])
                A(x1T[:, 1, :], btr[:, P:2 * P], ACT.Identity, scale=colsb[:, 1:2], bias=colsb[:, 3:4]).then_inc(s["mix_x1T"], 1)

            def mix_gelu(t):
                act.wait_ge(s["mix_h_product"], t + 1)
                for o in range(2):
                    last = A(hTm[:, o, :], bh[:, o * P:(o + 1) * P], ACT.Gelu, bias=colsb[:, 4 + o:5 + o])
                last.then_inc(s["mix_gelu"], 1)

            def turn_act(turn, t):
                mix_gelu(t)
                for j in range(BATCH[1][0], SORT):
                    values(turn, j)
                mix_sqrt(t + 1)
                for j in range(*BATCH[0]):
                    if j == 4:
                        mix_norm(t + 1)
                    values(turn + 1, j)
                mix_x1T(t + 1)
            act.wait_ge(s["columns_in"], 16)
            mix_sqrt(0, finish=False)
            mix_norm(0)
            mix_x1T(0)
            with act.Fori(0, (NCH - 1) * (ST // U)) as i:
                turn_act(i + CC // SORT, i)
            mix_gelu(TT - 1)
            mix_sqrt(TT, start=False)

            act.wait_ge(s["r_stats"], 2)
            A(rstd[:, :], mv[:, :].rearrange("p (t k) -> p t k", k=2)[:, :, 1], ACT.Sqrt, bias=eps).then_inc(s["r_deviation"], 1)

            def x2T_copy(p_, h, n=2):
                after(act, "r_transposed", p_)
                after(act, "r_logits_product", p_ - 2)
                A(x2T[:, h, 0:n * D], (btr, bspare)[h][:, 0:n * D], ACT.Copy).then_inc(s["r_xT_copied"], 1)
            with act.Fori(0, TT // 4) as i:
                x2T_copy(2 * i, 0)
                x2T_copy(2 * i + 1, 1)
            x2T_copy(TT // 2, 0, 1)
            act.wait_ge(s["top2_softmax"], 1)
            A(gw_[:, 1, :], pl[:, 3, 0:TT], ACT.Exp).then_inc(s["top2_softmax"], 1)
            for q in range(2):
                act.wait_ge(s["r_counts"], q + 1)
                A(TM[:, 8 * q:8 * q + 8, 0:PT], B[1 + q][:, 0:8 * PT].rearrange("p (b t) -> p b t", t=PT), ACT.Copy).then_inc(s["r_counts_copied"], 1)

            for q in range(PQ):
                act.wait_ge(s["r_onehot"], q + 1)
                A(OM[:, q * PB:(q + 1) * PB, 0, :], OM[:, q * PB:(q + 1) * PB, 0, :], ACT.Copy, scale=cs[:, C_ROW:C_ROW + 1]).then_inc(s["r_onehot_rows"], 1)

            def xT2_copy(m, r):
                after(act, "token_transposed", m)
                after(act, "hidden_product", m - 2)
                A(x2T[:, r, 0:D], btr[:, 0:D], ACT.Copy).then_inc(s["token_xT_copied"], 1)

            def relu(m, k, e):
                after(act, "hidden_transposed", m)
                after(act, "expert_product", m - 2)
                for c in range(4):
                    last = A(hT[:, k % 2, c, :], B[3 + k % 2][:, c * P:(c + 1) * P], ACT.Relu, bias=b1s[:, ds(e * 4 + c, 1)])
                last.then_inc(s["hT_ready"], 1)
            act.wait_ge(s["slots_ready"], 1)
            act.wait_ge(s["expert_params_in"], 64)
            eregs = [act.alloc_register(f"act_e{k}") for k in range(4)]
            xT2_copy(0, 0)
            xT2_copy(1, 1)
            with act.Fori(0, MT // 4 - 1) as i:
                act.load(eregs, etab[0:1, ds(i * 4, 4)])
                for k in range(4):
                    relu(4 * i + k, k, act.snap(eregs[k], min_val=0, max_val=E - 1))
                    xT2_copy(4 * i + k + 2, k % 2)
            act.load(eregs, etab[0:1, MT - 4:MT])
            for k in range(4):
                relu(MT - 4 + k, k, act.snap(eregs[k], min_val=0, max_val=E - 1))
                if k < 2:
                    xT2_copy(MT - 2 + k, k % 2)

            def weigh_rows(i):
                after(act, "t_rows_in", i)
                for r in range(G):
                    y = yw[:, ds((2 * (i * G + r) + 1) * D, D)]
                    last = A(y, y, ACT.Copy, scale=gw_[:, 1, ds(i * G + r, 1)])
                last.then_inc(s["t_rows_weighted"], 1)

            def last_norm(i):
                after(act, "t_stats", i)
                A(rstd[:, ds(i * G, G)], mv[:, 0:2 * G].rearrange("p (t k) -> p t k", k=2)[:, :, 1], ACT.Sqrt, bias=eps).then_inc(s["t_deviation"], 1)
                after(act, "t_scales", i)
                for r in range(G):
                    last = A(xu(i * G + r), xu(i * G + r), ACT.Identity, scale=rstd[:, ds(i * G + r, 1)], bias=nmr[:, ds(i * G + r, 1)])
                last.then_inc(s["t_normed"], 1)
            weigh_rows(0)
            with act.Fori(0, NG - 1) as i:
                weigh_rows(i + 1)
                last_norm(i)
            last_norm(NG - 1)

        @block.vector
        def _(dve):
            v = nc.vector
            TS, TTo, STT = v.tensor_scalar, v.tensor_tensor, v.scalar_tensor_tensor
            v.memset(srci[:, :], NB * P)
            v.memset(dsti[:, :], 0)
            v.memset(wt[:, :], 0.0)
            v.memset(eid[:, EC:EDGES], 0.0)
            v.memset(lohi[:, :, EC:EDGES], 0.0)
            v.memset(xa[:, (TT - 1) * D:TT * D], 0.0).then_inc(s["edge_table_cleared"], 1)
            v.memset(ones_b[:, :], 1.0)
            v.memset(ones_f[:, :], 1.0)
            dve.wait_ge(s["constants_in"], 16)
            v.tensor_copy(negtri[:, :], cs[:, C_NEG:C_NEG + P])
            dve.wait_ge(s["src_in"], 32)
            dve.wait_ge(s["dst_in"], 32)
            dve.wait_ge(s["edge_weights_in"], 32)
            TS(loi[:, :], srci[:, :], P - 1, None, ALU.bitwise_and)
            TS(srci[:, :], srci[:, :], 7, None, ALU.arith_shift_right)
            dve.drain()
            v.tensor_copy(lohi[:, 1, 0:EC], srci[:, :])
            STT(eid[:, 0:EC], dsti[:, :], float(P), loi[:, :], ALU.mult, ALU.add)
            dve.drain()

            def buckets(c):
                TTo(M[:, :, :], lohi[:, 1, ds(c * CC, CC)].unsqueeze(1).broadcast_to([P, NB, CC]),
                    cs[:, C_IOTA:C_IOTA + NB].unsqueeze(2).broadcast_to([P, NB, CC]), ALU.is_equal).then_inc(s["onehot_buckets"], 1)

            def bucket_sums(c):
                after(dve, "rank_copied", c * 2 * NQ + NQ - 1)
                v.tensor_reduce(nb_[:, :], T[:, :, 0:CC], AX.X, ALU.add)
                dve.drain()
                TS(nb_[:, :], nb_[:, :], float(P - 1), None, ALU.add)
                dve.drain()
                v.tensor_copy(nbi[:, :], nb_[:, :])
                dve.drain()
                TS(nbi[:, :], nbi[:, :], 7, 7, ALU.arith_shift_right, ALU.arith_shift_left)
                dve.drain()
                v.tensor_copy(endb[:, 0:NB], nbi[:, :])
                dve.drain()
                TTo(nb_[:, :], endb[:, 0:NB], nb_[:, :], ALU.subtract)
                dve.drain()
                TS(T[:, :, CC], nb_[:, :], float(P - 1), None, ALU.add)

            def running_sums():
                dve.drain()
                Tf = T[:, :, :].rearrange("p b t -> p (b t)")
                v.tensor_tensor_scan(S[:, :, :].rearrange("p b t -> p (b t)"), Tf, Tf, 0.0, ALU.add, ALU.bypass)
                dve.drain()
                v.tensor_copy(endb[:, 0:NB], S[:, :, CC])
                dve.drain()
                TS(nb_[:, :], endb[:, 0:NB], cs[:, C_SLOT:C_SLOT + 1], 0.0, ALU.is_le, ALU.add, accum_out=endb[:, 31:32])
                dve.drain()
                TS(endb[:, 30:31], endb[:, 31:32], float(NB - 1), None, ALU.min)
                dve.drain()
                TS(dcol[:, :], ident, endb[:, 30:31], None, ALU.mult).then_inc(s["tile_buckets"], 1)

            def place_parts(c):
                after(dve, "rank_copied", c * 2 * NQ + 2 * NQ - 1)
                TTo(V[:, :, :], V[:, :, :], S[:, :, 0:CC], ALU.add)
                dve.drain()
                TTo(V[:, :, :], V[:, :, :], M[:, :, :], ALU.mult)

            def places(c):
                dve.drain()
                lc, hc = lohi[:, 0, ds(c * CC, CC)], lohi[:, 1, ds(c * CC, CC)]
                v.tensor_reduce(lc, V[:, :, :].rearrange("p b t -> p t b"), AX.X, ALU.add)
                dve.drain()
                TS(lc, lc, -1.0, None, ALU.add)
                dve.drain()
                v.tensor_copy(posi[:, :], lc)
                dve.drain()
                TS(loi[:, 0:CC], posi[:, :], P - 1, None, ALU.bitwise_and)
                TS(posi[:, :], posi[:, :], 7, None, ALU.arith_shift_right)
                dve.drain()
                v.tensor_copy(lc, loi[:, 0:CC])
                v.tensor_copy(hc, posi[:, :])
                after(dve, "rank_product", c * NR + NR - 1)
                v.tensor_copy(btab[0:1, ds(c * P, ST)], bspare[0:1, 0:ST]).then_inc(s["places_known"], 1)
                dve.drain()
            def x_stats(i):
                a, b = x_parts[i]
                dve.wait_ge(s_x[i], 16 if b < TT else 32)
                for t in range(a, b):
                    v.bn_stats(stats[:, 6 * t:6 * t + 6], xa[:, t * D:(t + 1) * D])
            buckets(0)
            x_stats(0)
            x_stats(1)
            bucket_sums(0)
            running_sums()
            for i in range(2, len(x_parts)):
                x_stats(i)
            dve.drain()
            for t in range(TT):
                last = v.bn_aggr(mv[:, 2 * t:2 * t + 2], stats[:, 6 * t:6 * t + 6])
            last.then_inc(s["x_stats"], 1)
            dve.wait_ge(s["rows_in"], 16)
            TTo(cb[:, :], vec[:, 2, :], vec[:, 3, :], ALU.add)
            dve.wait_ge(s["x_deviation"], 1)
            v.reciprocal(rstd[:, :], rstd[:, :])
            dve.wait_ge(s["ones_set"], 1)
            dve.drain()

            def xn(t, r):
                after(dve, "x_transposed", t - P1)
                after(dve, "pass1_stored", t - P1)
                TS(xr[:, r, :], xt(t), mv[:, ds(2 * t, 1)], rstd[:, ds(t, 1)], ALU.subtract, ALU.mult).then_inc(s["x_normed"], 1)

            def kq_(t, r):
                after(dve, "elu_parts", t)
                after(dve, "q_transposed", t - P1)
                STT(kq[:, r, :], Er[:, r, :], 1.0, Rr[:, r, :], ALU.min, ALU.add).then_inc(s["kq_ready"], 1)

            def onehot(turn, b):
                j0, j1 = BATCH[b]
                n = j1 - j0
                after(dve, "sort_product", turn * SORT + j1 - 1 - SORT)
                for tab, dst_ in ((0, L[:, j0:j1, :]), (1, O[:, b, 0:n, :])):
                    last = TTo(dst_, cs[:, C_IOTA:C_IOTA + P].unsqueeze(1).broadcast_to([P, n, P]),
                               lohi[:, tab, ds(turn * SORT + j0, n)].unsqueeze(2).broadcast_to([P, n, P]), ALU.is_equal)
                last.then_inc(s["onehot_edges"], 1)

            def round1(i, c=None, half=0):
                for a in range(P1):
                    t = P1 * i + a
                    xn(t + 1, (a + 1) % P1)
                    kq_(t, a)
                    step = P1 * half + a
                    if c is not None and step == 0:
                        buckets(c)
                    onehot(*following(*following(i, a)))
                    if c is not None and step == 2:
                        bucket_sums(c)
                    if c is not None and step == 3:
                        running_sums()
                    if c is not None and step == 4:
                        place_parts(c)
                    if c is not None and step == 5:
                        places(c)
            xn(0, 0)
            place_parts(0)
            places(0)
            onehot(0, 0)
            onehot(0, 1)
            with dve.Fori(0, NCH - 1) as q:
                round1(2 * q, q + 1, 0)
                round1(2 * q + 1, q + 1, 1)
            with dve.Fori(2 * NCH - 2, TT // P1) as i:
                round1(i)
            kq_(TT - 1, 0)
            after(dve, "q_transposed", TT - 1)
            for h in range(2):
                src_b = (bkv0, bkv1)[h]
                for k in range(4):
                    p0 = 32 * k
                    v.tensor_copy(KV[p0:p0 + 32, h, p0:p0 + 32], src_b[p0:p0 + 32, p0:p0 + 32])
                    v.tensor_copy(KV[p0:p0 + 32, h, P + k:P + k + 1], src_b[p0:p0 + 32, P:P + 1])
            dve.wait_ge(s["biases_added"], TT)
            dve.drain()
            dve.sem_inc(s["kv_done"], 1)

            def records(c):
                after(dve, "chunk_sorted", c)
                v.tensor_copy(reci[:, 0, :], bsort[:, P:2 * P])
                v.tensor_copy(rec[:, 0, :], bsort[:, 0:P])
                dve.drain()
                TS(reci[:, 1, :], reci[:, 0, :], P - 1, None, ALU.bitwise_and)
                TS(reci[:, 2, :], reci[:, 0, :], 7, None, ALU.arith_shift_right)
                dve.drain()
                v.tensor_copy(rec[:, 1, :], reci[:, 1, :]).then_inc(s["records_ready"], 1)
                dve.drain()

            def window(at):
                v.tensor_copy(win[:, :, :], rec[:, :, ds(at * U, U)]).then_inc(s["window_ready"], 1)

            def indices(turn, q, at):
                after(dve, "message_product", turn * U + (q + 1) * QU - 1 - U)
                v.tensor_copy(idxw[:, q * QU:(q + 1) * QU], reci[:, 2, ds(at * U + q * QU, QU)]).then_inc(s["indices_ready"], 1)

            def select(k):
                TS(sel[:, k, :], iota, win[:, 1, k:k + 1], win[:, 0, k:k + 1], ALU.is_equal, ALU.mult).then_inc(s["selections"], 1)

            den = bt[:, 0:264].rearrange("p (h c) -> p h c", h=2)

            def start_0(t):
                dve.wait_ge(s["mix_product"], t + 1)
                TS(sm[:, 20:28].rearrange("p (h c) -> p h c", h=2), den[:, :, P:P + 4], 1e-6, None, ALU.add).then_inc(s["mix_denominator"], 1)

            def start_1(t):
                dve.wait_ge(s["mix_denominator"], t + 1)
                v.reciprocal(sm[:, 28:36], sm[:, 20:28]).then_inc(s["mix_reciprocal"], 1)

            def start_2(t):
                dve.wait_ge(s["mix_reciprocal"], t + 1)
                for h in range(2):
                    last = TTo(mu[:, h * P:(h + 1) * P].rearrange("p (k m) -> p k m", k=4), den[:, h, 0:P].rearrange("p (k m) -> p k m", k=4),
                               sm[:, 28 + 4 * h:32 + 4 * h].unsqueeze(2).broadcast_to([P, 4, 32]), ALU.mult)
                last.then_inc(s["mix_quotient"], 1)

            def start_3(t):
                dve.wait_ge(s["mix_quotient"], t + 1)
                TTo(mu[:, :], mu[:, :], mr[:, D:2 * D], ALU.add).then_inc(s["mix_record_used"], 1)

            def start_4(t):
                after(dve, "mix_record_used", t)
                v.bn_stats(sm[:, 0:6], mu[:, :]).then_inc(s["mix_bn1"], 1)

            def start_5(t):
                v.bn_aggr(sm[:, 6:8], sm[:, 0:6]).then_inc(s["mix_stats1"], 1)

            def finish_0(t):
                dve.wait_ge(s["mix_y_product"], t + 1)
                v.bn_stats(sm[:, 10:16], by[:, :]).then_inc(s["mix_bn2"], 1)

            def finish_1(t):
                v.bn_aggr(sm[:, 16:18], sm[:, 10:16]).then_inc(s["mix_stats2"], 1)

            def rsqrt(n):
                dve.wait_ge(s["mix_deviations"], n + 1)
                v.reciprocal(sm[:, 9:20:10], sm[:, 8:19:10]).then_inc(s["mix_scales"], 1)

            def start_6(t):
                dve.wait_ge(s["mix_scales"], t + 1)
                STT(sm[:, 36:37], sm[:, 6:7], -1.0, sm[:, 9:10], ALU.mult, ALU.mult).then_inc(s["mix_shift"], 1)

            def finish_2(t):
                dve.wait_ge(s["mix_scales"], t + 2)
                STT(y2[:, :], by[:, :], sm[:, 16:17], vec[:, 1, :], ALU.subtract, ALU.mult).then_inc(s["mix_y_read"], 1)

            def finish_3(t, message):
                after(dve, "mix_y_read", t)
                after(dve, "message_added", message)
                STT(xt(t), y2[:, :], sm[:, 19:20], xt(t), ALU.mult, ALU.add).then_inc(s["mix_added"], 1)

            regs = [dve.alloc_register(f"bucket{k}") for k in range(U)]

            TL = ST // U

            def turn_dve(turn, at, base, sort_turn, start, finish, follow, chunk=None):
                def add(k, mixed=False, also=None):
                    b = dve.snap(regs[k], min_val=0, max_val=NB - 1)
                    if k % 2 == 0:
                        after(dve, "message_product", turn * U + k + 1)
                    after(dve, "message_added", turn * U + k - 1)
                    if mixed:
                        dve.wait_ge(s["mix_added"], finish + 1)
                    if also is not None:
                        dve.wait_ge(s[also], finish + 1)
                    TTo(xt(b), xt(b), bmsg[k % 8], ALU.add).then_inc(s["message_added"], 1)
                then = {"turn": at + 1, "chunk": 0, None: None}[follow]
                for k in range(U):
                    if k == 7 and start is not None:
                        dve.wait_ge(s["mix_bn1"], start + 1)
                    if k < HU:
                        select(k + HU)
                    if sort_turn is not None and k in (0, 5):
                        onehot(*following(*following(sort_turn, k // 5)))
                    if k >= LAG:
                        add(k - LAG, finish is not None and k == 13, "mix_bn2" if finish is not None and k == 7 else None)
                    if k == 1:
                        dve.load(regs[HU:U], btab[0:1, ds(base + at * U + HU, HU)])
                    if k == HU + LAG and follow is not None:
                        dve.load(regs[0:HU], btab[0:1, ds(base + at * U + U, HU)])
                    if follow == "chunk" and k == HU + 1:
                        records(chunk)
                    if follow is not None and k == HU + 1:
                        after(dve, "selections", turn * U + U - 1)
                        window(then)
                        if follow == "chunk":
                            indices(turn + 1, 0, then)
                        indices(turn + 1, 1, then)
                    if follow == "turn" and k == QU + 1:
                        indices(turn + 1, 0, then)
                    if follow is not None and k == 3 * QU + 1:
                        indices(turn + 1, 2, then)
                    if follow is not None and k >= HU + 2:
                        if k == HU + 2:
                            after(dve, "window_ready", turn + 1)
                            select(0)
                            select(1)
                        select(k - HU)
                    if start is not None:
                        for at_, f in ((2, start_0), (3, start_1), (4, start_2), (5, start_3), (6, start_4), (7, start_5)):
                            if k == at_:
                                f(start)
                    if finish is not None:
                        for at_, f in ((6, finish_0), (7, finish_1)):
                            if k == at_:
                                f(finish)
                    if finish is not None and k == 10:
                        rsqrt(finish + 1)
                    if start is not None and k == 11:
                        start_6(start)
                    if finish is not None and k == 11:
                        finish_2(finish)
                    if finish is not None and k == 12:
                        finish_3(finish, turn * U + k - LAG)
                add(U - 2)
                if sort_turn is not None:
                    onehot(*following(*following(sort_turn, 2)))
                add(U - 1)
                if follow is not None:
                    indices(turn + 1, 3, then)

            v.memset(sm[:, 16:18], 1.0)
            records(0)
            window(0)
            for q in range(4):
                indices(0, q, 0)
            after(dve, "window_ready", 0)
            for k in range(HU):
                select(k)
            for f in (start_0, start_1, start_2, start_3, start_4):
                f(0)
            dve.drain()
            start_5(0)
            rsqrt(0)
            start_6(0)
            dve.load(regs[0:HU], btab[0:1, 0:HU])
            last_at = TL - 1
            with dve.Fori(0, NCH - 1) as c:
                with dve.Fori(0, last_at) as i:
                    turn = c * TL + i
                    turn_dve(turn, i, c * P, turn + TL, turn + 1, turn, "turn")
                turn = c * TL + last_at
                turn_dve(turn, last_at, c * P, turn + TL, turn + 1, turn, "chunk", c + 1)
            c = NCH - 1
            turn_dve(c * TL, 0, c * P, None, None, TT - 1, "turn")
            with dve.Fori(1, last_at) as i:
                turn_dve(c * TL + i, i, c * P, None, None, None, "turn")
            turn_dve(c * TL + last_at, last_at, c * P, None, None, None, None)

            dve.drain()
            dve.sem_inc(s["r_stats"], 1)
            for t in range(TT):
                v.bn_stats(stats[:, 6 * t:6 * t + 6], xa[:, t * D:(t + 1) * D])
            dve.drain()
            for t in range(TT):
                last = v.bn_aggr(mv[:, 2 * t:2 * t + 2], stats[:, 6 * t:6 * t + 6])
            last.then_inc(s["r_stats"], 1)
            dve.wait_ge(s["r_deviation"], 1)
            v.reciprocal(rstd[:, :], rstd[:, :])
            dve.wait_ge(s["expert_params_in"], 64)
            dve.drain()

            def xn2(t):
                TS(xu(t), xt(t), mv[:, ds(2 * t, 1)], rstd[:, ds(t, 1)], ALU.subtract, ALU.mult).then_inc(s["r_normed"], 1)

            def logits(p_, h, n=2):
                after(dve, "r_logits_product", p_)
                TTo(LG[:, ds(p_ * 2 * E, n * E)].rearrange("p (n e) -> p n e", e=E), B[1 + h][:, 0:n * E].rearrange("p (n e) -> p n e", e=E),
                    gbs[:, :].unsqueeze(1).broadcast_to([P, n, E]), ALU.add).then_inc(s["r_logits"], 1)
            for t in range(5):
                xn2(t)
            with dve.Fori(0, TT // 4 - 1) as i:
                for h in range(2):
                    xn2(4 * i + 2 * h + 5)
                    xn2(4 * i + 2 * h + 6)
                    logits(2 * i + h, h)
            logits(TT // 2 - 2, 0)
            logits(TT // 2 - 1, 1)
            logits(TT // 2, 0, 1)
            dve.drain()
            for t in range(TT):
                v.max(V8[:, t, :], LG[:, t * E:(t + 1) * E])
            dve.drain()
            for t in range(TT):
                v.max_index(I8[:, t, :], V8[:, t, :], LG[:, t * E:(t + 1) * E])
            TTo(pl[:, 3, 0:TT], V8[:, :, 1], V8[:, :, 0], ALU.subtract).then_inc(s["top2_softmax"], 1)
            dve.drain()
            for k in range(2):
                v.tensor_copy(IF[:, k, :], I8[:, :, k])
            dve.drain()
            for k in range(2):
                TTo(IF[:, k, :], IF[:, k, :], cs[:, C_INV:C_INV + TT], ALU.add)
            dve.drain()
            TTo(MM[:, :, :], IF[:, :, :].rearrange("p k t -> p (k t)").unsqueeze(1).broadcast_to([P, E, PT]),
                cs[:, C_IOTA:C_IOTA + E].unsqueeze(2).broadcast_to([P, E, PT]), ALU.is_equal).then_inc(s["onehot_buckets"], 1)
            dve.wait_ge(s["top2_softmax"], 2)
            TS(gw_[:, 0, :], gw_[:, 1, :], 1.0, None, ALU.add)
            dve.drain()
            v.reciprocal(gw_[:, 0, :], gw_[:, 0, :])
            dve.drain()
            TTo(gw_[:, 1, :], gw_[:, 1, :], gw_[:, 0, :], ALU.mult)
            dve.wait_ge(s["r_counts_copied"], 2)
            v.tensor_reduce(n16[:, :], TM[:, :, 0:PT], AX.X, ALU.add)
            dve.drain()
            TS(n16[:, :], n16[:, :], float(P - 1), None, ALU.add)
            dve.drain()
            v.tensor_copy(n16i[:, :], n16[:, :])
            dve.drain()
            TS(n16i[:, :], n16i[:, :], 7, 7, ALU.arith_shift_right, ALU.arith_shift_left)
            dve.drain()
            v.tensor_copy(mcol[:, 0:E], n16i[:, :])
            dve.drain()
            TTo(n16[:, :], mcol[:, 0:E], n16[:, :], ALU.subtract)
            dve.drain()
            TS(TM[:, :, PT], n16[:, :], float(P - 1), None, ALU.add)
            dve.drain()
            TMf = TM[:, :, :].rearrange("p b t -> p (b t)")
            v.tensor_tensor_scan(SM[:, :, :].rearrange("p b t -> p (b t)"), TMf, TMf, 0.0, ALU.add, ALU.bypass)
            dve.drain()
            for q in range(2):
                dve.wait_ge(s["r_behind"], q + 1)
                TTo(VM[:, 8 * q:8 * q + 8, :], B[3 + q][:, 0:8 * PT].rearrange("p (b t) -> p b t", t=PT), SM[:, 8 * q:8 * q + 8, 0:PT], ALU.add)
            v.tensor_copy(mcol[:, 0:E], SM[:, :, PT])
            dve.drain()
            TTo(VM[:, :, :], VM[:, :, :], MM[:, :, :], ALU.mult)
            TS(n16[:, :], mcol[:, 0:E], cs[:, C_SLOT:C_SLOT + 1], 0.0, ALU.is_le, ALU.add, accum_out=mcol[:, 31:32])
            dve.drain()
            v.tensor_reduce(pl[:, 0, :], VM[:, :, :].rearrange("p b t -> p t b"), AX.X, ALU.add)
            TS(mcol[:, 30:31], mcol[:, 31:32], float(E - 1), None, ALU.min)
            dve.drain()
            TS(mdiag[:, :], ident[:, 0:MT], mcol[:, 30:31], None, ALU.mult).then_inc(s["r_tile_experts"], 1)
            TS(pl[:, 0, :], pl[:, 0, :], -1.0, None, ALU.add)
            dve.drain()
            v.tensor_copy(pli[:, :], pl[:, 0, :])
            dve.drain()
            TS(sloti[:, 0, 0:PT], pli[:, :], P - 1, None, ALU.bitwise_and)
            TS(pli[:, :], pli[:, :], 7, None, ALU.arith_shift_right)
            dve.drain()
            v.tensor_copy(pl[:, 0, :], sloti[:, 0, 0:PT])
            v.tensor_copy(pl[:, 1, :], pli[:, :])
            dve.drain()
            for q in range(PQ):
                a, b = q * PB, (q + 1) * PB
                TTo(LM[:, a:b, :], iota.unsqueeze(1).broadcast_to([P, PB, P]), pl[:, 0, a:b].unsqueeze(2).broadcast_to([P, PB, P]), ALU.is_equal)
                TTo(OM[:, a:b, 0, :], iota[:, 0:MT].unsqueeze(1).broadcast_to([P, PB, MT]), pl[:, 1, a:b].unsqueeze(2).broadcast_to([P, PB, MT]), ALU.is_equal)
                dve.drain()
                TTo(OM[:, a:b, 1, :], OM[:, a:b, 0, :], iota[:, a:b].unsqueeze(2).broadcast_to([P, PB, MT]), ALU.mult).then_inc(s["r_onehot"], 1)
            dve.wait_ge(s["r_experts_product"], 1)
            v.tensor_copy(etab[0:1, 0:MT], B[1][0:1, 0:MT])
            dve.wait_ge(s["r_sorted"], 1)
            v.tensor_copy(slotf[:, 0, :], B[2][:, 0:MT])
            v.tensor_copy(slotf[:, 1, :], B[2][:, MT:2 * MT])
            dve.drain()
            TS(slotf[:, 2, :], slotf[:, 1, :], float(TT), None, ALU.is_ge)
            TS(slotf[:, 3, :], slotf[:, 0, :], 2.0, -1.0, ALU.mult, ALU.add)
            dve.drain()
            STT(slotf[:, 1, :], slotf[:, 2, :], float(-TT), slotf[:, 1, :], ALU.mult, ALU.add)
            TTo(slotf[:, 3, :], slotf[:, 3, :], slotf[:, 2, :], ALU.add)
            dve.drain()
            STT(slotf[:, 3, :], slotf[:, 1, :], 2.0 * P, slotf[:, 3, :], ALU.mult, ALU.add)
            TS(slotf[:, 2, :], slotf[:, 0, :], 1.0, None, ALU.min)
            dve.drain()
            TTo(slotf[:, 0, :], slotf[:, 3, :], slotf[:, 2, :], ALU.mult)
            dve.drain()
            TS(slotf[:, 1, :], slotf[:, 0, :], -1.0, 0.0, ALU.add, ALU.max)
            TS(slotf[:, 2, :], iota[:, 0:MT], float(P), cs[:, C_AT:C_AT + 1], ALU.mult, ALU.add)
            TS(slotf[:, 3, :], slotf[:, 0, :], 0.0, None, ALU.is_equal)
            v.memset(sloti[:, 0, MT:MT + 4], 0)
            dve.drain()
            TTo(slotf[:, 3, :], slotf[:, 3, :], slotf[:, 2, :], ALU.mult)
            dve.drain()
            TTo(slotf[:, 3, :], slotf[:, 1, :], slotf[:, 3, :], ALU.add)
            v.tensor_copy(sloti[:, 0, 0:MT], slotf[:, 1, :])
            dve.drain()
            TS(sloti[:, 0, 0:MT], sloti[:, 0, 0:MT], 1, None, ALU.arith_shift_right)
            v.tensor_copy(sloti[:, 1, 0:MT], slotf[:, 3, :])
            dve.drain()
            dve.sem_inc(s["slots_ready"], 1)

            def token_index(m, k):
                v.tensor_copy(gi[:, k:k + 1], sloti[:, 0, ds(m, 1)]).then_inc(s["token_index"], 1)

            def hidden(m, k):
                after(dve, "hidden_product", m)
                after(dve, "hidden_transposed", m - 2)
                v.tensor_copy(hs[:, k % 2, :], B[1 + k % 2][:, :]).then_inc(s["hidden_copied"], 1)

            def result(m, k, turn, e, first):
                if not first:
                    dve.wait_ge(s_sc[k], 16 * turn)
                v.tensor_copy(si[:, k:k + 1], sloti[:, 1, ds(m, 1)])
                after(dve, "expert_product", m)
                TTo(yo[:, k, :], B[5 + k % 2][:, 0:D], b2s[:, :, :].rearrange("p e d -> p (e d)")[:, ds(e * D, D)], ALU.add).then_inc(s["expert_result"], 1)
            for m in range(4):
                token_index(m, m)
            ereg = [dve.alloc_register(f"dve_e{k}") for k in range(4)]
            hidden(0, 0)
            hidden(1, 1)

            def four(turn, first=False, end=False):
                dve.load(ereg, etab[0:1, ds(4 * turn, 4)])
                for k in range(4):
                    m = 4 * turn + k
                    result(m, k, turn, dve.snap(ereg[k], min_val=0, max_val=E - 1), first)
                    if not end:
                        token_index(m + 4, k)
                    if not end or k < 2:
                        hidden(m + 2, k)
            four(0, first=True)
            with dve.Fori(1, MT // 4 - 1) as i:
                four(i)
            four(MT // 4 - 1, end=True)

            def group(a, i):
                return a[:, ds(i * G * D, G * D)].rearrange("p (t c) -> p t c", c=D)

            def combine(i):
                after(dve, "t_rows_in", i)
                for r in range(G):
                    t = i * G + r
                    STT(xu(t), yw[:, ds(2 * t * D, D)], gw_[:, 0, ds(t, 1)], xu(t), ALU.mult, ALU.add)
                dve.drain()
                after(dve, "t_rows_weighted", i)
                rows_ = yw[:, ds(i * G * 2 * D, G * 2 * D)].rearrange("p (t k c) -> p t k c", k=2, c=D)
                TTo(group(u, i), group(u, i), rows_[:, :, 1, :], ALU.add)
                dve.drain()
                for r in range(G):
                    v.bn_stats(stats[:, 6 * r:6 * r + 6], xu(i * G + r))
                dve.drain()
                for r in range(G):
                    last = v.bn_aggr(mv[:, 2 * r:2 * r + 2], stats[:, 6 * r:6 * r + 6])
                last.then_inc(s["t_stats"], 1)

            def scales(i):
                after(dve, "t_deviation", i)
                v.reciprocal(rstd[:, ds(i * G, G)], rstd[:, ds(i * G, G)])
                dve.drain()
                STT(nmr[:, ds(i * G, G)], mv[:, 0:2 * G].rearrange("p (t k) -> p t k", k=2)[:, :, 0], -1.0,
                    rstd[:, ds(i * G, G)], ALU.mult, ALU.mult).then_inc(s["t_scales"], 1)

            def finish(i):
                after(dve, "t_normed", i)
                TTo(group(u, i), group(u, i), vec[:, 4, :].unsqueeze(1).broadcast_to([P, G, D]), ALU.mult).then_inc(s["t_times_gamma"], 1)
            combine(0)
            scales(0)
            with dve.Fori(1, NG) as i:
                combine(i)
                finish(i - 1)
                scales(i)
            finish(NG - 1)

        @block.tensor
        def _(pe):
            mm, tr = nc.tensor.matmul, nc.tensor.transpose
            for n, k in credit.items():
                pe.sem_inc(s[n], k)

            Mf = M[:, :, :].rearrange("p b t -> p (b t)")

            def rank_product(c, n, bank):
                if n == 0:
                    after(pe, "onehot_buckets", c)
                if n == NR - 1:
                    after(pe, "tile_buckets", c)
                    after(pe, "rank_copied", c * 2 * NQ + 2 * NQ - 1)
                    mm(bank[:, 0:P], ones_f[:, :], dcol[:, :], start=True, stop=True).then_inc(s["rank_product"], 1)
                    return
                b, m, _ = rank_parts(n)
                mm(bank[:, 0:m * CC], (ones_b, negtri)[n // NQ][:, :], Mf[:, b * CC:(b + m) * CC], start=True, stop=True).then_inc(s["rank_product"], 1)
            for n in range(2 * NQ):
                if n >= 4:
                    after(pe, "rank_copied", n - 4)
                rank_product(0, n, brank[n % 4])
            rank_product(0, NR - 1, bspare)

            def T_(t, r):
                after(pe, "x_normed", t)
                after(pe, "xT_copied", t - 1)
                for k in range(2):
                    last = tr(btr[:, k * P:(k + 1) * P], xr[:, r, k * P:(k + 1) * P], ident)
                last.then_inc(s["x_transposed"], 1)

            def KQ(t, r):
                after(pe, "xT_copied", t)
                after(pe, "elu_parts", t - 1)
                for k in range(2):
                    last = mm(bkq[:, :], xT[:, r, k * P:(k + 1) * P], wAs[:, k, 0:2 * D], start=(k == 0), stop=(k == 1))
                last.then_inc(s["kq_product"], 1)

            def VS(t, r):
                after(pe, "vs_copied", t - 1)
                for k in range(2):
                    last = mm(bvs[:, :], xT[:, r, k * P:(k + 1) * P], wAs[:, k, 2 * D:4 * D], start=(k == 0), stop=(k == 1))
                last.then_inc(s["vs_product"], 1)

            def KVQ(t, r, rows_=P):
                after(pe, "kq_ready", t)
                after(pe, "vs_copied", t)
                for h in range(2):
                    mm((bkv0, bkv1)[h][:, 0:P + 1], kq[0:rows_, r, h * P:(h + 1) * P], vs[0:rows_, r, h, 0:P + 1], start=False, stop=False, skip_group_check=True)
                after(pe, "qT_copied", t - 1)
                for h in range(2):
                    last = tr(bqT[:, h * P:(h + 1) * P], kq[:, r, D + h * P:D + (h + 1) * P], ident)
                last.then_inc(s["q_transposed"], 1)

            def sort_open():
                mm(bsort[:, 0:2 * P], zeros[:, 0:P], zeros[:, 0:2 * P], start=True, stop=False, skip_group_check=True)

            def sort(turn, j):
                after(pe, "onehot_valued", turn * SORT + j)
                mm(bsort[:, 0:2 * P], L[:, j, :], OV[:, j, :, :].rearrange("p a b -> p (a b)"), start=False, stop=False, skip_group_check=True).then_inc(s["sort_product"], 1)

            def sort_close():
                mm(bsort[:, 0:2 * P], zeros[:, 0:P], zeros[:, 0:2 * P], start=False, stop=True, skip_group_check=True).then_inc(s["chunk_sorted"], 1)

            def round1(i, c=None, half=0):
                for a in range(P1):
                    def rank(slot):
                        n = woven(a, half, slot)
                        if c is not None and n is not None:
                            if n == 0:
                                after(pe, "places_known", c - 1)
                            elif n < NR - 1:
                                after(pe, "rank_copied", c * 2 * NQ + n - 1)
                            rank_product(c, n, bspare)
                    t = P1 * i + a
                    KQ(t, a)
                    rank(0)
                    VS(t, a)
                    rank(1)
                    T_(t + 1, (a + 1) % P1)
                    for j in range(BATCH[a][0], BATCH[a][0] + 2):
                        sort(i, j)
                    rank(2)
                    for j in range(BATCH[a][0] + 2, BATCH[a][1]):
                        sort(i, j)
                    KVQ(t, a)
                    rank(3)
            pe.wait_ge(s["proj_weights_in"], 16)
            pe.wait_ge(s["ones_set"], 1)
            for h in range(2):
                mm((bkv0, bkv1)[h][:, 0:P + 1], zeros[:, 0:P], zeros[:, 0:P + 1], start=True, stop=False, skip_group_check=True)
            sort_open()
            T_(0, 0)
            with pe.Fori(0, NCH - 1) as q:
                round1(2 * q, q + 1, 0)
                round1(2 * q + 1, q + 1, 1)
            with pe.Fori(2 * NCH - 2, TT // P1) as i:
                round1(i)
            sort_close()
            KQ(TT - 1, 0)
            VS(TT - 1, 0)
            KVQ(TT - 1, 0, LAST)

            def message(turn, k):
                pe.wait_ge(s_g[k], 16 * turn + 16)
                after(pe, "selections", turn * U + k)
                if k % 2 == 0:
                    after(pe, "message_added", turn * U + k + 1 - 8)
                mm(bmsg[k % 8], sel[:, k, :], g[:, k, :], start=True, stop=True).then_inc(s["message_product"], 1)

            def mix_t(t):
                pe.wait_ge(s["mix_record_in"], 16 * t + 16)
                for h in range(2):
                    last = mm(bt[:, h * 132:(h + 1) * 132], mr[:, h * P:(h + 1) * P], KV[:, h, :], start=True, stop=True)
                last.then_inc(s["mix_product"], 1)

            def mix_x(t):
                pe.wait_ge(s["mix_normed"], t + 1)
                for k in range(2):
                    last = tr(btr[:, k * P:(k + 1) * P], xh[:, k * P:(k + 1) * P], ident)
                last.then_inc(s["mix_transposed"], 1)

            def mix_h(t):
                pe.wait_ge(s["mix_x1T"], t + 1)
                after(pe, "mix_y_read", t - 1)
                for o in range(2):
                    for k in range(2):
                        last = mm(bh[:, o * P:(o + 1) * P], wms[:, k, 0, o * P:(o + 1) * P], x1T[:, k, :], start=(k == 0), stop=(k == 1))
                last.then_inc(s["mix_h_product"], 1)

            def mix_y(t):
                pe.wait_ge(s["mix_gelu"], t + 1)
                mm(by[:, :], hTm[:, 0, :], wms[:, 0, 1, :], start=True, stop=False, skip_group_check=True)
                mm(by[:, :], ones_f[0:1, :], vec[0:1, 0, :], start=False, stop=False, skip_group_check=True)
                for k in range(2):
                    mm(by[:, k * P:(k + 1) * P], x1T[:, k, :], ident, start=False, stop=False, skip_group_check=True)
                mm(by[:, :], hTm[:, 1, :], wms[:, 1, 1, :], start=False, stop=True, skip_group_check=True).then_inc(s["mix_y_product"], 1)

            pe.wait_ge(s["mix_weights_in"], 16)
            pe.wait_ge(s["rows_in"], 16)
            pe.wait_ge(s["kv_done"], 1)
            mix_t(0)
            mix_x(0)

            def turn_pe(turn, sort_turn, start, finish, closes=False):
                for k in range(U):
                    message(turn, k)
                    if sort_turn is not None:
                        for j in range(SORT):
                            if k == (j * HU // SORT if closes else j):
                                sort(sort_turn, j)
                    if k == 1 and start is not None:
                        mix_t(start)
                    if k == 1 and finish is not None:
                        mix_h(finish)
                    if k == 4 and finish is not None:
                        mix_y(finish)
                    if k == 15 and start is not None:
                        mix_x(start)
                    if closes and k == HU - 1:
                        sort_close()
            TL = ST // U
            with pe.Fori(0, NCH - 1) as c:
                after(pe, "records_ready", c)
                sort_open()
                with pe.Fori(0, TL - 1) as i:
                    turn = c * TL + i
                    turn_pe(turn, turn + TL, turn + 1, turn)
                turn = c * TL + TL - 1
                turn_pe(turn, turn + TL, turn + 1, turn, closes=True)
            turn_pe((NCH - 1) * TL, None, None, TT - 1)
            with pe.Fori((NCH - 1) * TL + 1, NCH * TL) as turn:
                turn_pe(turn, None, None, None)

            def RT(p_, h, n=2):
                after(pe, "r_normed", 2 * p_ + n - 1)
                after(pe, "r_xT_copied", p_ - 2)
                for k in range(2 * n):
                    last = tr((btr, bspare)[h][:, k * P:(k + 1) * P], u[:, p_ * 2 * D + k * P:p_ * 2 * D + (k + 1) * P], ident)
                last.then_inc(s["r_transposed"], 1)

            def RL(p_, h, n=2):
                after(pe, "r_xT_copied", p_)
                after(pe, "r_logits", p_ - 2)
                for j in range(n):
                    for k in range(2):
                        last = mm(B[1 + h][:, j * E:(j + 1) * E], x2T[:, h, (2 * j + k) * P:(2 * j + k + 1) * P], gws[:, k, :], start=(k == 0), stop=(k == 1))
                last.then_inc(s["r_logits_product"], 1)
            pe.wait_ge(s["expert_params_in"], 64)
            RT(0, 0)
            RT(1, 1)
            for p_ in range(TT // 2 + 1):
                RL(p_, p_ % 2, min(2, TT - 2 * p_))
                if 2 * p_ + 4 < TT:
                    RT(p_ + 2, p_ % 2, min(2, TT - 2 * p_ - 4))
            pe.wait_ge(s["onehot_buckets"], NCH + 1)
            after(pe, "r_logits", TT // 2)
            MMf = MM[:, :, :].rearrange("p b t -> p (b t)")
            for q in range(2):
                mm(B[1 + q][:, 0:8 * PT], ones_b[:, :], MMf[:, 8 * PT * q:8 * PT * (q + 1)], start=True, stop=True).then_inc(s["r_counts"], 1)
            for q in range(2):
                mm(B[3 + q][:, 0:8 * PT], negtri[:, :], MMf[:, 8 * PT * q:8 * PT * (q + 1)], start=True, stop=True).then_inc(s["r_behind"], 1)
            pe.wait_ge(s["r_tile_experts"], 1)
            mm(B[1][:, 0:MT], ones_f[:, :], mdiag[:, :], start=True, stop=True).then_inc(s["r_experts_product"], 1)

            for q in range(PQ):
                pe.wait_ge(s["r_onehot_rows"], q + 1)
                for n in range(q * PB, (q + 1) * PB):
                    last = mm(B[2][:, 0:2 * MT], LM[:, n, :], OM[:, n, :, :].rearrange("p a b -> p (a b)"), start=(n == 0), stop=(n == PT - 1))
            last.then_inc(s["r_sorted"], 1)

            def XT(m, k, turn):
                pe.wait_ge(s_gx[k], 16 * (turn + 1))
                after(pe, "token_xT_copied", m - 1)
                for c in range(2):
                    last = tr(btr[:, c * P:(c + 1) * P], gx[:, k, c * P:(c + 1) * P], ident)
                last.then_inc(s["token_transposed"], 1)

            w1f = w1s[:, :, :, :].rearrange("p e k f -> p (e k f)")

            def HH(m, k, e):
                after(pe, "token_xT_copied", m)
                after(pe, "hidden_copied", m - 2)
                for c in range(2):
                    last = mm(B[1 + k % 2][:, :], x2T[:, k % 2, c * P:(c + 1) * P], w1f[:, ds((e * 2 + c) * F, F)], start=(c == 0), stop=(c == 1))
                last.then_inc(s["hidden_product"], 1)

            def HT(m, k):
                after(pe, "hidden_copied", m)
                after(pe, "hT_ready", m - 2)
                for c in range(4):
                    last = tr(B[3 + k % 2][:, c * P:(c + 1) * P], hs[:, k % 2, c * P:(c + 1) * P], ident)
                last.then_inc(s["hidden_transposed"], 1)

            def YY(m, k, turn):
                after(pe, "hT_ready", m)
                pe.wait_ge(s[f"w2_in{k}"], 16 * (turn + 1))
                after(pe, "expert_result", m - 2)
                for c in range(4):
                    last = mm(B[5 + k % 2][:, 0:D], hT[:, k % 2, c, :], w2s[:, k, c, :], start=(c == 0), stop=(c == 3))
                last.then_inc(s["expert_product"], 1)
            pe.wait_ge(s["slots_ready"], 1)
            pe.wait_ge(s["w1_in"], 16 * E)
            er = [pe.alloc_register(f"pe_e{k}") for k in range(4)]

            def step(m, k, turn, e, end=False):
                HT(m - 1, (k - 1) % 4)
                HH(m, k, e)
                if not end:
                    XT(m + 1, (k + 1) % 4, turn + (k == 3))
                YY(m - 1, (k - 1) % 4, turn - (k == 0))
            pe.load(er, etab[0:1, 0:4])
            XT(0, 0, 0)
            HH(0, 0, pe.snap(er[0], min_val=0, max_val=E - 1))
            XT(1, 1, 0)
            for k in range(1, 4):
                step(k, k, 0, pe.snap(er[k], min_val=0, max_val=E - 1))
            with pe.Fori(1, MT // 4 - 1) as i:
                pe.load(er, etab[0:1, ds(4 * i, 4)])
                for k in range(4):
                    step(4 * i + k, k, i, pe.snap(er[k], min_val=0, max_val=E - 1))
            pe.load(er, etab[0:1, MT - 4:MT])
            for k in range(4):
                step(MT - 4 + k, k, MT // 4 - 1, pe.snap(er[k], min_val=0, max_val=E - 1), end=k == 3)
            HT(MT - 1, 3)
            YY(MT - 1, 3, MT // 4 - 1)


def kernel(**inputs):
    import numpy as np
    import concourse.bacc as bacc
    from concourse.bass_utils import run_bass_kernel_spmd as run

    a = {k: np.asarray(v) for k, v in inputs.items()}
    c = np.ascontiguousarray
    wq, wk, wv = (a["L0_mix_Wqkv"][i * D:(i + 1) * D].T for i in range(3))
    cst = np.zeros((P, CW), np.float32)
    cst[:, C_ID:C_ID + P] = np.eye(P)
    cst[:, C_IOTA:C_IOTA + P] = np.arange(P)
    cst[:, C_NEG:C_NEG + P] = -np.tril(np.ones((P, P)), -1)
    cst[LAST:, C_INV + TT - 1] = 100.0
    cst[:, C_SLOT] = P * np.arange(P)
    cst[:, C_ROW] = np.arange(P) + 1
    cst[:, C_LN] = 1e-5
    cst[:, C_AT] = 2 * TT * P + np.arange(P)
    feed = {
        "x": c(a["x"]), "src": c(a["src"]), "dst": c(a["dst"]), "ew": c(a["edge_weight"]),
        "wA": c(np.concatenate([wk, wq, wv, a["L0_gnn_weight"]], 1)),
        "wm": c(np.stack([a["L0_mix_W1"].T, a["L0_mix_W2"].T], 1)),
        "rows": c(np.stack([a[n] for n in ("L0_mix_b2", "L0_mix_ln2_g", "L0_mix_ln2_b", "L0_gnn_b", "L0_ffn_gamma", "L0_ffn_beta")])),
        "cols": c(np.concatenate([a[n].reshape(2, P).T for n in ("L0_mix_ln1_g", "L0_mix_ln1_b", "L0_mix_b1")], 1)),
        "gate_w": c(a["L0_ffn_gate_w"]), "gate_b": c(a["L0_ffn_gate_b"]),
        "w1": c(a["L0_ffn_w1"]), "b1": c(a["L0_ffn_b1"].reshape(E, 4, P).transpose(2, 0, 1).reshape(P, E * 4)),
        "w2": c(a["L0_ffn_w2"]), "b2": c(a["L0_ffn_b2"]), "cst": cst,
    }
    nc = bacc.Bacc("TRN2", target_bir_lowering=False, num_devices=1)
    args = {k: nc.dram_tensor(f"in_{k}", v.shape, mybir.dt.from_np(v.dtype), kind="ExternalInput").ap() for k, v in feed.items()}
    res = nc.dram_tensor("out_x", (N, D), mybir.dt.float32, kind="ExternalOutput").ap()
    gps_layer(nc, *args.values(), res)
    got = run(nc, [{f"in_{k}": v for k, v in feed.items()}], core_ids=[0])
    return got.results[0]["out_x"]
```
